# Optimizing a Trainium2 kernel written in Bass

```python
import numpy as np
import jax
import jax.numpy as jnp

def _softmax(x, axis=-1):
    return jax.nn.softmax(x, axis=axis)

def _gelu(x):
    return jax.nn.gelu(x, approximate=True)

def _silu(x):
    return jax.nn.silu(x)

def _sigmoid(x):
    return jax.nn.sigmoid(x)

def _layernorm(x, axis=-1, eps=1e-05):
    m = jnp.mean(x, axis=axis, keepdims=True)
    v = jnp.var(x, axis=axis, keepdims=True)
    return (x - m) / jnp.sqrt(v + eps)

def _scatter_add(tgt, idx, src, axis=0):
    return tgt.at[idx].add(src)

def _segment_sum(src, seg, n):
    return jax.ops.segment_sum(src, seg, n)
kernel_name = 'mk_flamingo_gated_d1_seqx_r4_d18867'

def setup_inputs(seed: int=0):
    np.random.seed(seed)
    _w = jnp.asarray

    def _rec_inputs():
        import jax
        import jax.numpy as jnp
        _rk = jax.random.key(seed)
        x = -0.000125 + 0.9999 * jax.random.normal(jax.random.fold_in(_rk, 1), (4, 512, 512), jnp.float32)
        _lenS = 512 - jax.random.randint(jax.random.fold_in(_rk, 7), (4,), 0, max(1, 512 // 4) + 1, jnp.int32)
        _lenS2 = 512 - jax.random.randint(jax.random.fold_in(_rk, 8), (4,), 0, max(1, 512 // 4) + 1, jnp.int32)
        itok_BxS_13_99985 = jax.random.randint(jax.random.fold_in(_rk, 11), (4, 512), 13, 99986, jnp.int32)
        _ctx_2048P = jax.random.normal(jax.random.fold_in(_rk, 12), (4, 16, 512), jnp.float32)
        _ctx_2048c = jax.random.dirichlet(jax.random.fold_in(_rk, 512), 0.3 * jnp.ones((16,), jnp.float32), (4, 512))
        _ctx_2048t = jnp.einsum('bsk,bkd->bsd', _ctx_2048c, _ctx_2048P)
        _ctx_2048t = _ctx_2048t * jax.lax.rsqrt(jnp.mean(jnp.square(_ctx_2048t)) + 1e-12) * 0.953939
        ctx_2048 = 6.82029e-06 + 0.0200006 * (_ctx_2048t + 0.3 * jax.random.normal(jax.random.fold_in(_rk, 612), (4, 512, 512), jnp.float32))
        _g = jax.random.normal(jax.random.fold_in(_rk, 9001), (2, 1), jnp.float32)
        _g = jnp.sign(_g) * jnp.maximum(jnp.abs(_g), 1.0) + (_g == 0) * 1.0
        g_xattn = _g[0]
        g_ffn = _g[1]
        return (x, itok_BxS_13_99985, ctx_2048, g_xattn, g_ffn)
    x, itok_BxS_13_99985, ctx_2048, g_xattn, g_ffn = _rec_inputs()

    def _L0_xattn_setup():
        import jax, jax.numpy as jnp
        import numpy as np
        B, S, D = (4, 1024, 512)
        E = 4
        F = 2048 // E
        VOCAB = 25000
        key = jax.random.key(seed)
        k1, k2, k3, k4, k5 = jax.random.split(key, 5)
        hidden_states = jax.random.normal(k1, (B, S, D), dtype=jnp.float32)
        token_ids = jax.random.randint(k2, (B, S), 0, VOCAB, dtype=jnp.int64)
        Wg = jax.random.normal(k3, (E, F, D), dtype=jnp.float32) * 0.02
        Wu = jax.random.normal(k4, (E, F, D), dtype=jnp.float32) * 0.02
        Wd = jax.random.normal(k5, (E, D, F), dtype=jnp.float32) * 0.02
        return {'hidden_states': hidden_states, 'token_ids': token_ids, 'Wg': Wg, 'Wu': Wu, 'Wd': Wd}
    _L0_xattn_all = _L0_xattn_setup()
    _L0_xattn_in = {k: v for k, v in _L0_xattn_all.items() if k in ()}
    del _L0_xattn_all

    def _L0_ffn_setup():
        import jax, jax.numpy as jnp
        import numpy as np
        TOP_K = 6
        N_GROUP = 8
        TOPK_GROUP = 3
        CAPACITY = 192
        RSF = 1.0
        key = jax.random.key(seed)
        ks = jax.random.split(key, 8)
        B, S, H = (1, 1024, 512)
        E, M = (64, 352)
        MS = 704
        sc = 0.02
        return {'hidden_states': jax.random.normal(ks[0], (B, S, H), jnp.float32), 'gate_weight': jax.random.normal(ks[1], (E, H), jnp.float32) * sc, 'Wg': jax.random.normal(ks[2], (E, M, H), jnp.float32) * sc, 'Wu': jax.random.normal(ks[3], (E, M, H), jnp.float32) * sc, 'Wd': jax.random.normal(ks[4], (E, H, M), jnp.float32) * sc, 'Sg': jax.random.normal(ks[5], (MS, H), jnp.float32) * sc, 'Su': jax.random.normal(ks[6], (MS, H), jnp.float32) * sc, 'Sd': jax.random.normal(ks[7], (H, MS), jnp.float32) * sc}
    _L0_ffn_all = _L0_ffn_setup()
    _L0_ffn_in = {k: v for k, v in _L0_ffn_all.items() if k in ('gate_weight', 'Wg', 'Wu', 'Wd', 'Sg', 'Su', 'Sd')}
    del _L0_ffn_all
    return {'x': x, 'itok_BxS_13_99985': itok_BxS_13_99985, 'ctx_2048': ctx_2048, 'g_xattn': g_xattn, 'g_ffn': g_ffn, 'L0_ffn_gate_weight': _L0_ffn_in['gate_weight'], 'L0_ffn_Wg': _L0_ffn_in['Wg'], 'L0_ffn_Wu': _L0_ffn_in['Wu'], 'L0_ffn_Wd': _L0_ffn_in['Wd'], 'L0_ffn_Sg': _L0_ffn_in['Sg'], 'L0_ffn_Su': _L0_ffn_in['Su'], 'L0_ffn_Sd': _L0_ffn_in['Sd']}

def reference(x, itok_BxS_13_99985, ctx_2048, g_xattn, g_ffn, L0_ffn_gate_weight, L0_ffn_Wg, L0_ffn_Wu, L0_ffn_Wd, L0_ffn_Sg, L0_ffn_Su, L0_ffn_Sd):
    import jax
    import jax.numpy as jnp

    def _L0_xattn_ref(hidden_states, token_ids, Wg, Wu, Wd):
        import jax, jax.numpy as jnp
        import numpy as np
        B, S, D = (4, 1024, 512)
        E = 4
        F = 2048 // E
        VOCAB = 25000
        tokens_per_expert = VOCAB // E
        tid = jnp.clip(token_ids, 0, VOCAB - 1)
        expert_ids = jnp.minimum(tid // tokens_per_expert, E - 1)
        out = jnp.zeros_like(hidden_states)
        for e in range(E):
            g = jax.nn.silu(jnp.einsum('bsd,fd->bsf', hidden_states, Wg[e]))
            u = jnp.einsum('bsd,fd->bsf', hidden_states, Wu[e])
            y = jnp.einsum('bsf,df->bsd', g * u, Wd[e])
            out = jnp.where((expert_ids == e)[..., None], y, out)
        return out

    def _L0_ffn_ref(hidden_states, gate_weight, Wg, Wu, Wd, Sg, Su, Sd):
        import jax, jax.numpy as jnp
        import numpy as np
        TOP_K = 6
        N_GROUP = 8
        TOPK_GROUP = 3
        CAPACITY = 192
        RSF = 1.0
        B, S, H = hidden_states.shape
        E, M, _ = Wg.shape
        K, NG, TG, C = (TOP_K, N_GROUP, TOPK_GROUP, CAPACITY)
        x = hidden_states.reshape(-1, H)
        T = x.shape[0]
        logits = x.astype(jnp.float32) @ gate_weight.astype(jnp.float32).T
        scores = jax.nn.softmax(logits, axis=-1)
        group_scores = scores.reshape(T, NG, E // NG).max(axis=-1)
        _, gidx = jax.lax.top_k(group_scores, TG)
        gmask = jnp.zeros((T, NG), scores.dtype).at[jnp.arange(T)[:, None], gidx].set(1.0)
        smask = jnp.repeat(gmask, E // NG, axis=1)
        tmp_scores = jnp.where(smask > 0, scores, 0.0)
        topk_w, topk_i = jax.lax.top_k(tmp_scores, K)
        topk_w = topk_w * RSF
        flat = topk_i.reshape(-1)
        oh = jax.nn.one_hot(flat, E, dtype=jnp.int32)
        pos = jnp.sum(jnp.cumsum(oh, axis=0) * oh, axis=-1) - 1
        slot = flat * C + jnp.minimum(pos, C - 1)
        tok = jnp.arange(T * K) // K
        buf = jnp.zeros((E * C, H), x.dtype).at[slot].set(x[tok]).reshape(E, C, H)
        g = jnp.einsum('ech,emh->ecm', buf, Wg)
        u = jnp.einsum('ech,emh->ecm', buf, Wu)
        out = jnp.einsum('ecm,ehm->ech', jax.nn.silu(g) * u, Wd).reshape(E * C, H)
        yk = out[slot].reshape(T, K, H)
        y = jnp.sum(yk * topk_w[..., None].astype(yk.dtype), axis=1)
        shared = jax.nn.silu(x @ Sg.T) * (x @ Su.T) @ Sd.T
        return (y + shared).reshape(B, S, H)
    x = x + jnp.tanh(g_xattn[0]) * _L0_xattn_ref(_layernorm(x, axis=-1), itok_BxS_13_99985, ctx_2048, ctx_2048, ctx_2048)
    x = x + jnp.tanh(g_ffn[0]) * _L0_ffn_ref(_layernorm(x, axis=-1), L0_ffn_gate_weight, L0_ffn_Wg, L0_ffn_Wu, L0_ffn_Wd, L0_ffn_Sg, L0_ffn_Su, L0_ffn_Sd)
    return x

_drawn_inputs = setup_inputs


def setup_inputs(seed=0):
    import zlib

    import numpy as np

    out = dict(_drawn_inputs(seed))
    spreads = {}
    factors = {'L0_ffn_gate_weight': 8.0,
     'L0_ffn_Wg': 7.833,
     'L0_ffn_Wu': 7.847,
     'L0_ffn_Wd': 7.608,
     'L0_ffn_Sg': 8.0,
     'L0_ffn_Su': 8.0,
     'L0_ffn_Sd': 8.0}
    for name, (base, spread) in spreads.items():
        noise = np.random.default_rng([zlib.crc32(name.encode()), seed]).standard_normal(out[name].shape)
        drawn = base * np.exp(spread * noise) if base else spread * noise
        out[name] = jnp.asarray(drawn.astype(out[name].dtype))
    for name, factor in factors.items():
        out[name] = (out[name] * factor).astype(out[name].dtype)
    return out
```

```python
from contextlib import ExitStack

import concourse.bass as bass
from concourse import mybir

P = 128
ALU = mybir.AluOpType
ACT = mybir.ActivationFunctionType
F32 = mybir.dt.float32
F32R = mybir.dt.float32r
BF16 = mybir.dt.bfloat16
I32 = mybir.dt.int32
U32 = mybir.dt.uint32
X = mybir.AxisListType.X

T, H = 2048, 512
KH = H // P
NTOK = T // P
XE, XF = 4, 512
PER_EXPERT = 25000 // XE
NT = NTOK + XE - 1
E, M = 64, 352
MT = [P, P, M - 2 * P]
CAP = 192
HC = CAP // 2
TOPK, NG, TOPG = 6, 8, 3
GS = E // NG
MS = 704
MST = [P] * 4 + [96] * 2
MSO = [P * min(i, 4) + 96 * max(i - 4, 0) for i in range(6)]
EPS = 1e-5
RW = H + E + 1
FLOOR = -87.3365
BIG = 1e30
SKIP = 2 * T
NOSLOT = 32768
GROUP = 2
NGRP = NTOK // GROUP
GN = GROUP * P
WGU, WD = KH * 2 * M, 3 * H
WE = WGU + WD
SGU, SD = KH * 2 * MS, 6 * H
WX = XE * KH * XF


def at_least(engine, sem, value):
    if not isinstance(value, int) or value > 0:
        engine.wait_ge(sem, value)


def build(nc, x, tid, ctxT, g_x, g_f, gateT, wgu, wdA, wdB, sgu, sdA, sdB, out):
    tok_list = nc.dram_tensor("tok_list", [NT * P, 1], F32).ap()
    x1_rows = nc.dram_tensor("x1_rows", [T, H], F32).ap()
    slots = nc.dram_tensor("slots", [E * CAP, RW], F32).ap()
    last_rows = nc.dram_tensor("last_rows", [E, H], F32).ap()

    ctx = ExitStack()
    with ctx:
        def sem(name):
            return ctx.enter_context(nc.semaphore(name))

        base = (nc.sbuf_base + 63) // 64 * 64
        top = [base]

        def sb(name, shape, dt, at=None):
            size = 1
            for d in shape[1:]:
                size *= d
            size *= 2 if dt == BF16 else 4
            size = (size + 31) // 32 * 32
            offset = top[0] if at is None else at
            t = nc.alloc_sbuf_tensor_at(name, shape, dt, offset=offset)
            if at is None:
                top[0] += size
            return t, offset, offset + size

        def keep(name, shape, dt):
            return sb(name, shape, dt)[0]

        ident = keep("ident", [P, P], F32)
        before = keep("before", [P, P], BF16)
        ones = keep("ones", [P, P], BF16)
        gate_w = keep("gate_w", [P, KH, E], F32)
        e_slot = keep("e_slot", [P, E], F32)
        tok_id = keep("tok_id", [P, NTOK], F32)
        pad_row = keep("pad_row", [P, RW], F32)
        minus_half = keep("minus_half", [P, KH], F32)
        last_skip = keep("last_skip", [HC, 2], F32)
        gates = keep("gates", [P, 2], F32)
        tg = keep("tg", [P, 2], F32)
        over_wT = keep("over_wT", [E, NTOK, P], F32)
        slot_of = keep("slot_of", [P, NTOK, 8], U32)
        logits, logits_at, _ = sb("logits", [P, NTOK, E], F32)
        over_w = sb("over_w", [P, NTOK, E], F32, at=logits_at)[0]
        mvB = keep("mvB", [P, NTOK, 2], F32)
        veB = keep("veB", [P, NTOK], F32)
        rsB = keep("rsB", [P, NTOK], F32)
        st6 = keep("st6", [P, 2, 6], F32)

        parts = keep("parts", [P, 2 * max(WX, SGU + SD, 2 * WE)], F32R)
        half = 2 * WE
        raw, raw_at, raw_end = sb("raw", [P, 2 * WE], F32)
        assert WX <= 2 * WE and SGU + SD == 2 * WE
        xs, xs_at, xs_end = sb("xs", [P, NT, H], F32)
        rows = sb("rows", [P, NTOK, RW], F32, at=xs_at)[0]
        scratch = top[0]

        def region(start):
            at = [start]

            def alloc(name, shape, dt):
                t, _, end = sb(name, shape, dt, at=at[0])
                at[0] = end
                return t
            return alloc

        a = region(scratch)
        hn = a("hn", [P, 2, H], F32)
        hT = a("hT", [P, 2, 2, KH, P], F32R)
        aT = a("aT", [P, 2, 2, KH, P], F32R)
        suA = a("suA", [P, 2, H], F32)
        acA = a("acA", [P, 2, H], F32)
        mvA = a("mvA", [P, 2, 2], F32)
        veA = a("veA", [P, 2], F32)
        rsA = a("rsA", [P, 2], F32)
        tidi = a("tidi", [P, NTOK], I32)
        tidf = a("tidf", [P, NTOK], F32)
        ge = a("ge", [P, XE + 1, NTOK], F32)
        ohA = a("ohA", [P, XE, NTOK], BF16)
        preA = a("preA", [P, XE, NTOK + 1], BF16)
        limit = a("limit", [P, XE, NTOK], F32)
        cntA = a("cntA", [P, XE], F32)
        over_m = a("over_m", [P, XE, NTOK], F32)
        tilesA = a("tilesA", [P, XE], F32)
        startA = a("startA", [P, XE], F32)
        base_slot = a("base_slot", [P, XE], F32)
        posA = a("posA", [P, XE, NTOK], F32)
        posB = a("posB", [P, XE, NTOK], F32)
        slotA = a("slotA", [P, NTOK], F32)
        slotU = a("slotU", [P, NTOK], U32)
        tile_no = a("tile_no", [1, NT + 1], F32)
        tile_e = a("tile_e", [1, 3, NT + 1], F32)
        tile_w = a("tile_w", [1, NT + 1], I32)
        padA = a("padA", [P, NT], F32)
        listT = a("listT", [NT, P], F32)
        list_g = a("list_g", [P, NT], U32)
        list_s = a("list_s", [P, NT], U32)
        hTf, _, b_start = sb("hTf", [P, 2, KH, P], F32, at=scratch)
        suB = sb("suB", [P, 2, GN], F32, at=scratch)[0]
        acB = sb("acB", [P, 2, GN], F32, at=scratch + 8 * GN)[0]
        b = region(b_start)
        hnB = b("hnB", [P, 2, H], F32)
        xrow = b("xrow", [P, 2, GROUP, H], F32)
        hTg = b("hTg", [P, 2, 2, KH, GN], F32R)
        actB = b("actB", [P, 2, 6, GN], F32R)
        cm1 = b("cm1", [P, E], F32)
        key8 = b("key8", [P, NTOK, 8], F32)
        none8 = b("none8", [P, NTOK, 8], F32)
        g13 = b("g13", [P, NTOK, NG + 5], F32)
        g13r = b("g13r", [P, NTOK, NG + 5], F32)
        g8 = b("g8", [P, NTOK, 8], F32)
        pen = b("pen", [P, NTOK, NG], F32)
        mx = b("mx", [P, NTOK], F32)
        sm = b("sm", [P, NTOK], F32)
        rc = b("rc", [P, NTOK], F32)
        EW = E + 2
        r_at = [raw_at]

        def ra(name, shape, dt, at=None):
            t, off, end = sb(name, shape, dt, at=r_at[0] if at is None else at)
            if at is None:
                r_at[0] = end
            return t, off
        z0, z0_at = ra("z0", [P, NTOK, EW], F32)
        z1, z1_at = ra("z1", [P, NTOK, EW], F32)
        z2, z2_at = ra("z2", [P, NTOK, EW], F32)
        z3, z3_at = ra("z3", [P, NTOK, EW], F32)
        z4, z4_at = ra("z4", [P, NTOK, EW], F32)
        z5, z5_at = ra("z5", [P, NTOK, EW], F32)
        z7, z7_at = ra("z7", [P, NTOK, EW], F32)
        mask, _ = ra("mask", [P, NTOK, E], BF16)
        pre, _ = ra("pre", [P, NTOK + 1, E], BF16)
        assert r_at[0] <= raw_end
        c_ = region(scratch)
        xg = c_("xg", [HC, 2, 2, RW], F32)
        xT = c_("xT", [P, 2, 2, KH, CAP], F32R)
        actC = c_("actC", [P, 2, 2, 3, CAP], F32R)
        suC = c_("suC", [P, 3, CAP], F32)
        acC = c_("acC", [P, 3, CAP], F32)
        ot = c_("ot", [HC, 2, 2, H], F32)
        wcol = c_("wcol", [HC, 2, 2], F32)
        tokc = c_("tokc", [HC, 2, 2], U32)
        lastS = c_("lastS", [E, H], F32)
        fb = sb("fb", [P, NTOK, H], F32, at=xs_at)[0]

        PS = ctx.enter_context(nc.psum_tensor("PS", [P, 8, H], F32))

        s_tid, s_gates, s_gatew = sem("tid_loaded"), sem("gates_loaded"), sem("gatew_loaded")
        s_wx = [sem(f"wx_loaded{e}") for e in range(XE)]
        s_sh = [sem(f"shared_loaded{i}") for i in range(2)]
        s_padl = sem("token_list_padded")
        s_pad = sem("slots_padded")
        s_const, s_const2 = sem("const_first"), sem("const_ready")
        s_tg = sem("tanh_ready")
        s_apart = sem("wait_carrier")
        v_a = sem("dve_chain")
        s_ohA, s_cntA, s_slotA = sem("ohA_ready"), sem("ranksA_ready"), sem("slotA_ready")
        s_lsc, s_lld = sem("token_list_scattered"), sem("token_list_loaded")
        s_lT, s_list = sem("token_list_turned"), sem("token_list_ready")
        s_wxhi, s_wxlo = sem("wx_hi_ready"), sem("wx_lo_ready")
        s_x = [sem(f"x_gathered{i}") for i in range(2)]
        s_var, s_rstd, s_hn = sem("varA_ready"), sem("rstdA_ready"), sem("hnA_ready")
        s_t1, s_h1hi, s_h1lo = sem("hA_turned"), sem("hTA_hi_ready"), sem("hTA_lo_ready")
        s_mm1, s_su, s_ac = sem("uA_ready"), sem("siluA_ready"), sem("actA_ready")
        s_t2, s_h2hi, s_h2lo = sem("actA_turned"), sem("aTA_hi_ready"), sem("aTA_lo_ready")
        s_mm2, s_x1, s_x1s = sem("yA_ready"), sem("x1_ready"), sem("x1_scattered")
        s_shhi, s_shlo = sem("shared_hi_ready"), sem("shared_lo_ready")
        s_x1l = [sem(f"x1_loaded{i}") for i in range(4)]
        s_varB, s_rstdB, s_hnB = sem("varB_ready"), sem("rstdB_ready"), sem("hnB_ready")
        s_row, s_tB, s_hTf = sem("row_kept"), sem("hB_turned"), sem("hTf_ready")
        s_lg, s_lgc = sem("logits_done"), sem("logits_kept")
        v_r = sem("routing_chain")
        s_d, s_exp, s_pre = sem("logits_shifted"), sem("exp_ready"), sem("prefix_ready")
        s_cnt, s_cm1, s_pos = sem("counts_done"), sem("counts_kept"), sem("ranks_done")
        s_posu, s_slot, s_over = sem("ranks_used"), sem("slots_ready"), sem("over_weights_ready")
        s_ovT, s_ovTc = sem("over_weights_turned"), sem("over_wT_ready")
        s_disp = sem("rows_dispatched")
        s_xr = [sem(f"x1_row_loaded{i}") for i in range(2)]
        s_hg, s_tg2, s_ghi, s_glo = sem("h_group_ready"), sem("h_group_turned"), sem("hTg_hi"), sem("hTg_lo")
        s_gu, s_suB, s_acB = sem("gateup_done"), sem("siluB_ready"), sem("actB_product")
        s_bhi, s_blo, s_dn = sem("actB_hi"), sem("actB_lo"), sem("downB_done")
        s_res = sem("shared_added")
        s_st = [sem(f"out_stored{i}") for i in range(2)]
        s_raw = [sem(f"expert_weights_loaded{i}") for i in range(2)]
        s_xg = [sem(f"expert_rows_loaded{i}") for i in range(2)]
        s_whi, s_wlo = sem("w_hi"), sem("w_lo")
        s_tx, s_xhi, s_xlo = sem("x_turned"), sem("xT_hi"), sem("xT_lo")
        s_cgu, s_csu, s_cac = sem("expert_gateup_done"), sem("expert_silu"), sem("expert_product")
        s_ahi, s_alo, s_cd = sem("expert_act_hi"), sem("expert_act_lo"), sem("expert_down_done")
        s_ot, s_wc = sem("expert_out_ready"), sem("slot_weights_ready")
        s_add = sem("rows_added")
        s_last = [sem(f"last_row_stored{i}") for i in range(2)]
        s_ll, s_f, s_fe, s_fa = sem("last_rows_loaded"), sem("over_done"), sem("over_copied"), sem("over_added")

        N_TOKSEM = 16 * NTOK
        SH_CHUNKS = [(k * 2 * MS, 2 * MS, P) for k in range(KH)] + \
                    [(SGU + i * H, H, MST[i]) for i in range(6)]
        W_CHUNKS = [(k * 2 * M, 2 * M, P) for k in range(KH)] + \
                   [(WGU + i * H, H, MT[i]) for i in range(3)]
        x1_tiled = x1_rows.rearrange("(i p) h -> p i h", p=P)
        out_tiled = out.rearrange("(i p) h -> p i h", p=P)

        def w_part(par, part, lo, n, rows_=P):
            o = par * 2 * WE + part * WE + lo
            return parts[0:rows_, o:o + n]

        def sh_part(part, lo, n, rows_=P):
            o = part * (SGU + SD) + lo
            return parts[0:rows_, o:o + n]

        def wait_apart(engine, sem_, value):
            at_least(engine, sem_, value)
            if not isinstance(value, int):
                engine.sem_inc(s_apart, 1)

        block = ctx.enter_context(nc.Block())

        @block.sync
        def _(sp):
            sp.dma_start(tidi[:, :], tid).then_inc(s_tid, 16)
            for e in range(XE):
                sp.dma_start(raw[:, e * KH * XF:(e + 1) * KH * XF], ctxT[e]).then_inc(s_wx[e], 16)
            sp.dma_start(gates[:, 0:1], g_x.broadcast_to([P, 1])).then_inc(s_gates, 16)
            sp.dma_start(gates[:, 1:2], g_f.broadcast_to([P, 1])).then_inc(s_gates, 16)
            sp.dma_start(gate_w[:, :, :], gateT).then_inc(s_gatew, 16)
            sp.wait_ge(s_lsc, N_TOKSEM)
            sp.dma_start(listT[:, :], tok_list.rearrange("(j p) o -> j (p o)", p=P)).then_inc(s_lld, 16)
            sp.wait_ge(s_wxlo, XE)
            sp.dma_start(raw[:, 0:SGU], sgu).then_inc(s_sh[0], 16)
            sp.dma_start(raw[:, SGU:SGU + 4 * H], sdA).then_inc(s_sh[1], 16)
            sp.dma_start(raw[0:96, SGU + 4 * H:SGU + SD], sdB).then_inc(s_sh[1], 16)
            sp.wait_ge(s_const2, 2)
            for i in range(8):
                sp.wait_ge(s_x1, 2 * i + 1)
                n = E * CAP // P // 8
                dst = slots.rearrange("(n p) w -> p n w", p=P)[:, i * n:(i + 1) * n, :]
                sp.dma_start(dst, pad_row[:, :].unsqueeze(1).broadcast_to([P, n, RW])).then_inc(s_pad, 16)
            sp.wait_ge(s_x1s, 16 * NT)
            for c in range(4):
                sp.dma_start(rows[:, 4 * c:4 * c + 4, 0:H], x1_tiled[:, 4 * c:4 * c + 4, :]).then_inc(s_x1l[c], 16)

            def b2_load(g, gp):
                if not (isinstance(g, int) and g < 2):
                    wait_apart(sp, s_st[gp], (g - gp) * 8)
                src = x1_rows[bass.ds(g * GN, GN), :].rearrange("(q p) h -> p q h", p=P)
                sp.dma_start(xrow[:, gp, :, :], src).then_inc(s_xr[gp], 16)

            def b2_store(g, gp):
                wait_apart(sp, s_res, GROUP * (g + 1))
                dst = out[bass.ds(g * GN, GN), :].rearrange("(q p) h -> p q h", p=P)
                sp.dma_start(dst, xrow[:, gp, :, :]).then_inc(s_st[gp], 16)

            sp.wait_ge(s_x1, NT)
            b2_load(0, 0)
            b2_load(1, 1)
            with sp.Fori(0, NGRP // 2 - 1) as it:
                for p in range(2):
                    b2_store(2 * it + p, p)
                    b2_load(2 * it + p + 2, p)
            b2_store(NGRP - 2, 0)
            b2_store(NGRP - 1, 1)

            def load_w(e, par):
                wait_apart(sp, s_wlo, 7 * (e - 1) if not isinstance(e, int) or e > 1 else 0)
                o = par * WE
                sp.dma_start(raw[:, o:o + WGU], wgu[bass.ds(e, 1)].rearrange("o p n -> (o p) n")).then_inc(s_raw[par], 16)
                sp.dma_start(raw[:, o + WGU:o + WGU + 2 * H], wdA[bass.ds(e, 1)].rearrange("o p n -> (o p) n")).then_inc(s_raw[par], 16)
                sp.dma_start(raw[0:MT[2], o + WGU + 2 * H:o + WE], wdB[bass.ds(e, 1)].rearrange("o p n -> (o p) n")).then_inc(s_raw[par], 16)

            def load_x(e, par):
                if not isinstance(e, int) or e > 1:
                    wait_apart(sp, s_tx, e - 1)
                    wait_apart(sp, s_wc, 2 * (e - 1))
                src = slots[bass.ds(e * CAP, CAP), :].rearrange("(c p) w -> p c w", p=HC)
                sp.dma_start(xg[:, par, :, :], src).then_inc(s_xg[par], 16)

            sp.wait_ge(s_over, 1)
            load_w(0, 0)
            load_w(1, 1)
            sp.wait_ge(s_disp, 16 * NTOK * TOPK)
            sp.wait_ge(s_res, NTOK)
            sp.wait_ge(s_st[0], 16 * NGRP // 2)
            sp.wait_ge(s_st[1], 16 * NGRP // 2)
            load_x(0, 0)
            load_x(1, 1)
            with sp.Fori(0, E // 2 - 1) as it:
                for p in range(2):
                    load_w(2 * it + 2 + p, p)
                    load_x(2 * it + 2 + p, p)
            sp.wait_ge(s_last[0], 16 * E // 2)
            sp.wait_ge(s_last[1], 16 * E // 2)
            sp.dma_start(lastS[:, :], last_rows).then_inc(s_ll, 16)

        @block.gpsimd
        def _(pool):
            pool.memset(padA[:, :], float(SKIP)).then_inc(s_const, 1)
            pool.memset(ident[:, :], 0.0).then_inc(s_const, 1)
            pool.iota(tok_id[:, :], [[P, NTOK]], base=0, channel_multiplier=1,
                      allow_small_or_imprecise_dtypes=True).then_inc(s_const2, 1)
            pool.memset(before[:, :], 1.0).then_inc(s_const, 1)
            pool.memset(ones[:, :], 1.0)
            pool.iota(limit[:, :, :], [[0, XE], [P, NTOK]], base=0, channel_multiplier=0,
                      allow_small_or_imprecise_dtypes=True)
            pool.iota(tile_no[:, :], [[1, NT + 1]], base=0, channel_multiplier=0,
                      allow_small_or_imprecise_dtypes=True)
            pool.wait_ge(s_const, 3)
            pool.affine_select(out=ident[:, :], in_=ident[:, :], compare_op=ALU.not_equal, fill=1.0,
                               base=0, pattern=[[-1, P]], channel_multiplier=1)
            pool.affine_select(out=before[:, :], in_=before[:, :], compare_op=ALU.is_gt, fill=0.0,
                               base=0, pattern=[[1, P]], channel_multiplier=-1)
            pool.memset(pad_row[:, 0:RW - 1], 0.0)
            pool.memset(pad_row[:, RW - 1:RW], float(SKIP))
            pool.memset(last_skip[:, :], 0.0).then_inc(s_const, 1)
            pool.memset(minus_half[:, :], -0.5)
            pool.wait_ge(s_const, 4)
            pool.affine_select(out=last_skip[:, 1:2], in_=last_skip[:, 1:2], compare_op=ALU.not_equal,
                               fill=float(SKIP), base=-(HC - 1), pattern=[[0, 1]], channel_multiplier=1)
            pool.iota(e_slot[:, :], [[CAP, E]], base=1, channel_multiplier=0,
                      allow_small_or_imprecise_dtypes=True).then_inc(s_const2, 1)
            pool.wait_ge(s_padl, 16)
            pool.wait_ge(s_slotA, 1)
            for i in range(NTOK):
                pool.indirect_dma_start(tok_list, bass.IndirectOffsetOnAxis(ap=slotU[:, i:i + 1], axis=0),
                                        tok_id[:, i:i + 1], None, bounds_check=NT * P - 1,
                                        oob_is_err=False).then_inc(s_lsc, 16)
            pool.wait_ge(s_list, 1)

            def rstdA(j):
                pool.wait_ge(s_var, j + 1)
                if j >= 2:
                    pool.wait_ge(s_hn, j - 1)
                pool.tensor_tensor(rsA[:, j % 2:j % 2 + 1], veA[:, j % 2:j % 2 + 1],
                                   minus_half[:, 0:1], ALU.pow).then_inc(s_rstd, 1)

            def gather(j):
                if j >= 2:
                    pool.wait_ge(s_x[j % 2], 16 * (j // 2))
                pool.indirect_dma_start(xs[:, j, :], None, x,
                                        bass.IndirectOffsetOnAxis(ap=list_g[:, j:j + 1], axis=0),
                                        bounds_check=T - 1, oob_is_err=False).then_inc(s_x[j % 2], 16)

            def scatter(j):
                pool.wait_ge(s_x1, j + 1)
                pool.indirect_dma_start(x1_rows, bass.IndirectOffsetOnAxis(ap=list_s[:, j:j + 1], axis=0),
                                        xs[:, j, :], None, bounds_check=T - 1,
                                        oob_is_err=False).then_inc(s_x1s, 16)
            AHEAD = 4
            for j in range(AHEAD):
                gather(j)
            rstdA(0)
            rstdA(1)
            for j in range(NT):
                if j + AHEAD < NT:
                    gather(j + AHEAD)
                if j + 2 < NT:
                    rstdA(j + 2)
                if j >= 1:
                    scatter(j - 1)
            scatter(NT - 1)
            for c in range(4):
                pool.wait_ge(s_varB, c + 1)
                pool.tensor_tensor(rsB[:, 4 * c:4 * c + 4], veB[:, 4 * c:4 * c + 4],
                                   minus_half[:, 0:4], ALU.pow).then_inc(s_rstdB, 1)
            for i in range(NTOK):
                pool.wait_ge(s_hnB, i + 1)
                pool.tensor_copy(rows[:, i, 0:H], hnB[:, i % 2, :]).then_inc(s_row, 1)
            pool.tensor_copy(rows[:, :, RW - 1:RW], tok_id[:, :].unsqueeze(2)).then_inc(s_row, 1)
            pool.wait_ge(s_row, NTOK + 1)
            pool.wait_ge(s_slot, 1)
            pool.wait_ge(s_pad, 16 * 8)
            for i in range(NTOK):
                for k in range(TOPK):
                    pool.indirect_dma_start(slots, bass.IndirectOffsetOnAxis(ap=slot_of[:, i, k:k + 1], axis=0),
                                            rows[:, i, :], None, bounds_check=E * CAP - 1,
                                            oob_is_err=False).then_inc(s_disp, 16)
            pool.wait_ge(s_st[0], 16 * NGRP // 2)
            pool.wait_ge(s_st[1], 16 * NGRP // 2)

            def add_rows(e, par):
                pool.wait_ge(s_wc, 2 * (e + 1))
                at_least(pool, s_add, 32 * e)
                for c in range(2):
                    wait_apart(pool, s_ot, 2 * e + c + 1)
                    pool.indirect_dma_start(out, bass.IndirectOffsetOnAxis(ap=tokc[:, par, c:c + 1], axis=0),
                                            ot[:, par, c, :], None, bounds_check=T - 1, oob_is_err=False,
                                            compute_op=ALU.add).then_inc(s_add, 16)
            add_rows(0, 0)
            add_rows(1, 1)
            with pool.Fori(0, E // 2 - 1) as it:
                for p in range(2):
                    add_rows(2 * it + 2 + p, p)
            for r in range(4):
                pool.wait_ge(s_fe, 4 * (r + 1))
                if r == 0:
                    pool.wait_ge(s_add, 32 * E)
                pool.dma_start(out_tiled[:, 4 * r:4 * r + 4, :], fb[:, 4 * r:4 * r + 4, :],
                               accum_op=ALU.add).then_inc(s_fa, 16)
            pool.wait_ge(s_fa, 64)

        @block.scalar
        def _(act):
            act.wait_ge(s_const, 1)
            act.dma_start(tok_list.rearrange("(p j) o -> p (j o)", p=P), padA[:, :]).then_inc(s_padl, 16)
            act.wait_ge(s_gates, 32)
            nc.scalar.activation(tg[:, :], gates[:, :], ACT.Tanh).then_inc(s_tg, 1)
            for e in range(XE):
                act.wait_ge(s_wx[e], 16)
                n = KH * XF
                nc.scalar.activation(parts[:, e * n:(e + 1) * n], raw[:, e * n:(e + 1) * n], ACT.Copy).then_inc(s_wxhi, 1)

            def hi1(j, p):
                act.wait_ge(s_t1, j + 1)
                at_least(act, s_mm1, j - 1 if not isinstance(j, int) or j > 1 else 0)
                nc.scalar.activation(hT[:, p, 0].rearrange("p k n -> p (k n)"), PS[:, 0, :], ACT.Copy).then_inc(s_h1hi, 1)

            def stepA(j, p, more):
                act.wait_ge(s_mm1, j + 1)
                if not isinstance(j, int) or j > 1:
                    act.wait_ge(s_ac, j - 1)
                nc.scalar.activation(suA[:, p, :], PS[:, 2 + p, :], ACT.Silu).then_inc(s_su, 1)
                if more:
                    hi1(j + 1, 1 - p)
                act.wait_ge(s_t2, j + 1)
                if not isinstance(j, int) or j > 1:
                    act.wait_ge(s_mm2, j - 1)
                nc.scalar.activation(aT[:, p, 0].rearrange("p k n -> p (k n)"), PS[:, 1, :], ACT.Copy).then_inc(s_h2hi, 1)
            hi1(0, 0)
            stepA(0, 0, True)
            stepA(1, 1, True)
            stepA(2, 0, True)
            with act.Fori(0, (NT - 5) // 2) as it:
                stepA(2 * it + 3, 1, True)
                stepA(2 * it + 4, 0, True)
            stepA(NT - 2, 1, True)
            stepA(NT - 1, 0, False)
            act.wait_ge(s_mm2, NT)
            act.wait_ge(s_sh[0], 16)
            for n_, (lo, n, r) in enumerate(SH_CHUNKS):
                if n_ == KH:
                    act.wait_ge(s_sh[1], 32)
                nc.scalar.activation(sh_part(0, lo, n, r), raw[0:r, lo:lo + n], ACT.Copy).then_inc(s_shhi, 1)

            def keepT(i, p):
                act.wait_ge(s_tB, i + 1)
                if not isinstance(i, int) or i > 1:
                    act.wait_ge(s_lg, i - 1)
                nc.scalar.activation(hTf[:, p].rearrange("p k n -> p (k n)"), PS[:, p, :], ACT.Copy).then_inc(s_hTf, 1)
            keepT(0, 0)
            keepT(1, 1)
            with act.Fori(0, NTOK // 2 - 1) as it:
                keepT(2 * it + 2, 0)
                keepT(2 * it + 3, 1)

            def hiB(g, gp):
                for q in range(GROUP):
                    act.wait_ge(s_tg2, GROUP * g + q + 1)
                    if not isinstance(g, int) or g > 1:
                        act.wait_ge(s_gu, 6 * (g - 1))
                    nc.scalar.activation(hTg[:, gp, 0, :, q * P:(q + 1) * P],
                                         PS[:, q, :].rearrange("p (k n) -> p k n", k=KH), ACT.Copy).then_inc(s_ghi, 1)

            def stepB(g, gp, more):
                for m in range(6):
                    n = 6 * g + m
                    r = MST[m]
                    act.wait_ge(s_gu, n + 1)
                    if not isinstance(g, int) or n > 1:
                        act.wait_ge(s_acB, n - 1)
                    nc.scalar.activation(suB[0:r, m % 2, :], PS[0:r, 2 + m % 2, 0:GN], ACT.Silu).then_inc(s_suB, 1)
                    act.wait_ge(s_acB, n + 1)
                    if not isinstance(g, int) or g > 0:
                        act.wait_ge(s_dn, GROUP * g)
                    nc.scalar.activation(actB[0:r, 0, m, :], acB[0:r, m % 2, :], ACT.Copy).then_inc(s_bhi, 1)
                if more:
                    hiB(g + 1, 1 - gp)

            def over_copy(c):
                act.wait_ge(s_ovT, c + 1)
                nc.scalar.activation(over_wT[:, 4 * c:4 * c + 4, :].rearrange("e i t -> e (i t)"),
                                     PS[0:E, 6 + c % 2, :], ACT.Copy).then_inc(s_ovTc, 1)
            hiB(0, 0)
            act.wait_ge(s_d, 1)
            nc.scalar.activation(z1[:, :, 0:E], z0[:, :, 0:E], ACT.Exp).then_inc(s_exp, 1)
            stepB(0, 0, True)
            stepB(1, 1, True)
            for c in range(4):
                over_copy(c)
            with act.Fori(0, NGRP // 2 - 2) as it:
                stepB(2 * it + 2, 0, True)
                stepB(2 * it + 3, 1, True)
            stepB(NGRP - 2, 0, True)
            stepB(NGRP - 1, 1, False)

            def hi_w(e, par, k):
                lo, n, r = W_CHUNKS[k]
                nc.scalar.activation(w_part(par, 0, lo, n, r), raw[0:r, par * WE + lo:par * WE + lo + n], ACT.Copy).then_inc(s_whi, 1)

            def wait_w(e, par):
                act.wait_ge(s_raw[par], (e - par) * 24 + 48)
                if not isinstance(e, int) or e > 1:
                    act.wait_ge(s_cd, 2 * (e - 1))

            def hi_x(e, par):
                act.wait_ge(s_tx, e + 1)
                if not isinstance(e, int) or e > 1:
                    act.wait_ge(s_cgu, 3 * (e - 1))
                for b_ in range(2):
                    nc.scalar.activation(xT[:, par, 0, 2 * b_:2 * b_ + 2, :].rearrange("p k n -> p (k n)"),
                                         PS[:, 3 + b_, 0:2 * CAP], ACT.Copy).then_inc(s_xhi, 1)

            def stepC(e, par, more):
                if more:
                    wait_w(e + 1, 1 - par)
                    hi_w(e + 1, 1 - par, 0)
                for m in range(3):
                    r = MT[m]
                    act.wait_ge(s_cgu, 3 * e + m + 1)
                    at_least(act, s_cac, 3 * e + m - 2 if not isinstance(e, int) or e > 0 else 0)
                    nc.scalar.activation(suC[0:r, m, :], PS[0:r, m, 0:CAP], ACT.Silu).then_inc(s_csu, 1)
                    act.wait_ge(s_cac, 3 * e + m + 1)
                    if not isinstance(e, int) or e > 1:
                        act.wait_ge(s_cd, 2 * (e - 1))
                    nc.scalar.activation(actC[0:r, par, 0, m, :], acC[0:r, m, :], ACT.Copy).then_inc(s_ahi, 1)
                    if more:
                        for k in ((1, 2), (3, 4), (5, 6))[m]:
                            hi_w(e + 1, 1 - par, k)
                if more:
                    hi_x(e + 1, 1 - par)
                act.wait_ge(s_wc, 2 * (e + 1))
                if not isinstance(e, int) or e > 1:
                    act.wait_ge(s_add, 32 * (e - 1))
                    act.wait_ge(s_last[par], (e - par) * 8)
                for c in range(2):
                    act.wait_ge(s_cd, 2 * e + c + 1)
                    nc.scalar.activation(ot[:, par, c, :], PS[0:HC, 5 + c, :], ACT.Copy,
                                         scale=wcol[:, par, c:c + 1]).then_inc(s_ot, 1)
                act.wait_ge(s_ot, 2 * (e + 1))
                act.dma_start(last_rows[bass.ds(e, 1), :], ot[HC - 1:HC, par, 1, :]).then_inc(s_last[par], 16)
            act.wait_ge(s_dn, NTOK)
            wait_w(0, 0)
            for k in range(len(W_CHUNKS)):
                hi_w(0, 0, k)
            hi_x(0, 0)
            stepC(0, 0, True)
            stepC(1, 1, True)
            with act.Fori(0, E // 2 - 2) as it:
                stepC(2 * it + 2, 0, True)
                stepC(2 * it + 3, 1, True)
            stepC(E - 2, 0, True)
            stepC(E - 1, 1, False)
            for i in range(NTOK):
                act.wait_ge(s_f, i + 1)
                nc.scalar.activation(fb[:, i, :], PS[:, i % 2, :], ACT.Copy).then_inc(s_fe, 1)

        @block.vector
        def _(dve):
            v = nc.vector
            count = [0]

            def link(ins):
                count[0] += 1
                ins.then_inc(v_a, 1)
                dve.wait_ge(v_a, count[0])
            dve.wait_ge(s_tid, 16)
            link(v.tensor_copy(tidf[:, :], tidi[:, :]))
            v.memset(ge[:, 0, :], 1.0)
            v.memset(ge[:, XE, :], 0.0)
            for e in range(1, XE - 1):
                v.tensor_scalar(ge[:, e, :], tidf[:, :], float(e * PER_EXPERT), None, ALU.is_ge)
            link(v.tensor_scalar(ge[:, XE - 1, :], tidf[:, :], float((XE - 1) * PER_EXPERT), None, ALU.is_ge))
            v.memset(preA[:, :, 0:1], 0.0)
            link(v.tensor_tensor(ohA[:, :, :], ge[:, 0:XE, :], ge[:, 1:XE + 1, :], ALU.subtract))
            for i in range(NTOK):
                link(v.tensor_tensor(preA[:, :, i + 1], preA[:, :, i], ohA[:, :, i], ALU.add))
            v.memset(tilesA[:, :], 0.0).then_inc(s_ohA, 1)
            dve.wait_ge(s_cntA, 1)
            dve.wait_ge(s_const2, 2)
            dve.wait_ge(s_ohA, 1)
            link(v.tensor_copy(cntA[:, :], PS[:, 6, 64:64 + XE]))
            link(v.tensor_tensor(over_m[:, :, :], cntA[:, :].unsqueeze(2).broadcast_to([P, XE, NTOK]),
                                 limit[:, :, :], ALU.is_gt))
            v.memset(startA[:, 0:1], 0.0)
            link(v.tensor_reduce(tilesA[:, :], over_m[:, :, :], X, ALU.add))
            for e in range(1, XE):
                link(v.tensor_tensor(startA[:, e:e + 1], startA[:, e - 1:e], tilesA[:, e - 1:e], ALU.add))
            link(v.tensor_scalar(base_slot[:, :], startA[:, :], float(P), None, ALU.mult))
            link(v.tensor_tensor(posA[:, :, :], PS[:, 6, 0:64].rearrange("p (e i) -> p e i", e=XE),
                                 base_slot[:, :].unsqueeze(2).broadcast_to([P, XE, NTOK]), ALU.add))
            link(v.tensor_tensor(posB[:, :, :], posA[:, :, :], ohA[:, :, :], ALU.mult))
            link(v.tensor_reduce(slotA[:, :], posB[:, :, :].rearrange("p e i -> p i e"), X, ALU.add))
            v.tensor_copy(slotU[:, :], slotA[:, :]).then_inc(s_slotA, 1)
            link(v.tensor_scalar(tile_e[:, 0, :], tile_no[:, :], startA[0:1, 1:2], None, ALU.is_ge))
            for e in (2, 3):
                link(v.scalar_tensor_tensor(tile_e[:, e - 1, :], tile_no[:, :], startA[0:1, e:e + 1],
                                            tile_e[:, e - 2, :], ALU.is_ge, ALU.add))
            v.tensor_scalar(tile_w[:, :], tile_e[:, 2, :], float(KH * XF), None, ALU.mult).then_inc(s_slotA, 1)
            for e in range(XE):
                dve.wait_ge(s_wxhi, e + 1)
                n = KH * XF
                v.tensor_tensor(parts[:, half + e * n:half + (e + 1) * n], raw[:, e * n:(e + 1) * n],
                                parts[:, e * n:(e + 1) * n].bitcast(F32), ALU.subtract).then_inc(s_wxlo, 1)
            dve.wait_ge(s_lT, 1)
            v.tensor_scalar(list_g[:, :], PS[:, 7, 0:NT], float(T - 1), None, ALU.min)
            v.tensor_copy(list_s[:, :], PS[:, 7, 0:NT]).then_inc(s_list, 1)
            dve.wait_ge(s_tg, 1)

            stat = sem("statsA")

            def stats(j, p, between=None):
                dve.wait_ge(s_x[p], (j - p) * 8 + 16)
                v.bn_stats(st6[:, p, :], xs[:, bass.ds(j, 1), :].rearrange("p o h -> p (o h)")).then_inc(stat, 1)
                dve.wait_ge(stat, 2 * j + 1)
                if between is not None:
                    between()
                v.bn_aggr(mvA[:, p, :], st6[:, p, :]).then_inc(stat, 1)
                dve.wait_ge(stat, 2 * j + 2)
                if not isinstance(j, int) or j > 1:
                    dve.wait_ge(s_rstd, j - 1)
                v.tensor_scalar(veA[:, p:p + 1], mvA[:, p, 1:2], EPS, None, ALU.add).then_inc(s_var, 1)

            def norm(j, p):
                dve.wait_ge(s_rstd, j + 1)
                if not isinstance(j, int) or j > 1:
                    dve.wait_ge(s_t1, j - 1)
                v.tensor_scalar(hn[:, p, :], xs[:, bass.ds(j, 1), :].rearrange("p o h -> p (o h)"),
                                mvA[:, p, 0:1], rsA[:, p:p + 1], ALU.subtract, ALU.mult).then_inc(s_hn, 1)

            def lo1(j, p):
                dve.wait_ge(s_h1hi, j + 1)
                v.tensor_tensor(hT[:, p, 1].rearrange("p k n -> p (k n)"), PS[:, 0, :],
                                hT[:, p, 0].rearrange("p k n -> p (k n)").bitcast(F32), ALU.subtract).then_inc(s_h1lo, 1)

            def product(j, p):
                dve.wait_ge(s_su, j + 1)
                if not isinstance(j, int) or j > 1:
                    dve.wait_ge(s_t2, j - 1)
                v.tensor_tensor(acA[:, p, :], PS[:, 2 + p, :], suA[:, p, :], ALU.mult).then_inc(s_ac, 1)

            def lo2(j, p):
                dve.wait_ge(s_h2hi, j + 1)
                v.tensor_tensor(aT[:, p, 1].rearrange("p k n -> p (k n)"), PS[:, 1, :],
                                aT[:, p, 0].rearrange("p k n -> p (k n)").bitcast(F32), ALU.subtract).then_inc(s_h2lo, 1)

            def resid(j, p):
                dve.wait_ge(s_mm2, j + 1)
                row = xs[:, bass.ds(j, 1), :].rearrange("p o h -> p (o h)")
                v.scalar_tensor_tensor(row, PS[:, 4 + p, :], tg[:, 0:1], row, ALU.mult, ALU.add).then_inc(s_x1, 1)

            for j in range(2):
                stats(j, j)
            norm(0, 0)
            lo1(0, 0)

            def stepA(j, p, more, more2):
                if more:
                    norm(j + 1, 1 - p)
                product(j, p)
                if more:
                    lo1(j + 1, 1 - p)
                if more2:
                    stats(j + 2, p, (lambda: resid(j - 1, 1 - p)) if not isinstance(j, int) or j > 0 else None)
                elif j > 0:
                    resid(j - 1, 1 - p)
                lo2(j, p)
            stepA(0, 0, True, True)
            stepA(1, 1, True, True)
            stepA(2, 0, True, True)
            with dve.Fori(0, (NT - 5) // 2) as it:
                stepA(2 * it + 3, 1, True, True)
                stepA(2 * it + 4, 0, True, True)
            stepA(NT - 2, 1, True, False)
            stepA(NT - 1, 0, False, False)
            resid(NT - 1, 0)

            for n_, (lo, n, r) in enumerate(SH_CHUNKS):
                dve.wait_ge(s_shhi, n_ + 1)
                v.tensor_tensor(sh_part(1, lo, n, r), raw[0:r, lo:lo + n],
                                sh_part(0, lo, n, r).bitcast(F32), ALU.subtract).then_inc(s_shlo, 1)
            statB = sem("statsB")
            for i in range(NTOK):
                if i % 4 == 0:
                    dve.wait_ge(s_x1l[i // 4], 16)
                v.bn_stats(st6[:, i % 2, :], rows[:, i, 0:H]).then_inc(statB, 1)
                dve.wait_ge(statB, 2 * i + 1)
                v.bn_aggr(mvB[:, i, :], st6[:, i % 2, :]).then_inc(statB, 1)
                if i % 4 == 3:
                    dve.wait_ge(statB, 2 * i + 2)
                    v.tensor_scalar(veB[:, i - 3:i + 1], mvB[:, i - 3:i + 1, 1], EPS, None, ALU.add).then_inc(s_varB, 1)

            def normB(i, p):
                if isinstance(i, int) and i % 4 == 0:
                    dve.wait_ge(s_rstdB, i // 4 + 1)
                if not isinstance(i, int) or i > 1:
                    dve.wait_ge(s_tB, i - 1)
                    dve.wait_ge(s_row, i - 1)
                ii = bass.ds(i, 1)
                v.tensor_scalar(hnB[:, p, :], rows[:, ii, 0:H].rearrange("p o h -> p (o h)"),
                                mvB[:, ii, 0:1].rearrange("p o h -> p (o h)"), rsB[:, ii],
                                ALU.subtract, ALU.mult).then_inc(s_hnB, 1)

            def keep_logits(i, p):
                dve.wait_ge(s_lg, i + 1)
                v.tensor_copy(logits[:, bass.ds(i, 1), :].rearrange("p o e -> p (o e)"), PS[:, 2 + p, 0:E]).then_inc(s_lgc, 1)
            normB(0, 0)
            normB(1, 1)
            dve.wait_ge(s_rstdB, 4)
            with dve.Fori(0, NTOK // 2 - 1) as it:
                for p in range(2):
                    normB(2 * it + p + 2, p)
                    keep_logits(2 * it + p, p)
            keep_logits(NTOK - 2, 0)
            keep_logits(NTOK - 1, 1)

            rcount = [0]

            def rlink(ins):
                rcount[0] += 1
                ins.then_inc(v_r, 1)
                dve.wait_ge(v_r, rcount[0])

            def by_tile(t, n=E):
                return t[:, :].unsqueeze(2).broadcast_to([P, NTOK, n])

            def by_expert(t):
                return t[:, :].unsqueeze(1).broadcast_to([P, NTOK, E])

            def each(op, *a_):
                for i in range(NTOK):
                    ins = op(i)
                rlink(ins)

            def r0():
                dve.wait_ge(s_lgc, NTOK)
                rlink(v.tensor_reduce(mx[:, :], logits[:, :, :], X, ALU.max))
                v.tensor_tensor(z0[:, :, 0:E], logits[:, :, :], by_tile(mx), ALU.subtract).then_inc(s_d, 1)
                dve.wait_ge(s_d, 1)
                v.memset(z4[:, :, E:EW], BIG)
                v.memset(g13[:, :, NG:NG + 5], BIG)
                rlink(v.tensor_scalar(z3[:, :, 0:E], z0[:, :, 0:E], FLOOR, None, ALU.max))
                rlink(v.tensor_reduce(g13[:, :, 0:NG], z3[:, :, 0:E].rearrange("p i (g s) -> p i g s", g=NG), X, ALU.max))

            def r1():
                each(lambda i: v.max(g8[:, i, :], g13[:, i, :]))
                each(lambda i: v.match_replace(g13r[:, i, :], g8[:, i, :], g13[:, i, :], -BIG))
                rlink(v.tensor_scalar(pen[:, :, :], g13r[:, :, 0:NG], -BIG, BIG, ALU.is_equal, ALU.mult))
                rlink(v.tensor_scalar(g8[:, :, :], pen[:, :, :], FLOOR, None, ALU.add))
                rlink(v.tensor_tensor(z4[:, :, 0:E].rearrange("p i (g s) -> p i g s", g=NG),
                                      z3[:, :, 0:E].rearrange("p i (g s) -> p i g s", g=NG),
                                      g8[:, :, :].unsqueeze(3).broadcast_to([P, NTOK, NG, GS]), ALU.min))

            def r2():
                each(lambda i: v.max(key8[:, i, :], z4[:, i, :]))
                each(lambda i: v.match_replace(z5[:, i, :], key8[:, i, :], z4[:, i, :], -BIG))
                v.memset(pre[:, 0, :], 0.0)
                rlink(v.tensor_scalar(mask[:, :, :], z5[:, :, 0:E], -BIG, None, ALU.is_equal))

            def r3():
                for i in range(NTOK):
                    rlink(v.tensor_tensor(pre[:, i + 1, :], pre[:, i, :], mask[:, i, :], ALU.add))
                v.memset(sm[:, :], 0.0).then_inc(s_pre, 1)

            def r4():
                dve.wait_ge(s_exp, 1)
                dve.wait_ge(s_pre, 1)
                rlink(v.tensor_reduce(sm[:, :], z1[:, :, 0:E], X, ALU.add))
                rlink(v.reciprocal(rc[:, :], sm[:, :]))
                rlink(v.tensor_tensor(z2[:, :, 0:E], z1[:, :, 0:E], by_tile(rc), ALU.mult))
                dve.wait_ge(s_cnt, 1)
                v.tensor_scalar(cm1[:, :], PS[:, 6, 0:E], -1.0, None, ALU.add).then_inc(s_cm1, 1)

            def r5():
                dve.wait_ge(s_pos, 1)
                dve.wait_ge(s_cm1, 1)
                pos = PS[:, 6:8, :].rearrange("p b (i e) -> p (b i) e", e=E)
                v.scalar_tensor_tensor(z0[:, :, 0:E], pos, float(CAP - 1), mask[:, :, :], ALU.is_lt, ALU.mult)
                rlink(v.tensor_tensor(z1[:, :, 0:E], pos, by_expert(cm1), ALU.is_equal))
                rlink(v.scalar_tensor_tensor(z3[:, :, 0:E], pos, float(CAP - 1), z1[:, :, 0:E], ALU.is_ge, ALU.mult))
                rlink(v.tensor_tensor(z1[:, :, 0:E], z3[:, :, 0:E], mask[:, :, :], ALU.mult))
                rlink(v.scalar_tensor_tensor(z5[:, :, 0:E], pos, float(CAP - 1), by_expert(e_slot), ALU.min, ALU.add))
                rlink(v.tensor_tensor(z4[:, :, 0:E], z0[:, :, 0:E], z1[:, :, 0:E], ALU.add))
                rlink(v.tensor_tensor(z7[:, :, 0:E], z4[:, :, 0:E], z5[:, :, 0:E], ALU.mult))
                each(lambda i: v.max(key8[:, i, :], z7[:, i, 0:E]))
                rlink(v.tensor_scalar(none8[:, :, :], key8[:, :, :], 0.0, float(NOSLOT), ALU.is_le, ALU.mult))
                v.scalar_tensor_tensor(slot_of[:, :, :], key8[:, :, :], -1.0, none8[:, :, :], ALU.add, ALU.add)
                rlink(v.tensor_tensor(z3[:, :, 0:E], z0[:, :, 0:E], z2[:, :, 0:E], ALU.mult))
                dve.wait_ge(s_row, NTOK)
                v.tensor_tensor(rows[:, :, H:H + E], z3[:, :, 0:E], z1[:, :, 0:E], ALU.add).then_inc(s_slot, 1)

            def r6():
                rlink(v.tensor_tensor(z4[:, :, 0:E], mask[:, :, :], z0[:, :, 0:E], ALU.subtract))
                v.tensor_tensor(over_w[:, :, :], z4[:, :, 0:E], z2[:, :, 0:E], ALU.mult).then_inc(s_over, 1)
            pieces = [r0, r1, r2, r3, r4, r5, r6]

            def norm_group(g, gp):
                dve.wait_ge(s_xr[gp], (g - gp) * 8 + 16)
                for q in range(GROUP):
                    i = GROUP * g + q
                    if isinstance(g, int) and g == 0:
                        dve.wait_ge(s_tB, NTOK - 1 + q)
                        dve.wait_ge(s_row, NTOK - 1 + q)
                    else:
                        dve.wait_ge(s_tg2, i - 1)
                    ii = bass.ds(i, 1)
                    v.tensor_scalar(hnB[:, q, :], xrow[:, gp, q, :], mvB[:, ii, 0:1].rearrange("p o h -> p (o h)"),
                                    rsB[:, ii], ALU.subtract, ALU.mult).then_inc(s_hg, 1)

            def loB(g, gp):
                for q in range(GROUP):
                    dve.wait_ge(s_ghi, GROUP * g + q + 1)
                    v.tensor_tensor(hTg[:, gp, 1, :, q * P:(q + 1) * P], PS[:, q, :].rearrange("p (k n) -> p k n", k=KH),
                                    hTg[:, gp, 0, :, q * P:(q + 1) * P].bitcast(F32), ALU.subtract).then_inc(s_glo, 1)

            def stepB(g, gp, more, routing=()):
                if more:
                    norm_group(g + 1, 1 - gp)
                for m in range(6):
                    n, r = 6 * g + m, MST[m]
                    dve.wait_ge(s_suB, n + 1)
                    if not isinstance(g, int) or n > 1:
                        dve.wait_ge(s_bhi, n - 1)
                    v.tensor_tensor(acB[0:r, m % 2, :], PS[0:r, 2 + m % 2, GN:2 * GN], suB[0:r, m % 2, :], ALU.mult).then_inc(s_acB, 1)
                    dve.wait_ge(s_bhi, n + 1)
                    v.tensor_tensor(actB[0:r, 1, m, :], acB[0:r, m % 2, :], actB[0:r, 0, m, :].bitcast(F32),
                                    ALU.subtract).then_inc(s_blo, 1)
                    if m < len(routing):
                        routing[m]()
                if more:
                    loB(g + 1, 1 - gp)
                for q in range(GROUP):
                    dve.wait_ge(s_dn, GROUP * g + q + 1)
                    v.scalar_tensor_tensor(xrow[:, gp, q, :], PS[:, 4 + q, :], tg[:, 1:2], xrow[:, gp, q, :],
                                           ALU.mult, ALU.add).then_inc(s_res, 1)
            norm_group(0, 0)
            loB(0, 0)
            r0()
            stepB(0, 0, True, pieces[1:5])
            stepB(1, 1, True, pieces[5:])
            with dve.Fori(0, NGRP // 2 - 2) as it:
                stepB(2 * it + 2, 0, True)
                stepB(2 * it + 3, 1, True)
            stepB(NGRP - 2, 0, True)
            stepB(NGRP - 1, 1, False)

            def lo_w(e, par, k):
                lo, n, r = W_CHUNKS[k]
                dve.wait_ge(s_whi, 7 * e + k + 1)
                v.tensor_tensor(w_part(par, 1, lo, n, r), raw[0:r, par * WE + lo:par * WE + lo + n],
                                w_part(par, 0, lo, n, r).bitcast(F32), ALU.subtract).then_inc(s_wlo, 1)

            def lo_x(e, par):
                for b_ in range(2):
                    dve.wait_ge(s_xhi, 2 * e + b_ + 1)
                    v.tensor_tensor(xT[:, par, 1, 2 * b_:2 * b_ + 2, :].rearrange("p k n -> p (k n)"), PS[:, 3 + b_, 0:2 * CAP],
                                    xT[:, par, 0, 2 * b_:2 * b_ + 2, :].rearrange("p k n -> p (k n)").bitcast(F32),
                                    ALU.subtract).then_inc(s_xlo, 1)

            def weights_of(e, par):
                dve.wait_ge(s_xg[par], (e - par) * 8 + 16)
                if not isinstance(e, int) or e > 1:
                    dve.wait_ge(s_add, 32 * (e - 1))
                    dve.wait_ge(s_ot, 2 * (e - 1))
                v.tensor_scalar(wcol[:, par, :], xg[:, par, :, bass.ds(e + H, 1)].rearrange("p c o -> p (c o)"),
                                tg[0:HC, 1:2], None, ALU.mult).then_inc(s_wc, 1)
                v.tensor_tensor(tokc[:, par, :], xg[:, par, :, RW - 1], last_skip[:, :], ALU.add).then_inc(s_wc, 1)

            def stepC(e, par, more):
                weights_of(e, par)
                for m in range(3):
                    r = MT[m]
                    dve.wait_ge(s_csu, 3 * e + m + 1)
                    if not isinstance(e, int) or e > 0:
                        dve.wait_ge(s_ahi, 3 * e + m - 2)
                    v.tensor_tensor(acC[0:r, m, :], PS[0:r, m, CAP:2 * CAP], suC[0:r, m, :], ALU.mult).then_inc(s_cac, 1)
                    dve.wait_ge(s_ahi, 3 * e + m + 1)
                    v.tensor_tensor(actC[0:r, par, 1, m, :], acC[0:r, m, :], actC[0:r, par, 0, m, :].bitcast(F32),
                                    ALU.subtract).then_inc(s_alo, 1)
                    if more:
                        for k in ((0, 1), (2,), (3,))[m]:
                            lo_w(e + 1, 1 - par, k)
                if more:
                    lo_x(e + 1, 1 - par)
                    for k in range(KH, 7):
                        lo_w(e + 1, 1 - par, k)
            for k in range(7):
                lo_w(0, 0, k)
            lo_x(0, 0)
            stepC(0, 0, True)
            stepC(1, 1, True)
            with dve.Fori(0, E // 2 - 2) as it:
                stepC(2 * it + 2, 0, True)
                stepC(2 * it + 3, 1, True)
            stepC(E - 2, 0, True)
            stepC(E - 1, 1, False)

        @block.tensor
        def _(pe):
            mm = nc.tensor.matmul

            def split_product(dst, terms):
                for n, (ah, al, bh, bl) in enumerate(terms):
                    mm(dst, ah, bh, start=(n == 0), stop=False)
                    mm(dst, ah, bl, start=False, stop=False)
                    last = mm(dst, al, bh, start=False, stop=(n == len(terms) - 1))
                return last

            pe.wait_ge(s_ohA, 1)
            pe.wait_ge(s_const2, 2)
            mm(PS[:, 6, 0:64], before[:, :], ohA[:, :, :].rearrange("p e i -> p (e i)"), start=True, stop=False)
            mm(PS[:, 6, 0:64], ones[:, :], preA[:, :, 0:NTOK], start=False, stop=True)
            mm(PS[:, 6, 64:64 + XE], ones[:, :], preA[:, :, NTOK], start=True, stop=True).then_inc(s_cntA, 1)
            pe.wait_ge(s_lld, 16)
            nc.tensor.transpose(PS[:, 7, 0:NT], listT[:, :], ident[0:NT, 0:NT]).then_inc(s_lT, 1)

            def turn1(j, p):
                pe.wait_ge(s_hn, j + 1)
                if not isinstance(j, int) or j > 0:
                    pe.wait_ge(s_h1lo, j)
                for k in range(KH):
                    last = nc.tensor.transpose(PS[:, 0, k * P:(k + 1) * P], hn[:, p, k * P:(k + 1) * P], ident[:, :])
                last.then_inc(s_t1, 1)

            def weights_at(w0):
                return [(parts[:, bass.ds(w0 + k * XF, XF)], parts[:, bass.ds(w0 + (half + k * XF), XF)]) for k in range(KH)]

            def first(j, p):
                w0 = nc.tensor.value_load(tile_w[0:1, bass.ds(j, 1)], min_val=0, max_val=(XE - 1) * KH * XF)
                pe.wait_ge(s_h1lo, j + 1)
                if not isinstance(j, int) or j > 1:
                    pe.wait_ge(s_ac, j - 1)
                split_product(PS[:, 2 + p, :], [(hT[:, p, 0, k, :], hT[:, p, 1, k, :], wh, wl)
                                                for k, (wh, wl) in enumerate(weights_at(w0))]).then_inc(s_mm1, 1)

            def second(j, p):
                w0 = nc.tensor.value_load(tile_w[0:1, bass.ds(j, 1)], min_val=0, max_val=(XE - 1) * KH * XF)
                pe.wait_ge(s_h2lo, j + 1)
                if not isinstance(j, int) or j > 1:
                    pe.wait_ge(s_x1, j - 1)
                split_product(PS[:, 4 + p, :], [(aT[:, p, 0, k, :], aT[:, p, 1, k, :], wh, wl)
                                                for k, (wh, wl) in enumerate(weights_at(w0))]).then_inc(s_mm2, 1)

            def turn2(j, p):
                pe.wait_ge(s_ac, j + 1)
                if not isinstance(j, int) or j > 0:
                    pe.wait_ge(s_h2lo, j)
                for k in range(KH):
                    last = nc.tensor.transpose(PS[:, 1, k * P:(k + 1) * P], acA[:, p, k * P:(k + 1) * P], ident[:, :])
                last.then_inc(s_t2, 1)

            def stepA(j, p, more):
                first(j, p)
                if more:
                    turn1(j + 1, 1 - p)
                if not isinstance(j, int) or j > 0:
                    second(j - 1, 1 - p)
                turn2(j, p)
            turn1(0, 0)
            pe.wait_ge(s_wxlo, XE)
            pe.wait_ge(s_slotA, 2)
            stepA(0, 0, True)
            stepA(1, 1, True)
            stepA(2, 0, True)
            with pe.Fori(0, (NT - 5) // 2) as it:
                stepA(2 * it + 3, 1, True)
                stepA(2 * it + 4, 0, True)
            stepA(NT - 2, 1, True)
            stepA(NT - 1, 0, False)
            second(NT - 1, 0)

            pe.wait_ge(s_gatew, 16)
            pe.wait_ge(s_h2lo, NT)
            pe.wait_ge(s_ac, NT)

            def turnB(i, p):
                pe.wait_ge(s_hnB, i + 1)
                if not isinstance(i, int) or i > 1:
                    pe.wait_ge(s_hTf, i - 1)
                for k in range(KH):
                    last = nc.tensor.transpose(PS[:, p, k * P:(k + 1) * P], hnB[:, p, k * P:(k + 1) * P], ident[:, :])
                last.then_inc(s_tB, 1)

            def logit(i, p):
                pe.wait_ge(s_hTf, i + 1)
                if not isinstance(i, int) or i > 1:
                    pe.wait_ge(s_lgc, i - 1)
                for k in range(KH):
                    last = mm(PS[:, 2 + p, 0:E], hTf[:, p, k, :], gate_w[:, k, :], start=(k == 0), stop=(k == KH - 1))
                last.then_inc(s_lg, 1)
            turnB(0, 0)
            turnB(1, 1)
            for i in range(2):
                logit(i, i)
                turnB(i + 2, i)
            with pe.Fori(0, NTOK // 2 - 2) as it:
                for p in range(2):
                    logit(2 * it + p + 2, p)
                    turnB(2 * it + p + 4, p)
            logit(NTOK - 2, 0)
            logit(NTOK - 1, 1)

            def turn_group(g, gp):
                for q in range(GROUP):
                    pe.wait_ge(s_hg, GROUP * g + q + 1)
                    if isinstance(g, int) and g == 0:
                        pe.wait_ge(s_hTf, NTOK)
                    else:
                        pe.wait_ge(s_glo, GROUP * g + q - 1)
                    for k in range(KH):
                        last = nc.tensor.transpose(PS[:, q, k * P:(k + 1) * P], hnB[:, q, k * P:(k + 1) * P], ident[:, :])
                    last.then_inc(s_tg2, 1)

            def gate_up(g, gp, m):
                n, r = 6 * g + m, MST[m]
                if not isinstance(g, int) or n > 1:
                    pe.wait_ge(s_acB, n - 1)
                for u in range(2):
                    terms = []
                    for k in range(KH):
                        lo = k * 2 * MS + u * MS + MSO[m]
                        terms.append((sh_part(0, lo, r), sh_part(1, lo, r), hTg[:, gp, 0, k, :], hTg[:, gp, 1, k, :]))
                    last = split_product(PS[0:r, 2 + m % 2, u * GN:(u + 1) * GN], terms)
                last.then_inc(s_gu, 1)

            def down(g, gp):
                def part(q, ms):
                    for m in ms:
                        r = MST[m]
                        lo = SGU + m * H
                        for pa, pb in ((0, 0), (0, 1), (1, 0)):
                            last = mm(PS[:, 4 + q, :], actB[0:r, pa, m, q * P:(q + 1) * P], sh_part(pb, lo, H, r),
                                      start=(m == 0 and pa == pb), stop=(m == 5 and pa == 1))
                    return last
                pe.wait_ge(s_blo, 6 * g + 5)
                if not isinstance(g, int) or g > 0:
                    pe.wait_ge(s_res, GROUP * g)
                for q in range(GROUP):
                    part(q, range(5))
                pe.wait_ge(s_blo, 6 * g + 6)
                for q in range(GROUP):
                    part(q, [5]).then_inc(s_dn, 1)

            def ranks():
                pe.wait_ge(s_pre, 1)
                mm(PS[:, 6, 0:E], ones[:, :], pre[:, NTOK, :], start=True, stop=True).then_inc(s_cnt, 1)
                pe.wait_ge(s_cm1, 1)
                for b_ in range(2):
                    dst = PS[:, 6 + b_, :]
                    mm(dst, before[:, :], mask[:, 8 * b_:8 * b_ + 8, :].rearrange("p i e -> p (i e)"), start=True, stop=False)
                    last = mm(dst, ones[:, :], pre[:, 8 * b_:8 * b_ + 8, :].rearrange("p i e -> p (i e)"), start=False, stop=True)
                last.then_inc(s_pos, 1)

            def turn_over():
                pe.wait_ge(s_over, 1)
                for c in range(4):
                    if c >= 2:
                        pe.wait_ge(s_ovTc, c - 1)
                    for n in range(4):
                        last = nc.tensor.transpose(PS[0:E, 6 + c % 2, n * P:(n + 1) * P], over_w[:, 4 * c + n, :], ident[:, :])
                    last.then_inc(s_ovT, 1)

            def stepB(g, gp, more):
                for m in range(6):
                    gate_up(g, gp, m)
                if more:
                    turn_group(g + 1, 1 - gp)
                down(g, gp)
            turn_group(0, 0)
            pe.wait_ge(s_shlo, len(SH_CHUNKS))
            pe.wait_ge(s_glo, GROUP)
            pe.wait_ge(s_lgc, NTOK)
            for m in range(6):
                gate_up(0, 0, m)
            ranks()
            turn_group(1, 1)
            down(0, 0)
            pe.wait_ge(s_glo, 2 * GROUP)
            stepB(1, 1, True)
            turn_over()
            with pe.Fori(0, NGRP // 2 - 2) as it:
                for p in range(2):
                    pe.wait_ge(s_glo, GROUP * (2 * it + 3 + p))
                    stepB(2 * it + 2 + p, p, True)
            pe.wait_ge(s_glo, GROUP * (NGRP - 1))
            stepB(NGRP - 2, 0, True)
            pe.wait_ge(s_glo, GROUP * NGRP)
            stepB(NGRP - 1, 1, False)

            def turn_x(e, par):
                pe.wait_ge(s_xg[par], (e - par) * 8 + 16)
                if not isinstance(e, int) or e > 0:
                    pe.wait_ge(s_xlo, 2 * e)
                for k in range(KH):
                    for c in range(2):
                        o = (k % 2) * CAP + c * HC
                        last = nc.tensor.transpose(PS[:, 3 + k // 2, o:o + HC], xg[:, par, c, k * P:(k + 1) * P], ident[0:HC, 0:HC])
                last.then_inc(s_tx, 1)

            def stepC(e, par, more):
                pe.wait_ge(s_xlo, 2 * (e + 1))
                pe.wait_ge(s_wlo, 7 * e + KH)
                for m in range(3):
                    r = MT[m]
                    if not isinstance(e, int) or e > 0:
                        pe.wait_ge(s_cac, 3 * e + m - 2)
                    for u in range(2):
                        terms = []
                        for k in range(KH):
                            lo = k * 2 * M + u * M + m * P
                            terms.append((w_part(par, 0, lo, r), w_part(par, 1, lo, r), xT[:, par, 0, k, :], xT[:, par, 1, k, :]))
                        last = split_product(PS[0:r, m, u * CAP:(u + 1) * CAP], terms)
                    last.then_inc(s_cgu, 1)
                if more:
                    turn_x(e + 1, 1 - par)
                pe.wait_ge(s_wlo, 7 * (e + 1))
                if not isinstance(e, int) or e > 0:
                    pe.wait_ge(s_ot, 2 * e)

                def part(c, ms):
                    for m in ms:
                        r = MT[m]
                        for pa, pb in ((0, 0), (0, 1), (1, 0)):
                            last = mm(PS[0:HC, 5 + c, :], actC[0:r, par, pa, m, c * HC:(c + 1) * HC],
                                      w_part(par, pb, WGU + m * H, H, r), start=(m == 0 and pa == pb), stop=(m == 2 and pa == 1))
                    return last
                pe.wait_ge(s_alo, 3 * e + 2)
                for c in range(2):
                    part(c, range(2))
                pe.wait_ge(s_alo, 3 * e + 3)
                for c in range(2):
                    part(c, [2]).then_inc(s_cd, 1)
            turn_x(0, 0)
            pe.wait_ge(s_acB, 6 * NGRP)
            pe.wait_ge(s_res, NTOK)
            stepC(0, 0, True)
            stepC(1, 1, True)
            with pe.Fori(0, E // 2 - 2) as it:
                stepC(2 * it + 2, 0, True)
                stepC(2 * it + 3, 1, True)
            stepC(E - 2, 0, True)
            stepC(E - 1, 1, False)

            pe.wait_ge(s_ll, 16)
            pe.wait_ge(s_ovTc, 4)
            pe.wait_ge(s_cac, 3 * E)
            for i in range(NTOK):
                if i >= 2:
                    pe.wait_ge(s_fe, i - 1)
                mm(PS[:, i % 2, :], over_wT[:, i, :], lastS[:, :], start=True, stop=True).then_inc(s_f, 1)


_OUTS = [((4, 512, 512), "float32")]


def kernel(x, itok_BxS_13_99985, ctx_2048, g_xattn, g_ffn, L0_ffn_gate_weight, L0_ffn_Wg, L0_ffn_Wu,
           L0_ffn_Wd, L0_ffn_Sg, L0_ffn_Su, L0_ffn_Sd):
    import numpy as np
    import concourse.bacc as bacc
    from concourse.bass_utils import run_bass_kernel_spmd

    def turned(w):
        w = np.asarray(w)
        n = w.ndim
        w = w.reshape(w.shape[:-1] + (w.shape[-1] // P, P))
        return np.moveaxis(np.moveaxis(w, -1, n - 2), -1, n - 1)

    def inner_tiles(w, whole):
        w = np.swapaxes(np.asarray(w), -1, -2)
        head = w[..., :whole * P, :].reshape(w.shape[:-2] + (whole, P, H))
        return np.moveaxis(head, -3, -2).reshape(w.shape[:-2] + (P, whole * H)), w[..., whole * P:, :]

    ffn_gu = np.concatenate([turned(L0_ffn_Wg), turned(L0_ffn_Wu)], axis=-1).reshape(E, P, WGU)
    wdA, wdB = inner_tiles(L0_ffn_Wd, 2)
    sgu = np.concatenate([turned(L0_ffn_Sg), turned(L0_ffn_Su)], axis=-1).reshape(P, SGU)
    sdA, sd_rest = inner_tiles(L0_ffn_Sd, 4)
    sdB = np.moveaxis(sd_rest.reshape(2, 96, H), 0, 1).reshape(96, 2 * H)
    arrays = {
        "x": np.asarray(x).reshape(T, H),
        "tid": np.asarray(itok_BxS_13_99985).reshape(NTOK, P).T,
        "ctxT": turned(ctx_2048).reshape(XE, P, KH * XF),
        "g_x": np.asarray(g_xattn).reshape(1, 1),
        "g_f": np.asarray(g_ffn).reshape(1, 1),
        "gateT": turned(L0_ffn_gate_weight),
        "wgu": ffn_gu, "wdA": wdA, "wdB": wdB, "sgu": sgu, "sdA": sdA, "sdB": sdB,
    }
    arrays = {k: np.ascontiguousarray(a) for k, a in arrays.items()}
    nc = bacc.Bacc("TRN2", target_bir_lowering=False, num_devices=1)
    args = [nc.dram_tensor(k, a.shape, mybir.dt.from_np(a.dtype), kind="ExternalInput").ap() for k, a in arrays.items()]
    out = nc.dram_tensor("out", (T, H), F32, kind="ExternalOutput").ap()
    build(nc, *args, out)
    r = run_bass_kernel_spmd(nc, [arrays], core_ids=[0])
    return r.results[0]["out"].reshape(4, 512, 512)
```

```python
from contextlib import ExitStack

import concourse.bass as bass
from concourse import mybir

P = 128
ALU = mybir.AluOpType
ACT = mybir.ActivationFunctionType
F32 = mybir.dt.float32
F32R = mybir.dt.float32r
BF16 = mybir.dt.bfloat16
I32 = mybir.dt.int32
U32 = mybir.dt.uint32
X = mybir.AxisListType.X

T, H = 2048, 512
KH = H // P
NTOK = T // P
XE, XF = 4, 512
PER_EXPERT = 25000 // XE
NT = NTOK + XE - 1
E, M = 64, 352
MT = [P, P, M - 2 * P]
CAP = 192
HC = CAP // 2
TOPK, NG, TOPG = 6, 8, 3
GS = E // NG
MS = 704
MST = [P] * 4 + [96] * 2
MSO = [P * min(i, 4) + 96 * max(i - 4, 0) for i in range(6)]
EPS = 1e-5
RW = H + E + 1
FLOOR = -87.3365
BIG = 1e30
SKIP = 2 * T
NOSLOT = 32768
GROUP = 2
NGRP = NTOK // GROUP
PADS = 32
GN = GROUP * P
WGU, WD = KH * 2 * M, 3 * H
WE = WGU + WD
SGU, SD = KH * 2 * MS, 6 * H
WX = XE * KH * XF


def at_least(engine, sem, value):
    if not isinstance(value, int) or value > 0:
        engine.wait_ge(sem, value)


def build(nc, x, tid, ctxT, g_x, g_f, gateT, wgu, wdA, wdB, sgu, sdA, sdB, out):
    x1_rows = nc.dram_tensor("x1_rows", [T, 2 * H], F32).ap()
    slots = nc.dram_tensor("slots", [E * CAP, RW], F32).ap()
    last_rows = nc.dram_tensor("last_rows", [E, H], F32).ap()

    ctx = ExitStack()
    with ctx:
        def sem(name):
            return ctx.enter_context(nc.semaphore(name))

        base = (nc.sbuf_base + 63) // 64 * 64
        top = [base]

        def sb(name, shape, dt, at=None):
            size = 1
            for d in shape[1:]:
                size *= d
            size *= 2 if dt == BF16 else 4
            size = (size + 31) // 32 * 32
            offset = top[0] if at is None else at
            t = nc.alloc_sbuf_tensor_at(name, shape, dt, offset=offset)
            if at is None:
                top[0] += size
            return t, offset, offset + size

        def keep(name, shape, dt):
            return sb(name, shape, dt)[0]

        ident = keep("ident", [P, P], F32)
        before = keep("before", [P, P], BF16)
        ones = keep("ones", [P, P], BF16)
        gate_w = keep("gate_w", [P, KH, E], F32)
        e_slot = keep("e_slot", [P, E], F32)
        tok_id = keep("tok_id", [P, NTOK], F32)
        pad_row = keep("pad_row", [P, RW], F32)
        minus_half = keep("minus_half", [P, KH], F32)
        last_skip = keep("last_skip", [HC, 2], F32)
        gates = keep("gates", [P, 2], F32)
        tg = keep("tg", [P, 2], F32)
        over_wT = keep("over_wT", [E, NTOK, P], F32)
        slot_of = keep("slot_of", [P, NTOK, 8], U32)
        logits, logits_at, _ = sb("logits", [P, NTOK, E], F32)
        over_w = sb("over_w", [P, NTOK, E], F32, at=logits_at)[0]

        parts = keep("parts", [P, 2 * max(WX, SGU + SD, 2 * WE)], F32R)
        half = 2 * WE
        raw, raw_at, raw_end = sb("raw", [P, 2 * WE], F32)
        assert WX <= 2 * WE and SGU + SD == 2 * WE
        xs, xs_at, xs_end = sb("xs", [P, NT, H], F32)
        rows = sb("rows", [P, NTOK, RW], F32, at=xs_at)[0]
        scratch = top[0]

        def region(start):
            at = [start]

            def alloc(name, shape, dt):
                t, _, end = sb(name, shape, dt, at=at[0])
                at[0] = end
                return t
            return alloc

        a = region(scratch)
        hn = a("hn", [P, 2, H], F32)
        hT = a("hT", [P, 2, 2, KH, P], F32R)
        aT = a("aT", [P, 2, 2, KH, P], F32R)
        suA = a("suA", [P, 2, H], F32)
        acA = a("acA", [P, 2, H], F32)
        yrow = a("yrow", [P, 2, 2 * H], F32)
        st6 = a("st6", [P, 2, 6], F32)
        st2 = a("st2", [P, 2, 6], F32)
        mv2 = a("mv2", [P, 2, 2], F32)
        ve2 = a("ve2", [P, 2], F32)
        rs2 = a("rs2", [P, 2], F32)
        mvA = a("mvA", [P, 2, 2], F32)
        veA = a("veA", [P, 2], F32)
        rsA = a("rsA", [P, 2], F32)
        tidi = a("tidi", [P, NTOK], I32)
        tidf = a("tidf", [P, NTOK], F32)
        ge = a("ge", [P, XE + 1, NTOK], F32)
        ohA = a("ohA", [P, XE, NTOK], BF16)
        preA = a("preA", [P, XE, NTOK + 1], BF16)
        sumA = a("sumA", [P, 2, XE, NTOK], BF16)
        limit = a("limit", [P, XE, NTOK], F32)
        cntA = a("cntA", [P, XE], F32)
        over_m = a("over_m", [P, XE, NTOK], F32)
        tilesA = a("tilesA", [P, XE], F32)
        startA = a("startA", [P, XE], F32)
        base_slot = a("base_slot", [P, XE], F32)
        posA = a("posA", [P, XE, NTOK], F32)
        posB = a("posB", [P, XE, NTOK], F32)
        slotA = a("slotA", [P, NTOK], F32)
        slotI = a("slotI", [P, NTOK], I32)
        slot_hi = a("slot_hi", [P, NTOK], I32)
        slot_lo = a("slot_lo", [P, NTOK], I32)
        place = a("place", [P, 2, NTOK], F32)
        row_no = a("row_no", [P, P], F32)
        part_no = a("part_no", [P, 1], F32)
        step_no = a("step_no", [P, NTOK], F32)
        at_row = a("at_row", [P, NTOK, P], BF16)
        at_tile = a("at_tile", [P, NTOK, 3, NT], BF16)
        list_f = a("list_f", [P, 2, NT], F32)
        tile_no = a("tile_no", [1, NT + 1], F32)
        tile_e = a("tile_e", [1, 3, NT + 1], F32)
        tile_w = a("tile_w", [1, NT + 1], I32)
        list_g = a("list_g", [P, NT], U32)
        list_s = a("list_s", [P, NT], U32)
        b = region(scratch)
        xrow = b("xrow", [P, 2, GROUP, 2 * H], F32)
        suB = b("suB", [P, 2, GN], F32)
        acB = b("acB", [P, 2, GN], F32)
        hTg, hTg_at, hTg_end = sb("hTg", [P, 2, 2, KH, GN], F32R, at=(scratch + 4 * 2 * (GROUP * 2 * H + 2 * GN)))
        hTf = sb("hTf", [P, 2, KH, H], F32, at=hTg_at)[0]
        b = region(hTg_end)
        lgT = sb("lgT", [E, 2, H], F32, at=hTg_end)[0]
        actB = b("actB", [P, 2, 6, GN], F32R)
        cm1 = b("cm1", [P, E], F32)
        b_ = region(xs_at + 4 * NTOK * RW)
        key8 = b_("key8", [P, NTOK, 8], F32)
        none8 = b_("none8", [P, NTOK, 8], F32)
        g13 = b_("g13", [P, NTOK, NG + 5], F32)
        g8 = b("g8", [P, NTOK, 8], F32)
        pen = b("pen", [P, NTOK, NG], F32)
        mx = b("mx", [P, NTOK], F32)
        sm = b("sm", [P, NTOK], F32)
        rc = b("rc", [P, NTOK], F32)
        EW = E + 2
        r_at = [raw_at]

        def ra(name, shape, dt, at=None):
            t, off, end = sb(name, shape, dt, at=r_at[0] if at is None else at)
            if at is None:
                r_at[0] = end
            return t, off
        z0, z0_at = ra("z0", [P, NTOK, EW], F32)
        z1, z1_at = ra("z1", [P, NTOK, EW], F32)
        z2, z2_at = ra("z2", [P, NTOK, EW], F32)
        z3, z3_at = ra("z3", [P, NTOK, EW], F32)
        z4, z4_at = ra("z4", [P, NTOK, EW], F32)
        z5, z5_at = ra("z5", [P, NTOK, EW], F32)
        z7, z7_at = ra("z7", [P, NTOK, EW], F32)
        mask, _ = ra("mask", [P, NTOK, E], BF16)
        pre, _ = ra("pre", [P, NTOK + 1, E], BF16)
        g13r, _ = ra("g13r", [P, NTOK, NG + 5], F32)
        assert r_at[0] <= raw_end
        c_ = region(xs_at)
        xg = c_("xg", [HC, 2, 2, RW], F32)
        xT = c_("xT", [P, 2, KH, 2, CAP], F32R)
        suC = c_("suC", [P, 3, CAP], F32)
        acC = c_("acC", [P, 3, CAP], F32)
        guC = c_("guC", [P, 3, 2, CAP], F32)
        c_ = region(hTg_at)
        actC = c_("actC", [P, 2, 2, 3, CAP], F32R)
        xlC = c_("xlC", [P, 3, 2, CAP], F32)
        ot = c_("ot", [HC, 2, 2, H], F32)
        wcol = c_("wcol", [HC, 2, 2], F32)
        tokc = c_("tokc", [HC, 2, 2], U32)
        lastS = c_("lastS", [E, H], F32)
        fb = sb("fb", [P, NTOK, H], F32, at=xs_at)[0]

        PS = ctx.enter_context(nc.psum_tensor("PS", [P, 8, H], F32))

        s_tid, s_gates, s_gatew = sem("tid_loaded"), sem("gates_loaded"), sem("gatew_loaded")
        s_wx = [sem(f"wx_loaded{e}") for e in range(XE)]
        s_sh = [sem(f"shared_loaded{i}") for i in range(2)]
        s_pad = sem("slots_padded")
        s_const, s_const2 = sem("const_first"), sem("const_ready")
        s_tg = sem("tanh_ready")
        s_apart = sem("wait_carrier")
        v_a = sem("dve_chain")
        s_ohA, s_cntA, s_slotA = sem("ohA_ready"), sem("ranksA_ready"), sem("slotA_ready")
        s_place, s_lmm, s_list = sem("places_ready"), sem("token_list_summed"), sem("token_list_ready")
        s_wxhi, s_wxlo = sem("wx_hi_ready"), sem("wx_lo_ready")
        s_x = [sem(f"x_gathered{i}") for i in range(2)]
        s_var, s_rstd, s_hn = sem("varA_ready"), sem("rstdA_ready"), sem("hnA_ready")
        s_t1, s_h1hi, s_h1lo = sem("hA_turned"), sem("hTA_hi_ready"), sem("hTA_lo_ready")
        s_mm1, s_su, s_ac = sem("uA_ready"), sem("siluA_ready"), sem("actA_ready")
        s_t2, s_h2hi, s_h2lo = sem("actA_turned"), sem("aTA_hi_ready"), sem("aTA_lo_ready")
        s_mm2, s_x1, s_x1s = sem("yA_ready"), sem("x1_ready"), [sem(f"x1_scattered{i}") for i in range(2)]
        s_var2, s_rstd2, s_h2 = sem("var2_ready"), sem("rstd2_ready"), sem("h2_ready")
        s_bn1, s_ag1, s_bn2, s_ag2 = sem("stats1"), sem("aggregate1"), sem("stats2"), sem("aggregate2")
        s_shhi, s_shlo = sem("shared_hi_ready"), sem("shared_lo_ready")
        s_hl = [sem(f"h_loaded{i}") for i in range(4)]
        s_row, s_tB, s_hTf = sem("row_ids_kept"), sem("hB_turned"), sem("hTf_ready")
        s_lg, s_lgT, s_lgb, s_lgc = sem("logitsT_done"), sem("logitsT_kept"), sem("logits_turned"), sem("logits_kept")
        v_r = sem("routing_chain")
        s_d, s_exp, s_pre = sem("logits_shifted"), sem("exp_ready"), sem("prefix_ready")
        s_cnt, s_cm1, s_pos = sem("counts_done"), sem("counts_kept"), sem("ranks_done")
        s_posu, s_slot, s_over = sem("ranks_used"), sem("slots_ready"), sem("over_weights_ready")
        s_ovT, s_ovTc = sem("over_weights_turned"), sem("over_wT_ready")
        s_disp = sem("rows_dispatched")
        s_xr = [sem(f"x1_row_loaded{i}") for i in range(2)]
        s_tg2, s_ghi, s_glo = sem("h_group_turned"), sem("hTg_hi"), sem("hTg_lo")
        s_gu, s_suB, s_acB = sem("gateup_done"), sem("siluB_ready"), sem("actB_product")
        s_bhi, s_blo, s_dn = sem("actB_hi"), sem("actB_lo"), sem("downB_done")
        s_res = sem("shared_added")
        s_st = [sem(f"out_stored{i}") for i in range(2)]
        s_raw = [sem(f"expert_weights_loaded{i}") for i in range(2)]
        s_xg = [sem(f"expert_rows_loaded{i}") for i in range(2)]
        s_whi, s_wlo = sem("w_hi"), sem("w_lo")
        s_tx, s_xhi, s_xlo = sem("x_turned"), sem("xT_hi"), sem("xT_lo")
        s_cxlc, s_cg = sem("x_lo_part_copied"), sem("expert_gateup_summed")
        s_cgu, s_csu, s_cac = sem("expert_gateup_done"), sem("expert_silu"), sem("expert_product")
        s_ahi, s_alo, s_cd = sem("expert_act_hi"), sem("expert_act_lo"), sem("expert_down_done")
        s_ot, s_wc = sem("expert_out_ready"), sem("slot_weights_ready")
        s_add = sem("rows_added")
        s_last = [sem(f"last_row_stored{i}") for i in range(2)]
        s_ll, s_f, s_fe, s_fa = sem("last_rows_loaded"), sem("over_done"), sem("over_copied"), sem("over_added")

        SH_CHUNKS = [(k * 2 * MS, 2 * MS, P) for k in range(KH)] + \
                    [(SGU + i * H, H, MST[i]) for i in range(6)]
        W_CHUNKS = [(k * 2 * M, 2 * M, P) for k in range(KH)] + \
                   [(WGU + i * H, H, MT[i]) for i in range(3)]
        x1_tiled = x1_rows.rearrange("(i p) h -> p i h", p=P)
        out_tiled = out.rearrange("(i p) h -> p i h", p=P)

        def w_part(par, part, lo, n, rows_=P):
            o = par * 2 * WE + (part * WGU + lo if lo < WGU else 2 * WGU + part * WD + lo - WGU)
            return parts[0:rows_, o:o + n]

        def sh_part(part, lo, n, rows_=P):
            o = part * (SGU + SD) + lo
            return parts[0:rows_, o:o + n]

        def wait_apart(engine, sem_, value):
            at_least(engine, sem_, value)
            if not isinstance(value, int):
                engine.sem_inc(s_apart, 1)

        def cbank(par, m):
            b0 = (6, 2)[(3 * par + m) % 2]
            return slice(b0, b0 + 2)

        block = ctx.enter_context(nc.Block())

        @block.sync
        def _(sp):
            sp.dma_start(tidi[:, :], tid).then_inc(s_tid, 16)
            for e in range(XE):
                sp.dma_start(raw[:, e * KH * XF:(e + 1) * KH * XF], ctxT[e]).then_inc(s_wx[e], 16)
            sp.dma_start(gates[:, 0:1], g_x.broadcast_to([P, 1])).then_inc(s_gates, 16)
            sp.dma_start(gates[:, 1:2], g_f.broadcast_to([P, 1])).then_inc(s_gates, 16)
            sp.dma_start(gate_w[:, :, :], gateT).then_inc(s_gatew, 16)
            sp.wait_ge(s_wxlo, XE)
            sp.wait_ge(s_x1, 1)
            sp.dma_start(raw[:, 0:SGU], sgu).then_inc(s_sh[0], 16)
            sp.dma_start(raw[:, SGU:SGU + 4 * H], sdA).then_inc(s_sh[1], 16)
            sp.dma_start(raw[0:96, SGU + 4 * H:SGU + SD], sdB).then_inc(s_sh[1], 16)
            sp.wait_ge(s_const2, 2)

            def empty_slots(i):
                n = E * CAP // P // PADS
                dst = slots.rearrange("(n p) w -> p n w", p=P)[:, i * n:(i + 1) * n, :]
                sp.dma_start(dst, pad_row[:, :].unsqueeze(1).broadcast_to([P, n, RW])).then_inc(s_pad, 16)
            for i in range(NT):
                sp.wait_ge(s_x1, i + 1)
                empty_slots(i)
            sp.wait_ge(s_x1s[0], 16 * ((NT + 1) // 2))
            sp.wait_ge(s_x1s[1], 16 * (NT // 2))
            for c in range(4):
                sp.dma_start(rows[:, 4 * c:4 * c + 4, 0:H], x1_tiled[:, 4 * c:4 * c + 4, H:2 * H]).then_inc(s_hl[c], 16)

            def b2_load(g, gp):
                if not (isinstance(g, int) and g < 2):
                    wait_apart(sp, s_st[gp], (g - gp) * 8)
                src = x1_rows[bass.ds(g * GN, GN), :].rearrange("(q p) h -> p q h", p=P)
                sp.dma_start(xrow[:, gp, :, :], src).then_inc(s_xr[gp], 16)

            def b2_store(g, gp):
                wait_apart(sp, s_res, GROUP * (g + 1))
                dst = out[bass.ds(g * GN, GN), :].rearrange("(q p) h -> p q h", p=P)
                sp.dma_start(dst, xrow[:, gp, :, 0:H]).then_inc(s_st[gp], 16)

            b2_load(0, 0)
            b2_load(1, 1)
            for i in range(NT, PADS):
                empty_slots(i)
            with sp.Fori(0, NGRP // 2 - 1) as it:
                for p in range(2):
                    b2_store(2 * it + p, p)
                    b2_load(2 * it + p + 2, p)

            def load_w(e, par):
                wait_apart(sp, s_wlo, 7 * (e - 1) if not isinstance(e, int) or e > 1 else 0)
                o = par * WE
                sp.dma_start(raw[:, o:o + WGU], wgu[bass.ds(e, 1)].rearrange("o p n -> (o p) n")).then_inc(s_raw[par], 16)
                sp.dma_start(raw[:, o + WGU:o + WGU + 2 * H], wdA[bass.ds(e, 1)].rearrange("o p n -> (o p) n")).then_inc(s_raw[par], 16)
                sp.dma_start(raw[0:MT[2], o + WGU + 2 * H:o + WE], wdB[bass.ds(e, 1)].rearrange("o p n -> (o p) n")).then_inc(s_raw[par], 16)

            def load_x(e, par):
                if not isinstance(e, int) or e > 1:
                    wait_apart(sp, s_tx, e - 1)
                    wait_apart(sp, s_wc, 2 * (e - 1))
                src = slots[bass.ds(e * CAP, CAP), :].rearrange("(c p) w -> p c w", p=HC)
                sp.dma_start(xg[:, par, :, :], src).then_inc(s_xg[par], 16)

            sp.wait_ge(s_over, 1)
            load_w(0, 0)
            load_w(1, 1)
            sp.wait_ge(s_disp, 16 * NTOK * TOPK)
            load_x(0, 0)
            load_x(1, 1)
            b2_store(NGRP - 2, 0)
            b2_store(NGRP - 1, 1)
            def store_last(e, par):
                wait_apart(sp, s_ot, 2 * (e + 1))
                sp.dma_start(last_rows[bass.ds(e, 1), :], ot[HC - 1:HC, par, 1, :]).then_inc(s_last[par], 16)
            for e in (2, 3):
                load_w(e, e % 2)
                load_x(e, e % 2)
            store_last(0, 0)
            with sp.Fori(0, E // 2 - 2) as it:
                for p in range(2):
                    load_w(2 * it + 4 + p, p)
                    load_x(2 * it + 4 + p, p)
                    store_last(2 * it + 1 + p, 1 - p)
            for e in (E - 3, E - 2, E - 1):
                store_last(e, e % 2)
            sp.wait_ge(s_last[0], 16 * E // 2)
            sp.wait_ge(s_last[1], 16 * E // 2)
            sp.dma_start(lastS[:, :], last_rows).then_inc(s_ll, 16)

        @block.gpsimd
        def _(pool):
            pool.memset(ident[:, :], 0.0).then_inc(s_const, 1)
            pool.iota(tok_id[:, :], [[P, NTOK]], base=0, channel_multiplier=1,
                      allow_small_or_imprecise_dtypes=True).then_inc(s_const2, 1)
            pool.memset(before[:, :], 1.0).then_inc(s_const, 1)
            pool.iota(row_no[:, :], [[1, P]], base=0, channel_multiplier=0, allow_small_or_imprecise_dtypes=True)
            pool.iota(part_no[:, :], [[0, 1]], base=0, channel_multiplier=1, allow_small_or_imprecise_dtypes=True)
            pool.iota(step_no[:, :], [[1, NTOK]], base=0, channel_multiplier=0, allow_small_or_imprecise_dtypes=True)
            pool.memset(ones[:, :], 1.0)
            pool.iota(limit[:, :, :], [[0, XE], [P, NTOK]], base=0, channel_multiplier=0,
                      allow_small_or_imprecise_dtypes=True)
            pool.iota(tile_no[:, :], [[1, NT + 1]], base=0, channel_multiplier=0,
                      allow_small_or_imprecise_dtypes=True)
            pool.wait_ge(s_const, 2)
            pool.affine_select(out=ident[:, :], in_=ident[:, :], compare_op=ALU.not_equal, fill=1.0,
                               base=0, pattern=[[-1, P]], channel_multiplier=1)
            pool.affine_select(out=before[:, :], in_=before[:, :], compare_op=ALU.is_gt, fill=0.0,
                               base=0, pattern=[[1, P]], channel_multiplier=-1)
            pool.memset(pad_row[:, 0:RW - 1], 0.0)
            pool.memset(pad_row[:, RW - 1:RW], float(SKIP))
            pool.memset(last_skip[:, :], 0.0).then_inc(s_const, 1)
            pool.memset(minus_half[:, :], -0.5)
            pool.wait_ge(s_const, 3)
            pool.affine_select(out=last_skip[:, 1:2], in_=last_skip[:, 1:2], compare_op=ALU.not_equal,
                               fill=float(SKIP), base=-(HC - 1), pattern=[[0, 1]], channel_multiplier=1)
            pool.iota(e_slot[:, :], [[CAP, E]], base=1, channel_multiplier=0,
                      allow_small_or_imprecise_dtypes=True).then_inc(s_const2, 1)
            pool.wait_ge(s_list, 1)

            def rstdA(j):
                pool.wait_ge(s_var, j + 1)
                if j >= 2:
                    pool.wait_ge(s_hn, j - 1)
                pool.tensor_tensor(rsA[:, j % 2:j % 2 + 1], veA[:, j % 2:j % 2 + 1],
                                   minus_half[:, 0:1], ALU.pow).then_inc(s_rstd, 1)

            def gather(j):
                if j >= 2:
                    pool.wait_ge(s_x[j % 2], 16 * (j // 2))
                pool.indirect_dma_start(xs[:, j, :], None, x,
                                        bass.IndirectOffsetOnAxis(ap=list_g[:, j:j + 1], axis=0),
                                        bounds_check=T - 1, oob_is_err=False).then_inc(s_x[j % 2], 16)

            def rstd2(j):
                pool.wait_ge(s_var2, j + 1)
                if j >= 2:
                    pool.wait_ge(s_h2, j - 1)
                pool.tensor_tensor(rs2[:, j % 2:j % 2 + 1], ve2[:, j % 2:j % 2 + 1],
                                   minus_half[:, 0:1], ALU.pow).then_inc(s_rstd2, 1)

            def scatter(j):
                pool.wait_ge(s_h2, j + 1)
                pool.indirect_dma_start(x1_rows, bass.IndirectOffsetOnAxis(ap=list_s[:, j:j + 1], axis=0),
                                        yrow[:, j % 2, :], None, bounds_check=T - 1,
                                        oob_is_err=False).then_inc(s_x1s[j % 2], 16)
            AHEAD = 5
            for j in range(AHEAD):
                gather(j)
            rstdA(0)
            rstdA(1)
            rstdA(2)
            for j in range(NT):
                if j + AHEAD < NT:
                    gather(j + AHEAD)
                if j + 3 < NT:
                    rstdA(j + 3)
                if j >= 1:
                    rstd2(j - 1)
                if j >= 2:
                    scatter(j - 2)
            scatter(NT - 2)
            rstd2(NT - 1)
            scatter(NT - 1)
            pool.wait_ge(s_x1s[0], 16 * ((NT + 1) // 2))
            pool.tensor_copy(rows[:, :, RW - 1:RW], tok_id[:, :].unsqueeze(2)).then_inc(s_row, 1)
            pool.wait_ge(s_row, 1)
            for c in range(4):
                pool.wait_ge(s_hl[c], 16)
            pool.wait_ge(s_slot, 1)
            pool.wait_ge(s_pad, 16 * PADS)
            for i in range(NTOK):
                for k in range(TOPK):
                    pool.indirect_dma_start(slots, bass.IndirectOffsetOnAxis(ap=slot_of[:, i, k:k + 1], axis=0),
                                            rows[:, i, :], None, bounds_check=E * CAP - 1,
                                            oob_is_err=False).then_inc(s_disp, 16)
            pool.wait_ge(s_st[0], 16 * NGRP // 2)
            pool.wait_ge(s_st[1], 16 * NGRP // 2)

            def add_rows(e, par):
                pool.wait_ge(s_wc, 2 * (e + 1))
                at_least(pool, s_add, 32 * e)
                for c in range(2):
                    wait_apart(pool, s_ot, 2 * e + c + 1)
                    pool.indirect_dma_start(out, bass.IndirectOffsetOnAxis(ap=tokc[:, par, c:c + 1], axis=0),
                                            ot[:, par, c, :], None, bounds_check=T - 1, oob_is_err=False,
                                            compute_op=ALU.add).then_inc(s_add, 16)
            add_rows(0, 0)
            add_rows(1, 1)
            with pool.Fori(0, E // 2 - 1) as it:
                for p in range(2):
                    add_rows(2 * it + 2 + p, p)
            for r in range(4):
                pool.wait_ge(s_fe, 4 * (r + 1))
                if r == 0:
                    pool.wait_ge(s_add, 32 * E)
                pool.dma_start(out_tiled[:, 4 * r:4 * r + 4, :], fb[:, 4 * r:4 * r + 4, :],
                               accum_op=ALU.add).then_inc(s_fa, 16)
            pool.wait_ge(s_fa, 64)

        @block.scalar
        def _(act):
            act.wait_ge(s_gates, 32)
            nc.scalar.activation(tg[:, :], gates[:, :], ACT.Tanh).then_inc(s_tg, 1)
            for e in range(XE):
                act.wait_ge(s_wx[e], 16)
                n = KH * XF
                nc.scalar.activation(parts[:, e * n:(e + 1) * n], raw[:, e * n:(e + 1) * n], ACT.Copy).then_inc(s_wxhi, 1)

            def hi1(j, p):
                act.wait_ge(s_t1, j + 1)
                at_least(act, s_mm1, j - 1 if not isinstance(j, int) or j > 1 else 0)
                nc.scalar.activation(hT[:, p, 0].rearrange("p k n -> p (k n)"), PS[:, 0, :], ACT.Copy).then_inc(s_h1hi, 1)

            def stepA(j, p, more):
                act.wait_ge(s_mm1, j + 1)
                if not isinstance(j, int) or j > 1:
                    act.wait_ge(s_ac, j - 1)
                nc.scalar.activation(suA[:, p, :], PS[:, 2 + p, :], ACT.Silu).then_inc(s_su, 1)
                if more:
                    hi1(j + 1, 1 - p)
                act.wait_ge(s_t2, j + 1)
                if not isinstance(j, int) or j > 1:
                    act.wait_ge(s_mm2, j - 1)
                nc.scalar.activation(aT[:, p, 0].rearrange("p k n -> p (k n)"), PS[:, 1, :], ACT.Copy).then_inc(s_h2hi, 1)
            hi1(0, 0)
            stepA(0, 0, True)
            stepA(1, 1, True)
            stepA(2, 0, True)
            with act.Fori(0, (NT - 5) // 2) as it:
                stepA(2 * it + 3, 1, True)
                stepA(2 * it + 4, 0, True)
            stepA(NT - 2, 1, True)
            stepA(NT - 1, 0, False)
            act.wait_ge(s_mm2, NT)
            act.wait_ge(s_sh[0], 16)
            for n_, (lo, n, r) in enumerate(SH_CHUNKS):
                if n_ == KH:
                    act.wait_ge(s_sh[1], 32)
                nc.scalar.activation(sh_part(0, lo, n, r), raw[0:r, lo:lo + n], ACT.Copy).then_inc(s_shhi, 1)

            act.wait_ge(s_x1s[1], 16 * (NT // 2))
            for c in range(4):
                for k in range(KH):
                    act.wait_ge(s_tB, KH * c + k + 1)
                    if c >= 2:
                        act.wait_ge(s_lg, c - 1)
                    nc.scalar.activation(hTf[:, c % 2, k, :], PS[:, k, :], ACT.Copy).then_inc(s_hTf, 1)

            def hiB(g, gp):
                for q in range(GROUP):
                    act.wait_ge(s_tg2, GROUP * g + q + 1)
                    if not isinstance(g, int) or g > 1:
                        act.wait_ge(s_gu, 6 * (g - 1))
                    elif g == 0:
                        act.wait_ge(s_lg, 4)
                    nc.scalar.activation(hTg[:, gp, 0, :, q * P:(q + 1) * P],
                                         PS[:, q, :].rearrange("p (k n) -> p k n", k=KH), ACT.Copy).then_inc(s_ghi, 1)

            def stepB(g, gp, more):
                for m in range(6):
                    n = 6 * g + m
                    r = MST[m]
                    act.wait_ge(s_gu, n + 1)
                    if not isinstance(g, int) or n > 1:
                        act.wait_ge(s_acB, n - 1)
                    nc.scalar.activation(suB[0:r, m % 2, :], PS[0:r, 2 + m % 2, 0:GN], ACT.Silu).then_inc(s_suB, 1)
                    act.wait_ge(s_acB, n + 1)
                    if not isinstance(g, int) or g > 0:
                        act.wait_ge(s_dn, GROUP * g)
                    nc.scalar.activation(actB[0:r, 0, m, :], acB[0:r, m % 2, :], ACT.Copy).then_inc(s_bhi, 1)
                if more:
                    hiB(g + 1, 1 - gp)

            def over_copy(c):
                act.wait_ge(s_ovT, c + 1)
                nc.scalar.activation(over_wT[:, 4 * c:4 * c + 4, :].rearrange("e i t -> e (i t)"),
                                     PS[0:E, 6 + c % 2, :], ACT.Copy).then_inc(s_ovTc, 1)
            hiB(0, 0)
            act.wait_ge(s_d, 1)
            nc.scalar.activation(z1[:, :, 0:E], z0[:, :, 0:E], ACT.Exp).then_inc(s_exp, 1)
            stepB(0, 0, True)
            stepB(1, 1, True)
            for c in range(4):
                over_copy(c)
            with act.Fori(0, NGRP // 2 - 2) as it:
                stepB(2 * it + 2, 0, True)
                stepB(2 * it + 3, 1, True)
            stepB(NGRP - 2, 0, True)
            stepB(NGRP - 1, 1, False)

            def hi_w(e, par, k):
                lo, n, r = W_CHUNKS[k]
                nc.scalar.activation(w_part(par, 0, lo, n, r), raw[0:r, par * WE + lo:par * WE + lo + n], ACT.Copy).then_inc(s_whi, 1)

            def wait_w(e, par):
                act.wait_ge(s_raw[par], (e - par) * 24 + 48)
                if not isinstance(e, int) or e > 1:
                    act.wait_ge(s_cd, 2 * (e - 1))

            def hi_x(e, par, b_):
                act.wait_ge(s_tx, e + 1)
                if not isinstance(e, int) or e > 1:
                    act.wait_ge(s_cgu, 3 * (e - 1))
                nc.scalar.activation(xT[:, par, 2 * b_:2 * b_ + 2, 0, :],
                                     PS[:, b_, 0:2 * CAP].rearrange("p (k n) -> p k n", k=2), ACT.Copy).then_inc(s_xhi, 1)

            def stepC(e, par, more):
                if more:
                    wait_w(e + 1, 1 - par)
                    hi_w(e + 1, 1 - par, 0)
                def keep_x_lo(m):
                    act.wait_ge(s_cgu, 3 * e + m + 1)
                    at_least(act, s_cg, 3 * e + m - 2 if not isinstance(e, int) or e > 0 else 0)
                    nc.scalar.activation(xlC[0:MT[m], m, :, :], PS[0:MT[m], cbank(par, m), CAP:2 * CAP],
                                         ACT.Copy).then_inc(s_cxlc, 1)

                def silu(m):
                    act.wait_ge(s_cg, 3 * e + m + 1)
                    at_least(act, s_cac, 3 * e + m - 2 if not isinstance(e, int) or e > 0 else 0)
                    nc.scalar.activation(suC[0:MT[m], m, :], guC[0:MT[m], m, 0, :], ACT.Silu).then_inc(s_csu, 1)

                def hi_act(m):
                    act.wait_ge(s_cac, 3 * e + m + 1)
                    if not isinstance(e, int) or e > 1:
                        act.wait_ge(s_cd, 2 * (e - 1))
                    nc.scalar.activation(actC[0:MT[m], par, 0, m, :], acC[0:MT[m], m, :], ACT.Copy).then_inc(s_ahi, 1)
                keep_x_lo(0)
                if more:
                    hi_w(e + 1, 1 - par, 1)
                silu(0)
                hi_act(0)
                keep_x_lo(1)
                if more:
                    hi_w(e + 1, 1 - par, 2)
                silu(1)
                keep_x_lo(2)
                hi_act(1)
                if more:
                    hi_x(e + 1, 1 - par, 0)
                silu(2)
                if more:
                    hi_x(e + 1, 1 - par, 1)
                hi_act(2)
                if more:
                    for k in range(3, 7):
                        hi_w(e + 1, 1 - par, k)
                act.wait_ge(s_wc, 2 * (e + 1))
                if not isinstance(e, int) or e > 1:
                    act.wait_ge(s_add, 32 * (e - 1))
                    act.wait_ge(s_last[par], (e - par) * 8)
                for c in range(2):
                    act.wait_ge(s_cd, 2 * e + c + 1)
                    nc.scalar.activation(ot[:, par, c, :], PS[0:HC, 4 + c, :], ACT.Copy,
                                         scale=wcol[:, par, c:c + 1]).then_inc(s_ot, 1)
            act.wait_ge(s_gu, 6 * NGRP)
            wait_w(0, 0)
            for k in range(KH):
                hi_w(0, 0, k)
            hi_x(0, 0, 0)
            hi_x(0, 0, 1)
            act.wait_ge(s_dn, NTOK)
            for k in range(KH, len(W_CHUNKS)):
                hi_w(0, 0, k)
            stepC(0, 0, True)
            stepC(1, 1, True)
            with act.Fori(0, E // 2 - 2) as it:
                stepC(2 * it + 2, 0, True)
                stepC(2 * it + 3, 1, True)
            stepC(E - 2, 0, True)
            stepC(E - 1, 1, False)
            for i in range(NTOK):
                act.wait_ge(s_f, i + 1)
                nc.scalar.activation(fb[:, i, :], PS[:, i % 2, :], ACT.Copy).then_inc(s_fe, 1)

        @block.vector
        def _(dve):
            v = nc.vector
            count = [0]

            def link(ins):
                count[0] += 1
                ins.then_inc(v_a, 1)
                dve.wait_ge(v_a, count[0])
            dve.wait_ge(s_tid, 16)
            link(v.tensor_copy(tidf[:, :], tidi[:, :]))
            v.memset(ge[:, 0, :], 1.0)
            v.memset(ge[:, XE, :], 0.0)
            for e in range(1, XE - 1):
                v.tensor_scalar(ge[:, e, :], tidf[:, :], float(e * PER_EXPERT), None, ALU.is_ge)
            link(v.tensor_scalar(ge[:, XE - 1, :], tidf[:, :], float((XE - 1) * PER_EXPERT), None, ALU.is_ge))
            v.memset(preA[:, :, 0:1], 0.0)
            link(v.tensor_tensor(ohA[:, :, :], ge[:, 0:XE, :], ge[:, 1:XE + 1, :], ALU.subtract))
            src = ohA[:, :, :]
            for n_ in range(4):
                d = 1 << n_
                dst = sumA[:, n_ % 2] if n_ < 3 else preA[:, :, 1:NTOK + 1]
                v.tensor_copy(dst[:, :, 0:d], src[:, :, 0:d])
                link(v.tensor_tensor(dst[:, :, d:NTOK], src[:, :, d:NTOK], src[:, :, 0:NTOK - d], ALU.add))
                src = dst
            v.memset(tilesA[:, :], 0.0).then_inc(s_ohA, 1)
            dve.wait_ge(s_cntA, 1)
            dve.wait_ge(s_const2, 2)
            dve.wait_ge(s_ohA, 1)
            link(v.tensor_copy(cntA[:, :], PS[:, 6, 64:64 + XE]))
            link(v.tensor_tensor(over_m[:, :, :], cntA[:, :].unsqueeze(2).broadcast_to([P, XE, NTOK]),
                                 limit[:, :, :], ALU.is_gt))
            v.memset(startA[:, 0:1], 0.0)
            link(v.tensor_reduce(tilesA[:, :], over_m[:, :, :], X, ALU.add))
            for e in range(1, XE):
                link(v.tensor_tensor(startA[:, e:e + 1], startA[:, e - 1:e], tilesA[:, e - 1:e], ALU.add))
            link(v.tensor_scalar(base_slot[:, :], startA[:, :], float(P), None, ALU.mult))
            link(v.tensor_tensor(posA[:, :, :], PS[:, 6, 0:64].rearrange("p (e i) -> p e i", e=XE),
                                 base_slot[:, :].unsqueeze(2).broadcast_to([P, XE, NTOK]), ALU.add))
            link(v.tensor_tensor(posB[:, :, :], posA[:, :, :], ohA[:, :, :], ALU.mult))
            link(v.tensor_reduce(slotA[:, :], posB[:, :, :].rearrange("p e i -> p i e"), X, ALU.add))
            link(v.tensor_copy(slotI[:, :], slotA[:, :]))
            v.tensor_scalar(slot_hi[:, :], slotI[:, :], 7, None, ALU.logical_shift_right)
            link(v.tensor_scalar(slot_lo[:, :], slotI[:, :], P - 1, None, ALU.bitwise_and))
            v.tensor_copy(place[:, 0, :], slot_hi[:, :])
            link(v.tensor_copy(place[:, 1, :], slot_lo[:, :]))
            link(v.tensor_tensor(at_tile[:, :, 2, :], row_no[:, 0:NT].unsqueeze(1).broadcast_to([P, NTOK, NT]),
                                 place[:, 0, :].unsqueeze(2).broadcast_to([P, NTOK, NT]), ALU.is_equal))
            v.tensor_scalar(at_tile[:, :, 0, :], at_tile[:, :, 2, :], part_no[:, 0:1], None, ALU.mult)
            v.tensor_tensor(at_tile[:, :, 1, :], at_tile[:, :, 2, :],
                            step_no[:, :].unsqueeze(2).broadcast_to([P, NTOK, NT]), ALU.mult)
            v.tensor_tensor(at_row[:, :, :], row_no[:, :].unsqueeze(1).broadcast_to([P, NTOK, P]),
                            place[:, 1, :].unsqueeze(2).broadcast_to([P, NTOK, P]), ALU.is_equal).then_inc(s_place, 1)
            link(v.tensor_scalar(tile_e[:, 0, :], tile_no[:, :], startA[0:1, 1:2], None, ALU.is_ge))
            for e in (2, 3):
                link(v.scalar_tensor_tensor(tile_e[:, e - 1, :], tile_no[:, :], startA[0:1, e:e + 1],
                                            tile_e[:, e - 2, :], ALU.is_ge, ALU.add))
            v.tensor_scalar(tile_w[:, :], tile_e[:, 2, :], float(KH * XF), None, ALU.mult).then_inc(s_slotA, 1)
            dve.wait_ge(s_lmm, 1)
            link(v.tensor_scalar(list_f[:, 0, :], PS[:, 7, NT:2 * NT], float(P), float(SKIP), ALU.mult, ALU.add))
            link(v.tensor_tensor(list_f[:, 1, :], PS[:, 7, 0:NT], list_f[:, 0, :], ALU.add))
            link(v.scalar_tensor_tensor(list_f[:, 0, :], PS[:, 7, 2 * NT:3 * NT], -float(SKIP), list_f[:, 1, :],
                                        ALU.mult, ALU.add))
            v.tensor_scalar(list_g[:, :], list_f[:, 0, :], float(T - 1), None, ALU.min)
            v.tensor_copy(list_s[:, :], list_f[:, 0, :]).then_inc(s_list, 1)
            for e in range(XE):
                dve.wait_ge(s_wxhi, e + 1)
                n = KH * XF
                v.tensor_tensor(parts[:, half + e * n:half + (e + 1) * n], raw[:, e * n:(e + 1) * n],
                                parts[:, e * n:(e + 1) * n].bitcast(F32), ALU.subtract).then_inc(s_wxlo, 1)
            dve.wait_ge(s_tg, 1)

            def bn1(j, p):
                dve.wait_ge(s_x[p], (j - p) * 8 + 16)
                v.bn_stats(st6[:, p, :], xs[:, bass.ds(j, 1), :].rearrange("p o h -> p (o h)")).then_inc(s_bn1, 1)

            def ve1(j, p):
                dve.wait_ge(s_ag1, j + 1)
                if not isinstance(j, int) or j > 1:
                    dve.wait_ge(s_rstd, j - 1)
                v.tensor_scalar(veA[:, p:p + 1], mvA[:, p, 1:2], EPS, None, ALU.add).then_inc(s_var, 1)

            def bn2(j, p):
                dve.wait_ge(s_x1, j + 1)
                v.bn_stats(st2[:, p, :], yrow[:, p, 0:H]).then_inc(s_bn2, 1)

            def var2(j, p):
                dve.wait_ge(s_ag2, j + 1)
                if not isinstance(j, int) or j > 1:
                    dve.wait_ge(s_rstd2, j - 1)
                v.tensor_scalar(ve2[:, p:p + 1], mv2[:, p, 1:2], EPS, None, ALU.add).then_inc(s_var2, 1)

            def norm2(j, p):
                dve.wait_ge(s_rstd2, j + 1)
                v.tensor_scalar(yrow[:, p, H:2 * H], yrow[:, p, 0:H], mv2[:, p, 0:1], rs2[:, p:p + 1],
                                ALU.subtract, ALU.mult).then_inc(s_h2, 1)

            def norm(j, p):
                dve.wait_ge(s_rstd, j + 1)
                if not isinstance(j, int) or j > 1:
                    dve.wait_ge(s_t1, j - 1)
                v.tensor_scalar(hn[:, p, :], xs[:, bass.ds(j, 1), :].rearrange("p o h -> p (o h)"),
                                mvA[:, p, 0:1], rsA[:, p:p + 1], ALU.subtract, ALU.mult).then_inc(s_hn, 1)

            def lo1(j, p):
                dve.wait_ge(s_h1hi, j + 1)
                v.tensor_tensor(hT[:, p, 1].rearrange("p k n -> p (k n)"), PS[:, 0, :],
                                hT[:, p, 0].rearrange("p k n -> p (k n)").bitcast(F32), ALU.subtract).then_inc(s_h1lo, 1)

            def product(j, p):
                dve.wait_ge(s_su, j + 1)
                if not isinstance(j, int) or j > 1:
                    dve.wait_ge(s_t2, j - 1)
                v.tensor_tensor(acA[:, p, :], PS[:, 2 + p, :], suA[:, p, :], ALU.mult).then_inc(s_ac, 1)

            def lo2(j, p):
                dve.wait_ge(s_h2hi, j + 1)
                v.tensor_tensor(aT[:, p, 1].rearrange("p k n -> p (k n)"), PS[:, 1, :],
                                aT[:, p, 0].rearrange("p k n -> p (k n)").bitcast(F32), ALU.subtract).then_inc(s_h2lo, 1)

            def resid(j, p):
                dve.wait_ge(s_mm2, j + 1)
                if not isinstance(j, int) or j > 1:
                    dve.wait_ge(s_x1s[p], (j - p) * 8)
                row = xs[:, bass.ds(j, 1), :].rearrange("p o h -> p (o h)")
                v.scalar_tensor_tensor(yrow[:, p, 0:H], PS[:, 4 + p, :], tg[:, 0:1], row, ALU.mult, ALU.add).then_inc(s_x1, 1)

            for j in range(3):
                bn1(j, j % 2)
                dve.wait_ge(s_bn1, j + 1)
                v.bn_aggr(mvA[:, j % 2, :], st6[:, j % 2, :]).then_inc(s_ag1, 1)
                ve1(j, j % 2)
                if j < 2:
                    norm(j, j)
                if j == 0:
                    lo1(0, 0)

            def stepA(j, p, more, more2, more3):
                q = 1 - p
                back = not isinstance(j, int) or j > 0
                back2 = not isinstance(j, int) or j > 1
                product(j, p)
                if more:
                    lo1(j + 1, q)
                if more2:
                    norm(j + 2, p)
                if back2:
                    norm2(j - 2, p)
                if more3:
                    bn1(j + 3, q)
                if back:
                    resid(j - 1, q)
                    if more3:
                        dve.wait_ge(s_bn1, j + 4)
                    bn2(j - 1, q)
                elif more3:
                    dve.wait_ge(s_bn1, j + 4)
                if more3:
                    v.bn_aggr(mvA[:, q, :], st6[:, q, :]).then_inc(s_ag1, 1)
                    if back:
                        dve.wait_ge(s_bn2, j)
                    ve1(j + 3, q)
                elif back:
                    dve.wait_ge(s_bn2, j)
                if back:
                    v.bn_aggr(mv2[:, q, :], st2[:, q, :]).then_inc(s_ag2, 1)
                lo2(j, p)
                if back:
                    var2(j - 1, q)
            for j in range(4):
                stepA(j, j % 2, True, True, True)
            with dve.Fori(0, (NT - 7) // 2) as it:
                for p in range(2):
                    stepA(2 * it + 4 + p, p, True, True, True)
            stepA(NT - 3, 0, True, True, False)
            stepA(NT - 2, 1, True, False, False)
            stepA(NT - 1, 0, False, False, False)
            norm2(NT - 2, 1)
            resid(NT - 1, 0)
            bn2(NT - 1, 0)
            dve.wait_ge(s_bn2, NT)
            v.bn_aggr(mv2[:, 0, :], st2[:, 0, :]).then_inc(s_ag2, 1)
            var2(NT - 1, 0)
            norm2(NT - 1, 0)

            for n_, (lo, n, r) in enumerate(SH_CHUNKS):
                dve.wait_ge(s_shhi, n_ + 1)
                v.tensor_tensor(sh_part(1, lo, n, r), raw[0:r, lo:lo + n],
                                sh_part(0, lo, n, r).bitcast(F32), ALU.subtract).then_inc(s_shlo, 1)
            for c in range(5):
                if c < 4:
                    dve.wait_ge(s_lg, c + 1)
                    if c >= 2:
                        dve.wait_ge(s_lgb, c - 1)
                    v.tensor_copy(lgT[:, c % 2, :], PS[0:E, 4 + c % 2, :]).then_inc(s_lgT, 1)
                if c > 0:
                    dve.wait_ge(s_lgb, c)
                    v.tensor_copy(logits[:, 4 * c - 4:4 * c, :].rearrange("p i e -> p (i e)"),
                                  PS[:, 6 + (c - 1) % 2, 0:4 * E]).then_inc(s_lgc, 1)

            rcount = [0]

            def rlink(ins):
                rcount[0] += 1
                ins.then_inc(v_r, 1)
                dve.wait_ge(v_r, rcount[0])

            def by_tile(t, n=E):
                return t[:, :].unsqueeze(2).broadcast_to([P, NTOK, n])

            def by_expert(t):
                return t[:, :].unsqueeze(1).broadcast_to([P, NTOK, E])

            def each(op, *a_):
                for i in range(NTOK):
                    ins = op(i)
                rlink(ins)

            def r0():
                dve.wait_ge(s_lgc, 4)
                rlink(v.tensor_reduce(mx[:, :], logits[:, :, :], X, ALU.max))
                v.tensor_tensor(z0[:, :, 0:E], logits[:, :, :], by_tile(mx), ALU.subtract).then_inc(s_d, 1)
                dve.wait_ge(s_d, 1)
                v.memset(z4[:, :, E:EW], BIG)
                v.memset(g13[:, :, NG:NG + 5], BIG)
                rlink(v.tensor_scalar(z3[:, :, 0:E], z0[:, :, 0:E], FLOOR, None, ALU.max))
                rlink(v.tensor_reduce(g13[:, :, 0:NG], z3[:, :, 0:E].rearrange("p i (g s) -> p i g s", g=NG), X, ALU.max))

            def r1():
                each(lambda i: v.max(g8[:, i, :], g13[:, i, :]))
                each(lambda i: v.match_replace(g13r[:, i, :], g8[:, i, :], g13[:, i, :], -BIG))
                rlink(v.tensor_scalar(pen[:, :, :], g13r[:, :, 0:NG], -BIG, BIG, ALU.is_equal, ALU.mult))
                rlink(v.tensor_scalar(g8[:, :, :], pen[:, :, :], FLOOR, None, ALU.add))
                rlink(v.tensor_tensor(z4[:, :, 0:E].rearrange("p i (g s) -> p i g s", g=NG),
                                      z3[:, :, 0:E].rearrange("p i (g s) -> p i g s", g=NG),
                                      g8[:, :, :].unsqueeze(3).broadcast_to([P, NTOK, NG, GS]), ALU.min))

            def r2():
                each(lambda i: v.max(key8[:, i, :], z4[:, i, :]))
                each(lambda i: v.match_replace(z5[:, i, :], key8[:, i, :], z4[:, i, :], -BIG))
                v.memset(pre[:, 0, :], 0.0)
                rlink(v.tensor_scalar(mask[:, :, :], z5[:, :, 0:E], -BIG, None, ALU.is_equal))

            def r3():
                for i in range(NTOK):
                    rlink(v.tensor_tensor(pre[:, i + 1, :], pre[:, i, :], mask[:, i, :], ALU.add))
                v.memset(sm[:, :], 0.0).then_inc(s_pre, 1)

            def r4():
                dve.wait_ge(s_exp, 1)
                dve.wait_ge(s_pre, 1)
                rlink(v.tensor_reduce(sm[:, :], z1[:, :, 0:E], X, ALU.add))
                rlink(v.reciprocal(rc[:, :], sm[:, :]))
                rlink(v.tensor_tensor(z2[:, :, 0:E], z1[:, :, 0:E], by_tile(rc), ALU.mult))
                dve.wait_ge(s_cnt, 1)
                v.tensor_scalar(cm1[:, :], PS[:, 6, 0:E], -1.0, None, ALU.add).then_inc(s_cm1, 1)

            def r5():
                dve.wait_ge(s_pos, 1)
                dve.wait_ge(s_cm1, 1)
                pos = PS[:, 6:8, :].rearrange("p b (i e) -> p (b i) e", e=E)
                v.scalar_tensor_tensor(z0[:, :, 0:E], pos, float(CAP - 1), mask[:, :, :], ALU.is_lt, ALU.mult)
                rlink(v.tensor_tensor(z1[:, :, 0:E], pos, by_expert(cm1), ALU.is_equal))
                rlink(v.scalar_tensor_tensor(z3[:, :, 0:E], pos, float(CAP - 1), z1[:, :, 0:E], ALU.is_ge, ALU.mult))
                rlink(v.tensor_tensor(z1[:, :, 0:E], z3[:, :, 0:E], mask[:, :, :], ALU.mult))
                rlink(v.scalar_tensor_tensor(z5[:, :, 0:E], pos, float(CAP - 1), by_expert(e_slot), ALU.min, ALU.add))
                rlink(v.tensor_tensor(z4[:, :, 0:E], z0[:, :, 0:E], z1[:, :, 0:E], ALU.add))
                rlink(v.tensor_tensor(z7[:, :, 0:E], z4[:, :, 0:E], z5[:, :, 0:E], ALU.mult))
                each(lambda i: v.max(key8[:, i, :], z7[:, i, 0:E]))
                rlink(v.tensor_scalar(none8[:, :, :], key8[:, :, :], 0.0, float(NOSLOT), ALU.is_le, ALU.mult))
                v.scalar_tensor_tensor(slot_of[:, :, :], key8[:, :, :], -1.0, none8[:, :, :], ALU.add, ALU.add)
                rlink(v.tensor_tensor(z3[:, :, 0:E], z0[:, :, 0:E], z2[:, :, 0:E], ALU.mult))
                v.tensor_tensor(rows[:, :, H:H + E], z3[:, :, 0:E], z1[:, :, 0:E], ALU.add).then_inc(s_slot, 1)

            def r6():
                rlink(v.tensor_tensor(z4[:, :, 0:E], mask[:, :, :], z0[:, :, 0:E], ALU.subtract))
                v.tensor_tensor(over_w[:, :, :], z4[:, :, 0:E], z2[:, :, 0:E], ALU.mult).then_inc(s_over, 1)
            pieces = [r0, r1, r2, r3, r4, r5, r6]

            def loB(g, gp):
                for q in range(GROUP):
                    dve.wait_ge(s_ghi, GROUP * g + q + 1)
                    v.tensor_tensor(hTg[:, gp, 1, :, q * P:(q + 1) * P], PS[:, q, :].rearrange("p (k n) -> p k n", k=KH),
                                    hTg[:, gp, 0, :, q * P:(q + 1) * P].bitcast(F32), ALU.subtract).then_inc(s_glo, 1)

            def residB(g, gp):
                for q in range(GROUP):
                    dve.wait_ge(s_dn, GROUP * g + q + 1)
                    v.scalar_tensor_tensor(xrow[:, gp, q, 0:H], PS[:, 4 + q, :], tg[:, 1:2], xrow[:, gp, q, 0:H],
                                           ALU.mult, ALU.add).then_inc(s_res, 1)

            def stepB(g, gp, more, routing=()):
                for m in range(6):
                    n, r = 6 * g + m, MST[m]
                    dve.wait_ge(s_suB, n + 1)
                    if not isinstance(g, int) or n > 1:
                        dve.wait_ge(s_bhi, n - 1)
                    v.tensor_tensor(acB[0:r, m % 2, :], PS[0:r, 2 + m % 2, GN:2 * GN], suB[0:r, m % 2, :], ALU.mult).then_inc(s_acB, 1)
                    dve.wait_ge(s_bhi, n + 1)
                    v.tensor_tensor(actB[0:r, 1, m, :], acB[0:r, m % 2, :], actB[0:r, 0, m, :].bitcast(F32),
                                    ALU.subtract).then_inc(s_blo, 1)
                    if m < len(routing):
                        routing[m]()
                if more:
                    loB(g + 1, 1 - gp)
                    residB(g, gp)
            loB(0, 0)
            r0()
            stepB(0, 0, True, pieces[1:5])
            stepB(1, 1, True, pieces[5:])
            with dve.Fori(0, NGRP // 2 - 2) as it:
                stepB(2 * it + 2, 0, True)
                stepB(2 * it + 3, 1, True)
            stepB(NGRP - 2, 0, True)
            stepB(NGRP - 1, 1, False)

            def lo_w(e, par, k):
                lo, n, r = W_CHUNKS[k]
                dve.wait_ge(s_whi, 7 * e + k + 1)
                v.tensor_tensor(w_part(par, 1, lo, n, r), raw[0:r, par * WE + lo:par * WE + lo + n],
                                w_part(par, 0, lo, n, r).bitcast(F32), ALU.subtract).then_inc(s_wlo, 1)

            def lo_x(e, par, b_):
                dve.wait_ge(s_xhi, 2 * e + b_ + 1)
                v.tensor_tensor(xT[:, par, 2 * b_:2 * b_ + 2, 1, :],
                                PS[:, b_, 0:2 * CAP].rearrange("p (k n) -> p k n", k=2),
                                xT[:, par, 2 * b_:2 * b_ + 2, 0, :].bitcast(F32),
                                ALU.subtract).then_inc(s_xlo, 1)

            def weights_of(e, par):
                dve.wait_ge(s_xg[par], (e - par) * 8 + 16)
                if not isinstance(e, int) or e > 1:
                    dve.wait_ge(s_add, 32 * (e - 1))
                    dve.wait_ge(s_ot, 2 * (e - 1))
                v.tensor_scalar(wcol[:, par, :], xg[:, par, :, bass.ds(e + H, 1)].rearrange("p c o -> p (c o)"),
                                tg[0:HC, 1:2], None, ALU.mult).then_inc(s_wc, 1)
                v.tensor_tensor(tokc[:, par, :], xg[:, par, :, RW - 1], last_skip[:, :], ALU.add).then_inc(s_wc, 1)

            def stepC(e, par, more):
                weights_of(e, par)
                if more:
                    lo_w(e + 1, 1 - par, 0)
                def gu_sum(m):
                    dve.wait_ge(s_cxlc, 3 * e + m + 1)
                    if not isinstance(e, int) or e > 0:
                        dve.wait_ge(s_cac, 3 * e + m - 2)
                    v.tensor_tensor(guC[0:MT[m], m, :, :], PS[0:MT[m], cbank(par, m), 0:CAP], xlC[0:MT[m], m, :, :],
                                    ALU.add).then_inc(s_cg, 1)

                def gated(m):
                    dve.wait_ge(s_csu, 3 * e + m + 1)
                    if not isinstance(e, int) or e > 0:
                        dve.wait_ge(s_ahi, 3 * e + m - 2)
                    v.tensor_tensor(acC[0:MT[m], m, :], guC[0:MT[m], m, 1, :], suC[0:MT[m], m, :], ALU.mult).then_inc(s_cac, 1)

                def lo_act(m):
                    dve.wait_ge(s_ahi, 3 * e + m + 1)
                    v.tensor_tensor(actC[0:MT[m], par, 1, m, :], acC[0:MT[m], m, :],
                                    actC[0:MT[m], par, 0, m, :].bitcast(F32), ALU.subtract).then_inc(s_alo, 1)
                gu_sum(0)
                gated(0)
                if more:
                    lo_w(e + 1, 1 - par, 1)
                lo_act(0)
                gu_sum(1)
                gated(1)
                gu_sum(2)
                lo_act(1)
                if more:
                    lo_x(e + 1, 1 - par, 0)
                gated(2)
                if more:
                    lo_x(e + 1, 1 - par, 1)
                lo_act(2)
                if more:
                    for k in range(2, 7):
                        lo_w(e + 1, 1 - par, k)
            for k in range(KH):
                lo_w(0, 0, k)
            lo_x(0, 0, 0)
            lo_x(0, 0, 1)
            residB(NGRP - 1, 1)
            for k in range(KH, 7):
                lo_w(0, 0, k)
            stepC(0, 0, True)
            stepC(1, 1, True)
            with dve.Fori(0, E // 2 - 2) as it:
                stepC(2 * it + 2, 0, True)
                stepC(2 * it + 3, 1, True)
            stepC(E - 2, 0, True)
            stepC(E - 1, 1, False)

        @block.tensor
        def _(pe):
            mm = nc.tensor.matmul

            def split_product(dst, terms):
                for n, (ah, al, bh, bl) in enumerate(terms):
                    mm(dst, ah, bh, start=(n == 0), stop=False)
                    mm(dst, ah, bl, start=False, stop=False)
                    last = mm(dst, al, bh, start=False, stop=(n == len(terms) - 1))
                return last

            pe.wait_ge(s_ohA, 1)
            pe.wait_ge(s_const2, 2)
            mm(PS[:, 6, 0:64], before[:, :], ohA[:, :, :].rearrange("p e i -> p (e i)"), start=True, stop=False)
            mm(PS[:, 6, 0:64], ones[:, :], preA[:, :, 0:NTOK], start=False, stop=True)
            mm(PS[:, 6, 64:64 + XE], ones[:, :], preA[:, :, NTOK], start=True, stop=True).then_inc(s_cntA, 1)
            pe.wait_ge(s_place, 1)
            for i in range(NTOK):
                last = mm(PS[:, 7, 0:3 * NT], at_row[:, i, :], at_tile[:, i, :, :].rearrange("p c j -> p (c j)"),
                          start=(i == 0), stop=(i == NTOK - 1))
            last.then_inc(s_lmm, 1)

            def turn1(j, p):
                pe.wait_ge(s_hn, j + 1)
                if not isinstance(j, int) or j > 0:
                    pe.wait_ge(s_h1lo, j)
                for k in range(KH):
                    last = nc.tensor.transpose(PS[:, 0, k * P:(k + 1) * P], hn[:, p, k * P:(k + 1) * P], ident[:, :])
                last.then_inc(s_t1, 1)

            def weights_at(w0):
                return [(parts[:, bass.ds(w0 + k * XF, XF)], parts[:, bass.ds(w0 + (half + k * XF), XF)]) for k in range(KH)]

            def first(j, p):
                w0 = nc.tensor.value_load(tile_w[0:1, bass.ds(j, 1)], min_val=0, max_val=(XE - 1) * KH * XF)
                pe.wait_ge(s_h1lo, j + 1)
                if not isinstance(j, int) or j > 1:
                    pe.wait_ge(s_ac, j - 1)
                split_product(PS[:, 2 + p, :], [(hT[:, p, 0, k, :], hT[:, p, 1, k, :], wh, wl)
                                                for k, (wh, wl) in enumerate(weights_at(w0))]).then_inc(s_mm1, 1)

            def second(j, p):
                w0 = nc.tensor.value_load(tile_w[0:1, bass.ds(j, 1)], min_val=0, max_val=(XE - 1) * KH * XF)
                pe.wait_ge(s_h2lo, j + 1)
                if not isinstance(j, int) or j > 1:
                    pe.wait_ge(s_x1, j - 1)
                split_product(PS[:, 4 + p, :], [(aT[:, p, 0, k, :], aT[:, p, 1, k, :], wh, wl)
                                                for k, (wh, wl) in enumerate(weights_at(w0))]).then_inc(s_mm2, 1)

            def turn2(j, p):
                pe.wait_ge(s_ac, j + 1)
                if not isinstance(j, int) or j > 0:
                    pe.wait_ge(s_h2lo, j)
                for k in range(KH):
                    last = nc.tensor.transpose(PS[:, 1, k * P:(k + 1) * P], acA[:, p, k * P:(k + 1) * P], ident[:, :])
                last.then_inc(s_t2, 1)

            def stepA(j, p, more):
                first(j, p)
                if more:
                    turn1(j + 1, 1 - p)
                if not isinstance(j, int) or j > 0:
                    second(j - 1, 1 - p)
                turn2(j, p)
            turn1(0, 0)
            pe.wait_ge(s_wxlo, XE)
            pe.wait_ge(s_slotA, 1)
            stepA(0, 0, True)
            stepA(1, 1, True)
            stepA(2, 0, True)
            with pe.Fori(0, (NT - 5) // 2) as it:
                stepA(2 * it + 3, 1, True)
                stepA(2 * it + 4, 0, True)
            stepA(NT - 2, 1, True)
            stepA(NT - 1, 0, False)
            second(NT - 1, 0)

            pe.wait_ge(s_gatew, 16)
            pe.wait_ge(s_h2lo, NT)
            pe.wait_ge(s_ac, NT)

            def turnB(c):
                pe.wait_ge(s_hl[c], 16)
                for k in range(KH):
                    if c > 0:
                        pe.wait_ge(s_hTf, KH * (c - 1) + k + 1)
                    for n in range(4):
                        last = nc.tensor.transpose(PS[:, k, n * P:(n + 1) * P], rows[:, 4 * c + n, k * P:(k + 1) * P], ident[:, :])
                    last.then_inc(s_tB, 1)

            def logit(c):
                if c > 1:
                    pe.wait_ge(s_lgT, c - 1)
                for k in range(KH):
                    pe.wait_ge(s_hTf, KH * c + k + 1)
                    last = mm(PS[0:E, 4 + c % 2, :], gate_w[:, k, :], hTf[:, c % 2, k, :], start=(k == 0), stop=(k == KH - 1))
                last.then_inc(s_lg, 1)

            def turn_logits(c):
                pe.wait_ge(s_lgT, c + 1)
                if c > 1:
                    pe.wait_ge(s_lgc, c - 1)
                for n in range(4):
                    last = nc.tensor.transpose(PS[:, 6 + c % 2, n * E:(n + 1) * E], lgT[:, c % 2, n * P:(n + 1) * P], ident[0:E, 0:E])
                last.then_inc(s_lgb, 1)
            turnB(0)
            for c in range(4):
                if c < 3:
                    turnB(c + 1)
                logit(c)
                if c > 0:
                    turn_logits(c - 1)
            turn_logits(3)

            def turn_group(g, gp):
                for q in range(GROUP):
                    if q == 0:
                        pe.wait_ge(s_xr[gp], (g - gp) * 8 + 16)
                    if isinstance(g, int) and g == 0:
                        pe.wait_ge(s_hTf, 4 * KH)
                    else:
                        pe.wait_ge(s_glo, GROUP * g + q - 1)
                    for k in range(KH):
                        last = nc.tensor.transpose(PS[:, q, k * P:(k + 1) * P], xrow[:, gp, q, H + k * P:H + (k + 1) * P], ident[:, :])
                    last.then_inc(s_tg2, 1)

            def gate_up(g, gp, m):
                n, r = 6 * g + m, MST[m]
                if not isinstance(g, int) or n > 1:
                    pe.wait_ge(s_acB, n - 1)
                for u in range(2):
                    terms = []
                    for k in range(KH):
                        lo = k * 2 * MS + u * MS + MSO[m]
                        terms.append((sh_part(0, lo, r), sh_part(1, lo, r), hTg[:, gp, 0, k, :], hTg[:, gp, 1, k, :]))
                    last = split_product(PS[0:r, 2 + m % 2, u * GN:(u + 1) * GN], terms)
                last.then_inc(s_gu, 1)

            def down(g, gp):
                def part(q, ms):
                    for m in ms:
                        r = MST[m]
                        lo = SGU + m * H
                        for pa, pb in ((0, 0), (0, 1), (1, 0)):
                            last = mm(PS[:, 4 + q, :], actB[0:r, pa, m, q * P:(q + 1) * P], sh_part(pb, lo, H, r),
                                      start=(m == 0 and pa == pb), stop=(m == 5 and pa == 1))
                    return last
                pe.wait_ge(s_blo, 6 * g + 5)
                if not isinstance(g, int) or g > 0:
                    pe.wait_ge(s_res, GROUP * g)
                for q in range(GROUP):
                    part(q, range(5))
                pe.wait_ge(s_blo, 6 * g + 6)
                for q in range(GROUP):
                    part(q, [5]).then_inc(s_dn, 1)

            def ranks():
                pe.wait_ge(s_pre, 1)
                pe.wait_ge(s_lgc, 4)
                mm(PS[:, 6, 0:E], ones[:, :], pre[:, NTOK, :], start=True, stop=True).then_inc(s_cnt, 1)
                pe.wait_ge(s_cm1, 1)
                for b_ in range(2):
                    dst = PS[:, 6 + b_, :]
                    mm(dst, before[:, :], mask[:, 8 * b_:8 * b_ + 8, :].rearrange("p i e -> p (i e)"), start=True, stop=False)
                    last = mm(dst, ones[:, :], pre[:, 8 * b_:8 * b_ + 8, :].rearrange("p i e -> p (i e)"), start=False, stop=True)
                last.then_inc(s_pos, 1)

            def turn_over():
                pe.wait_ge(s_over, 1)
                for c in range(4):
                    if c >= 2:
                        pe.wait_ge(s_ovTc, c - 1)
                    for n in range(4):
                        last = nc.tensor.transpose(PS[0:E, 6 + c % 2, n * P:(n + 1) * P], over_w[:, 4 * c + n, :], ident[:, :])
                    last.then_inc(s_ovT, 1)

            def turn_x(e, par):
                pe.wait_ge(s_xg[par], (e - par) * 8 + 16)
                if not isinstance(e, int) or e > 0:
                    pe.wait_ge(s_xlo, 2 * e)
                else:
                    pe.wait_ge(s_glo, GROUP * NGRP)
                for k in range(KH):
                    for c in range(2):
                        o = (k % 2) * CAP + c * HC
                        last = nc.tensor.transpose(PS[:, k // 2, o:o + HC], xg[:, par, c, k * P:(k + 1) * P], ident[0:HC, 0:HC])
                last.then_inc(s_tx, 1)

            def stepB(g, gp, more):
                for m in range(6):
                    gate_up(g, gp, m)
                if more:
                    turn_group(g + 1, 1 - gp)
                else:
                    turn_x(0, 0)
                down(g, gp)
            turn_group(0, 0)
            pe.wait_ge(s_shlo, len(SH_CHUNKS))
            pe.wait_ge(s_glo, GROUP)
            for m in range(6):
                gate_up(0, 0, m)
            ranks()
            turn_group(1, 1)
            down(0, 0)
            pe.wait_ge(s_glo, 2 * GROUP)
            stepB(1, 1, True)
            turn_over()
            with pe.Fori(0, NGRP // 2 - 2) as it:
                for p in range(2):
                    pe.wait_ge(s_glo, GROUP * (2 * it + 3 + p))
                    stepB(2 * it + 2 + p, p, True)
            pe.wait_ge(s_glo, GROUP * (NGRP - 1))
            stepB(NGRP - 2, 0, True)
            pe.wait_ge(s_glo, GROUP * NGRP)
            stepB(NGRP - 1, 1, False)

            def stepC(e, par, more):
                pe.wait_ge(s_xlo, 2 * (e + 1))
                for m in range(3):
                    r = MT[m]
                    if not isinstance(e, int) or e > 0 or m > 1:
                        pe.wait_ge(s_cg, 3 * e + m - 1)
                    b0 = cbank(par, m).start
                    for u in range(2):
                        for k in range(KH):
                            if m == 0 and u == 0:
                                pe.wait_ge(s_wlo, 7 * e + k + 1)
                            lo = k * 2 * M + u * M + m * P
                            mm(PS[0:r, b0 + u, 0:2 * CAP], w_part(par, 0, lo, r),
                               xT[:, par, k, :, :].rearrange("p t n -> p (t n)"), start=(k == 0), stop=False)
                            last = mm(PS[0:r, b0 + u, 0:CAP], w_part(par, 1, lo, r), xT[:, par, k, 0, :],
                                      start=False, stop=(k == KH - 1))
                    last.then_inc(s_cgu, 1)
                if more:
                    turn_x(e + 1, 1 - par)
                pe.wait_ge(s_wlo, 7 * (e + 1))
                if not isinstance(e, int) or e > 0:
                    pe.wait_ge(s_ot, 2 * e)
                else:
                    pe.wait_ge(s_res, NTOK)

                def part(c, ms):
                    for m in ms:
                        r = MT[m]
                        for pa, pb in ((0, 0), (0, 1), (1, 0)):
                            last = mm(PS[0:HC, 4 + c, :], actC[0:r, par, pa, m, c * HC:(c + 1) * HC],
                                      w_part(par, pb, WGU + m * H, H, r), start=(m == 0 and pa == pb), stop=(m == 2 and pa == 1))
                    return last
                for m in range(2):
                    pe.wait_ge(s_alo, 3 * e + m + 1)
                    for c in range(2):
                        part(c, [m])
                pe.wait_ge(s_alo, 3 * e + 3)
                for c in range(2):
                    part(c, [2]).then_inc(s_cd, 1)
            pe.wait_ge(s_acB, 6 * NGRP)
            pe.wait_ge(s_ovTc, 4)
            stepC(0, 0, True)
            stepC(1, 1, True)
            with pe.Fori(0, E // 2 - 2) as it:
                stepC(2 * it + 2, 0, True)
                stepC(2 * it + 3, 1, True)
            stepC(E - 2, 0, True)
            stepC(E - 1, 1, False)

            pe.wait_ge(s_ll, 16)
            pe.wait_ge(s_ovTc, 4)
            pe.wait_ge(s_cac, 3 * E)
            for i in range(NTOK):
                if i >= 2:
                    pe.wait_ge(s_fe, i - 1)
                mm(PS[:, i % 2, :], over_wT[:, i, :], lastS[:, :], start=True, stop=True).then_inc(s_f, 1)


_OUTS = [((4, 512, 512), "float32")]


def kernel(x, itok_BxS_13_99985, ctx_2048, g_xattn, g_ffn, L0_ffn_gate_weight, L0_ffn_Wg, L0_ffn_Wu,
           L0_ffn_Wd, L0_ffn_Sg, L0_ffn_Su, L0_ffn_Sd):
    import numpy as np
    import concourse.bacc as bacc
    from concourse.bass_utils import run_bass_kernel_spmd

    def turned(w):
        w = np.asarray(w)
        n = w.ndim
        w = w.reshape(w.shape[:-1] + (w.shape[-1] // P, P))
        return np.moveaxis(np.moveaxis(w, -1, n - 2), -1, n - 1)

    def inner_tiles(w, whole):
        w = np.swapaxes(np.asarray(w), -1, -2)
        head = w[..., :whole * P, :].reshape(w.shape[:-2] + (whole, P, H))
        return np.moveaxis(head, -3, -2).reshape(w.shape[:-2] + (P, whole * H)), w[..., whole * P:, :]

    ffn_gu = np.concatenate([turned(L0_ffn_Wg), turned(L0_ffn_Wu)], axis=-1).reshape(E, P, WGU)
    wdA, wdB = inner_tiles(L0_ffn_Wd, 2)
    sgu = np.concatenate([turned(L0_ffn_Sg), turned(L0_ffn_Su)], axis=-1).reshape(P, SGU)
    sdA, sd_rest = inner_tiles(L0_ffn_Sd, 4)
    sdB = np.moveaxis(sd_rest.reshape(2, 96, H), 0, 1).reshape(96, 2 * H)
    arrays = {
        "x": np.asarray(x).reshape(T, H),
        "tid": np.asarray(itok_BxS_13_99985).reshape(NTOK, P).T,
        "ctxT": turned(ctx_2048).reshape(XE, P, KH * XF),
        "g_x": np.asarray(g_xattn).reshape(1, 1),
        "g_f": np.asarray(g_ffn).reshape(1, 1),
        "gateT": turned(L0_ffn_gate_weight),
        "wgu": ffn_gu, "wdA": wdA, "wdB": wdB, "sgu": sgu, "sdA": sdA, "sdB": sdB,
    }
    arrays = {k: np.ascontiguousarray(a) for k, a in arrays.items()}
    nc = bacc.Bacc("TRN2", target_bir_lowering=False, num_devices=1)
    args = [nc.dram_tensor(k, a.shape, mybir.dt.from_np(a.dtype), kind="ExternalInput").ap() for k, a in arrays.items()]
    out = nc.dram_tensor("out", (T, H), F32, kind="ExternalOutput").ap()
    build(nc, *args, out)
    r = run_bass_kernel_spmd(nc, [arrays], core_ids=[0])
    return r.results[0]["out"].reshape(4, 512, 512)
```

```python
from contextlib import ExitStack

import concourse.bass as bass
from concourse import mybir

P = 128
ALU = mybir.AluOpType
ACT = mybir.ActivationFunctionType
F32 = mybir.dt.float32
F32R = mybir.dt.float32r
BF16 = mybir.dt.bfloat16
I32 = mybir.dt.int32
U32 = mybir.dt.uint32
X = mybir.AxisListType.X

T, H = 2048, 512
KH = H // P
NTOK = T // P
XE, XF = 4, 512
PER_EXPERT = 25000 // XE
NT = NTOK + XE - 1
E, M = 64, 352
MT = [P, P, M - 2 * P]
CAP = 192
HC = CAP // 2
TOPK, NG, TOPG = 6, 8, 3
GS = E // NG
MS = 704
MST = [P] * 4 + [96] * 2
MSO = [P * min(i, 4) + 96 * max(i - 4, 0) for i in range(6)]
EPS = 1e-5
RW = H + E
FLOOR = -87.3365
BIG = 1e30
SKIP = 2 * T
NOSLOT = 32768
GROUP = 2
NGRP = NTOK // GROUP
GN = GROUP * P
WGU, WD = KH * 2 * M, 3 * H
WE = WGU + WD
SGU, SD = KH * 2 * MS, 6 * H
WX = XE * KH * XF


def at_least(engine, sem, value):
    if not isinstance(value, int) or value > 0:
        engine.wait_ge(sem, value)


def build(nc, x, tid, ctxT, g_x, g_f, gateT, wgu, wdA, wdB, sgu, sdA, sdB, out):
    x1_rows = nc.dram_tensor("x1_rows", [T, 2 * H], F32).ap()
    token_rows = nc.dram_tensor("token_rows", [T, RW], F32).ap()
    slot_token = nc.dram_tensor("slot_token", [E * CAP, 1], F32).ap()
    last_rows = nc.dram_tensor("last_rows", [E, H], F32).ap()

    ctx = ExitStack()
    with ctx:
        def sem(name):
            return ctx.enter_context(nc.semaphore(name))

        base = (nc.sbuf_base + 63) // 64 * 64
        top = [base]

        def sb(name, shape, dt, at=None):
            size = 1
            for d in shape[1:]:
                size *= d
            size *= 2 if dt == BF16 else 4
            size = (size + 31) // 32 * 32
            offset = top[0] if at is None else at
            t = nc.alloc_sbuf_tensor_at(name, shape, dt, offset=offset)
            if at is None:
                top[0] += size
            return t, offset, offset + size

        def keep(name, shape, dt):
            return sb(name, shape, dt)[0]

        ident = keep("ident", [P, P], F32)
        before = keep("before", [P, P], BF16)
        ones = keep("ones", [P, P], BF16)
        gate_w = keep("gate_w", [P, KH, E], F32)
        e_slot = keep("e_slot", [P, E], F32)
        tok_id = keep("tok_id", [P, NTOK], F32)
        no_token = keep("no_token", [P, E * CAP // P], F32)
        minus_half = keep("minus_half", [P, KH], F32)
        last_skip = keep("last_skip", [HC, 2], F32)
        gates = keep("gates", [P, 2], F32)
        tg = keep("tg", [P, 2], F32)
        over_wT = keep("over_wT", [2 * E, NTOK, P], F32)
        slot_of = keep("slot_of", [P, NTOK, 8], U32)
        logits, logits_at, _ = sb("logits", [P, NTOK, E], F32)
        over_w = sb("over_w", [P, NTOK, E], F32, at=logits_at)[0]

        parts = keep("parts", [P, 2 * max(WX, SGU + SD, 2 * WE)], F32R)
        half = 2 * WE
        raw, raw_at, raw_end = sb("raw", [P, 2 * WE], F32)
        assert WX <= 2 * WE and SGU + SD == 2 * WE
        xs, xs_at, xs_end = sb("xs", [P, NT, H], F32)
        rows = sb("rows", [P, NTOK, RW], F32, at=xs_at)[0]
        scratch = top[0]

        def region(start):
            at = [start]

            def alloc(name, shape, dt):
                t, _, end = sb(name, shape, dt, at=at[0])
                at[0] = end
                return t
            return alloc

        a = region(scratch)
        hn = a("hn", [P, 2, H], F32)
        hT = a("hT", [P, 2, 2, KH, P], F32R)
        aT = a("aT", [P, 2, 2, KH, P], F32R)
        suA = a("suA", [P, 2, H], F32)
        acA = a("acA", [P, 2, H], F32)
        yrow = a("yrow", [P, 2, 2 * H], F32)
        st6 = a("st6", [P, 2, 6], F32)
        st2 = a("st2", [P, 2, 6], F32)
        mv2 = a("mv2", [P, 2, 2], F32)
        ve2 = a("ve2", [P, 2], F32)
        rs2 = a("rs2", [P, 2], F32)
        mvA = a("mvA", [P, 2, 2], F32)
        veA = a("veA", [P, 2], F32)
        rsA = a("rsA", [P, 2], F32)
        tidi = a("tidi", [P, NTOK], I32)
        tidf = a("tidf", [P, NTOK], F32)
        ge = a("ge", [P, XE + 1, NTOK], F32)
        ohA = a("ohA", [P, XE, NTOK], BF16)
        preA = a("preA", [P, XE, NTOK + 1], BF16)
        sumA = a("sumA", [P, 2, XE, NTOK], BF16)
        limit = a("limit", [P, XE, NTOK], F32)
        cntA = a("cntA", [P, XE], F32)
        over_m = a("over_m", [P, XE, NTOK], F32)
        tilesA = a("tilesA", [P, XE], F32)
        startA = a("startA", [P, XE], F32)
        base_slot = a("base_slot", [P, XE], F32)
        posA = a("posA", [P, XE, NTOK], F32)
        posB = a("posB", [P, XE, NTOK], F32)
        slotA = a("slotA", [P, NTOK], F32)
        slotI = a("slotI", [P, NTOK], I32)
        slot_hi = a("slot_hi", [P, NTOK], I32)
        slot_lo = a("slot_lo", [P, NTOK], I32)
        place = a("place", [P, 2, NTOK], F32)
        row_no = a("row_no", [P, P], F32)
        part_no = a("part_no", [P, 1], F32)
        step_no = a("step_no", [P, NTOK], F32)
        at_row = a("at_row", [P, NTOK, P], BF16)
        at_tile = a("at_tile", [P, NTOK, 3, NT], BF16)
        list_f = a("list_f", [P, 2, NT], F32)
        tile_no = a("tile_no", [1, NT + 1], F32)
        tile_e = a("tile_e", [1, 3, NT + 1], F32)
        tile_w = a("tile_w", [1, NT + 1], I32)
        list_g = a("list_g", [P, NT], U32)
        list_s = a("list_s", [P, NT], U32)
        b = region(scratch)
        xrow = b("xrow", [P, 2, GROUP, 2 * H], F32)
        suB = b("suB", [P, 2, GN], F32)
        acB = b("acB", [P, 2, GN], F32)
        hTg, hTg_at, hTg_end = sb("hTg", [P, 2, 2, KH, GN], F32R, at=scratch + 4 * 2 * (GROUP * 2 * H + 2 * GN))
        hTf = sb("hTf", [P, 2, KH, H], F32, at=hTg_at)[0]
        b = region(hTg_end)
        lgT = sb("lgT", [E, 2, H], F32, at=hTg_end)[0]
        actB = b("actB", [P, 2, 6, GN], F32R)
        cm1 = b("cm1", [P, E], F32)
        b_ = region(xs_at + 4 * NTOK * RW)
        key8 = b_("key8", [P, NTOK, 8], F32)
        none8 = b_("none8", [P, NTOK, 8], F32)
        g13 = b_("g13", [P, NTOK, NG + 5], F32)
        g8 = b("g8", [P, NTOK, 8], F32)
        pen = b("pen", [P, NTOK, NG], F32)
        mx = b("mx", [P, NTOK], F32)
        sm = b("sm", [P, NTOK], F32)
        rc = b("rc", [P, NTOK], F32)
        EW = E + 2
        ra = region(raw_at)
        z0 = ra("z0", [P, NTOK, EW], F32)
        z1 = ra("z1", [P, NTOK, EW], F32)
        z2 = ra("z2", [P, NTOK, EW], F32)
        z3 = ra("z3", [P, NTOK, EW], F32)
        z4 = ra("z4", [P, NTOK, EW], F32)
        z5 = ra("z5", [P, NTOK, EW], F32)
        z7 = ra("z7", [P, NTOK, EW], F32)
        mask = ra("mask", [P, NTOK, E], BF16)
        pre = ra("pre", [P, NTOK + 1, E], BF16)
        g13r = ra("g13r", [P, NTOK, NG + 5], F32)
        assert 4 * (7 * NTOK * EW + NTOK * (NG + 5)) + 2 * (2 * NTOK + 1) * E <= raw_end - raw_at
        c_ = region(xs_at)
        xg = c_("xg", [HC, 2, 2, RW], F32)
        slot_list = c_("slot_list", [2 * E, HC], F32)
        list_T = c_("list_T", [HC, E, 2], F32)
        xT = c_("xT", [P, 2, KH, 2, CAP], F32R)
        gtok = c_("gtok", [HC, 2, 2], U32)
        suC = c_("suC", [P, 3, CAP], F32)
        acC = c_("acC", [P, 3, CAP], F32)
        guC = c_("guC", [P, 3, 2, CAP], F32)
        c_ = region(hTg_at)
        actC = c_("actC", [P, 2, 2, 3, CAP], F32R)
        xlC = c_("xlC", [P, 3, 2, CAP], F32)
        ot = c_("ot", [HC, 2, 2, H], F32)
        wcol = c_("wcol", [HC, 2, 2], F32)
        tokc = c_("tokc", [HC, 2, 2], U32)
        lastS = c_("lastS", [2 * E, H], F32)
        last_p = c_("last_p", [2 * E, 2, H], F32R)
        fb = sb("fb", [P, NTOK, H], F32, at=xs_at)[0]
        d_ = region(raw_at)
        over_p = d_("over_p", [2 * E, NTOK, P], F32R)
        assert 8 * NTOK * P <= 4 * WE

        PS = ctx.enter_context(nc.psum_tensor("PS", [P, 8, H], F32))

        s_tid, s_gates, s_gatew = sem("tid_loaded"), sem("gates_loaded"), sem("gatew_loaded")
        s_wx = [sem(f"wx_loaded{e}") for e in range(XE)]
        s_sh = [sem(f"shared_loaded{i}") for i in range(2)]
        s_pad = sem("slots_padded")
        s_const, s_const2 = sem("const_first"), sem("const_ready")
        s_tg = sem("tanh_ready")
        s_apart = sem("wait_carrier")
        v_a = sem("dve_chain")
        s_ohA, s_cntA, s_slotA = sem("ohA_ready"), sem("ranksA_ready"), sem("slotA_ready")
        s_place, s_lmm, s_list = sem("places_ready"), sem("token_list_summed"), sem("token_list_ready")
        s_wxhi, s_wxlo, s_wxlo0 = sem("wx_hi_ready"), sem("wx_lo_ready"), sem("wx_lo_first_ready")
        s_x = [sem(f"x_gathered{i}") for i in range(2)]
        s_var, s_rstd, s_hn = sem("varA_ready"), sem("rstdA_ready"), sem("hnA_ready")
        s_t1, s_h1hi, s_h1lo = sem("hA_turned"), sem("hTA_hi_ready"), sem("hTA_lo_ready")
        s_mm1, s_su, s_ac = sem("uA_ready"), sem("siluA_ready"), sem("actA_ready")
        s_t2, s_h2hi, s_h2lo = sem("actA_turned"), sem("aTA_hi_ready"), sem("aTA_lo_ready")
        s_mm2, s_x1, s_x1s = sem("yA_ready"), sem("x1_ready"), [sem(f"x1_scattered{i}") for i in range(2)]
        s_var2, s_rstd2, s_h2 = sem("var2_ready"), sem("rstd2_ready"), sem("h2_ready")
        s_bn1, s_ag1, s_bn2, s_ag2 = sem("stats1"), sem("aggregate1"), sem("stats2"), sem("aggregate2")
        s_shhi, s_shlo = sem("shared_hi_ready"), sem("shared_lo_ready")
        s_h0 = [sem(f"h_first_loaded{k}") for k in range(KH)]
        s_hl = [None] + [sem(f"h_loaded{i}") for i in range(1, 4)]
        s_tB, s_hTf = sem("hB_turned"), sem("hTf_ready")
        s_lg, s_lgT, s_lgb, s_lgc = sem("logitsT_done"), sem("logitsT_kept"), sem("logits_turned"), sem("logits_kept")
        v_r = sem("routing_chain")
        s_d, s_exp, s_pre = sem("logits_shifted"), sem("exp_ready"), sem("prefix_ready")
        s_cnt, s_cm1, s_pos = sem("counts_done"), sem("counts_kept"), sem("ranks_done")
        s_slot, s_over = sem("slots_ready"), sem("over_weights_ready")
        s_ovT, s_ovTc = sem("over_weights_turned"), sem("over_wT_ready")
        s_disp, s_roww, s_rows = sem("tokens_dispatched"), sem("row_weights_ready"), sem("rows_stored")
        s_lc, s_lct, s_lcc, s_gt = sem("slot_list_loaded"), sem("slot_list_turned"), sem("slot_list_ready"), sem("row_indices_ready")
        s_xr = [sem(f"x1_row_loaded{i}") for i in range(2)]
        s_tg2, s_ghi, s_glo = sem("h_group_turned"), sem("hTg_hi"), sem("hTg_lo")
        s_gu, s_suB, s_acB = sem("gateup_done"), sem("siluB_ready"), sem("actB_product")
        s_bhi, s_blo, s_dn = sem("actB_hi"), sem("actB_lo"), sem("downB_done")
        s_res = sem("shared_added")
        s_st = [sem(f"out_stored{i}") for i in range(2)]
        s_raw = [sem(f"expert_gateup_loaded{i}") for i in range(2)]
        s_rawd = [sem(f"expert_down_loaded{i}") for i in range(2)]
        s_xg = [sem(f"expert_rows_loaded{i}") for i in range(2)]
        s_whi, s_wlo = sem("w_hi"), sem("w_lo")
        s_tx, s_xhi, s_xlo = sem("x_turned"), sem("xT_hi"), sem("xT_lo")
        s_cxlc, s_cg = sem("x_lo_part_copied"), sem("expert_gateup_summed")
        s_cgu, s_csu, s_cac = sem("expert_gateup_done"), sem("expert_silu"), sem("expert_product")
        s_ahi, s_alo, s_cd = sem("expert_act_hi"), sem("expert_act_lo"), sem("expert_down_done")
        s_ot, s_wc = sem("expert_out_ready"), sem("slot_weights_ready")
        s_add = sem("rows_added")
        s_last = [sem(f"last_row_stored{i}") for i in range(2)]
        s_twice = sem("over_wT_copied")
        s_ophi, s_opp, s_lhi, s_llo = sem("over_hi_ready"), sem("over_parts_ready"), \
            sem("last_hi_ready"), sem("last_lo_ready")
        s_ll, s_f, s_fe, s_fa = sem("last_rows_loaded"), sem("over_done"), [sem(f"over_copied{i}") for i in range(2)], sem("over_added")

        SH_CHUNKS = [(k * 2 * MS, 2 * MS, P) for k in range(KH)] + \
                    [(SGU + i * H, H, MST[i]) for i in range(6)]
        W_CHUNKS = [(k * 2 * M, 2 * M, P) for k in range(KH)] + \
                   [(WGU + i * H, H, MT[i]) for i in range(3)]
        x1_tiled = x1_rows.rearrange("(i p) h -> p i h", p=P)
        out_tiled = out.rearrange("(i p) h -> p i h", p=P)

        def w_part(par, part, lo, n, rows_=P):
            o = par * 2 * WE + (part * WGU + lo if lo < WGU else 2 * WGU + part * WD + lo - WGU)
            return parts[0:rows_, o:o + n]

        def sh_part(part, lo, n, rows_=P):
            o = part * (SGU + SD) + lo
            return parts[0:rows_, o:o + n]

        def wait_apart(engine, sem_, value):
            at_least(engine, sem_, value)
            if not isinstance(value, int):
                engine.sem_inc(s_apart, 1)

        def cbank(par, m):
            b0 = (6, 2)[(3 * par + m) % 2]
            return slice(b0, b0 + 2)

        block = ctx.enter_context(nc.Block())

        @block.sync
        def _(sp):
            sp.dma_start(tidi[:, :], tid).then_inc(s_tid, 16)
            sp.dma_start(gates[:, 0:1], g_x.broadcast_to([P, 1])).then_inc(s_gates, 16)
            sp.dma_start(gates[:, 1:2], g_f.broadcast_to([P, 1])).then_inc(s_gates, 16)
            for e in range(XE):
                sp.dma_start(raw[:, e * KH * XF:(e + 1) * KH * XF], ctxT[e]).then_inc(s_wx[e], 16)
            sp.dma_start(gate_w[:, :, :], gateT).then_inc(s_gatew, 16)
            sp.wait_ge(s_const2, 2)
            sp.dma_start(slot_token.rearrange("(p n) o -> p (n o)", p=P), no_token[:, :]).then_inc(s_pad, 16)
            sp.wait_ge(s_wxlo, XE - 1)
            sp.wait_ge(s_wxlo0, 1)
            for i in range(KH + 2):
                sp.wait_ge(s_x1, i + 1)
                if i < KH:
                    o = i * 2 * MS
                    sp.dma_start(raw[:, o:o + 2 * MS], sgu[:, o:o + 2 * MS]).then_inc(s_sh[0], 16)
                elif i == KH:
                    sp.dma_start(raw[:, SGU:SGU + 4 * H], sdA).then_inc(s_sh[1], 16)
                else:
                    sp.dma_start(raw[0:96, SGU + 4 * H:SGU + SD], sdB).then_inc(s_sh[1], 16)
            sp.wait_ge(s_x1s[0], 16 * ((NT + 1) // 2))
            sp.wait_ge(s_x1s[1], 16 * (NT // 2))
            for k in range(KH):
                sp.dma_start(rows[:, 0:4, k * P:(k + 1) * P], x1_tiled[:, 0:4, H + k * P:H + (k + 1) * P]).then_inc(s_h0[k], 16)
            for c in range(1, 4):
                sp.dma_start(rows[:, 4 * c:4 * c + 4, 0:H], x1_tiled[:, 4 * c:4 * c + 4, H:2 * H]).then_inc(s_hl[c], 16)

            def b2_load(g, gp):
                if not (isinstance(g, int) and g < 2):
                    wait_apart(sp, s_st[gp], (g - gp) * 8)
                src = x1_rows[bass.ds(g * GN, GN), :].rearrange("(q p) h -> p q h", p=P)
                sp.dma_start(xrow[:, gp, :, :], src).then_inc(s_xr[gp], 16)

            def b2_store(g, gp):
                wait_apart(sp, s_res, GROUP * (g + 1))
                dst = out[bass.ds(g * GN, GN), :].rearrange("(q p) h -> p q h", p=P)
                sp.dma_start(dst, xrow[:, gp, :, 0:H]).then_inc(s_st[gp], 16)

            b2_load(0, 0)
            b2_load(1, 1)
            def load_w(e, par):
                first_two = isinstance(e, int) and e < 2
                wait_apart(sp, s_wlo, 0 if first_two else 7 * (e - 2) + KH)
                o = par * WE
                sp.dma_start(raw[:, o:o + WGU], wgu[bass.ds(e, 1)].rearrange("o p n -> (o p) n")).then_inc(s_raw[par], 16)
                wait_apart(sp, s_wlo, 0 if first_two else 7 * (e - 1))
                sp.dma_start(raw[:, o + WGU:o + WGU + 2 * H], wdA[bass.ds(e, 1)].rearrange("o p n -> (o p) n")).then_inc(s_rawd[par], 16)
                sp.dma_start(raw[0:MT[2], o + WGU + 2 * H:o + WE], wdB[bass.ds(e, 1)].rearrange("o p n -> (o p) n")).then_inc(s_rawd[par], 16)

            for g in range(NGRP - 2):
                b2_store(g, g % 2)
                b2_load(g + 2, g % 2)
                if g in (2, 3):
                    sp.wait_ge(s_roww, 1)
                    for c in (2 * g - 4, 2 * g - 3):
                        sp.dma_start(token_rows.rearrange("(i p) w -> p i w", p=P)[:, 4 * c:4 * c + 4, :],
                                     rows[:, 4 * c:4 * c + 4, :]).then_inc(s_rows, 16)
                if g in (4, 5):
                    sp.wait_ge(s_over, 1)
                    load_w(g - 4, g - 4)
                if g == 5:
                    sp.wait_ge(s_ovTc, 4)
                    sp.dma_start(over_wT[E:2 * E, :, :], over_wT[0:E, :, :]).then_inc(s_twice, 16)
            sp.wait_ge(s_disp, 16 * NTOK * TOPK)
            sp.wait_ge(s_rows, 64)
            sp.dma_start(slot_list[:, :], slot_token.rearrange("(r p) o -> r (p o)", p=HC)).then_inc(s_lc, 16)
            b2_store(NGRP - 2, 0)
            b2_store(NGRP - 1, 1)

            def store_last(e, par):
                wait_apart(sp, s_ot, 2 * (e + 1))
                sp.dma_start(last_rows[bass.ds(e, 1), :], ot[HC - 1:HC, par, 1, :]).then_inc(s_last[par], 16)
            for e in (2, 3):
                load_w(e, e % 2)
            store_last(0, 0)
            with sp.Fori(0, E // 2 - 2) as it:
                for p in range(2):
                    load_w(2 * it + 4 + p, p)
                    store_last(2 * it + 1 + p, 1 - p)
            for e in (E - 3, E - 2):
                store_last(e, e % 2)
            sp.wait_ge(s_last[0], 16 * E // 2)
            sp.wait_ge(s_last[1], 16 * (E // 2 - 1))
            for o in (0, E):
                sp.dma_start(lastS[o:o + E - 1, :], last_rows[0:E - 1, :]).then_inc(s_ll, 16)
            sp.wait_ge(s_ot, 2 * E)
            for o in (0, E):
                sp.dma_start(lastS[o + E - 1:o + E, :], ot[HC - 1:HC, 1, 1, :]).then_inc(s_ll, 16)

        @block.gpsimd
        def _(pool):
            pool.memset(ident[:, :], 0.0).then_inc(s_const, 1)
            pool.iota(tok_id[:, :], [[P, NTOK]], base=0, channel_multiplier=1,
                      allow_small_or_imprecise_dtypes=True).then_inc(s_const2, 1)
            pool.memset(before[:, :], 1.0).then_inc(s_const, 1)
            pool.iota(row_no[:, :], [[1, P]], base=0, channel_multiplier=0, allow_small_or_imprecise_dtypes=True)
            pool.iota(part_no[:, :], [[0, 1]], base=0, channel_multiplier=1, allow_small_or_imprecise_dtypes=True)
            pool.iota(step_no[:, :], [[1, NTOK]], base=0, channel_multiplier=0, allow_small_or_imprecise_dtypes=True)
            pool.memset(ones[:, :], 1.0)
            pool.iota(limit[:, :, :], [[0, XE], [P, NTOK]], base=0, channel_multiplier=0,
                      allow_small_or_imprecise_dtypes=True)
            pool.iota(tile_no[:, :], [[1, NT + 1]], base=0, channel_multiplier=0,
                      allow_small_or_imprecise_dtypes=True)
            pool.wait_ge(s_const, 2)
            pool.affine_select(out=ident[:, :], in_=ident[:, :], compare_op=ALU.not_equal, fill=1.0,
                               base=0, pattern=[[-1, P]], channel_multiplier=1)
            pool.affine_select(out=before[:, :], in_=before[:, :], compare_op=ALU.is_gt, fill=0.0,
                               base=0, pattern=[[1, P]], channel_multiplier=-1)
            pool.memset(no_token[:, :], float(SKIP))
            pool.memset(last_skip[:, :], 0.0).then_inc(s_const, 1)
            pool.memset(minus_half[:, :], -0.5)
            pool.wait_ge(s_const, 3)
            pool.affine_select(out=last_skip[:, 1:2], in_=last_skip[:, 1:2], compare_op=ALU.not_equal,
                               fill=float(SKIP), base=-(HC - 1), pattern=[[0, 1]], channel_multiplier=1)
            pool.iota(e_slot[:, :], [[CAP, E]], base=1, channel_multiplier=0,
                      allow_small_or_imprecise_dtypes=True).then_inc(s_const2, 1)
            pool.wait_ge(s_wxhi, 1)
            pool.tensor_tensor(parts[:, half:half + KH * XF], raw[:, 0:KH * XF], parts[:, 0:KH * XF].bitcast(F32),
                               ALU.subtract).then_inc(s_wxlo0, 1)
            pool.wait_ge(s_list, 1)

            def rstdA(j):
                pool.wait_ge(s_var, j + 1)
                if j >= 2:
                    pool.wait_ge(s_hn, j - 1)
                pool.tensor_tensor(rsA[:, j % 2:j % 2 + 1], veA[:, j % 2:j % 2 + 1],
                                   minus_half[:, 0:1], ALU.pow).then_inc(s_rstd, 1)

            def gather(j):
                if j >= 2:
                    pool.wait_ge(s_x[j % 2], 16 * (j // 2))
                pool.indirect_dma_start(xs[:, j, :], None, x,
                                        bass.IndirectOffsetOnAxis(ap=list_g[:, j:j + 1], axis=0),
                                        bounds_check=T - 1, oob_is_err=False).then_inc(s_x[j % 2], 16)

            def rstd2(j):
                pool.wait_ge(s_var2, j + 1)
                if j >= 2:
                    pool.wait_ge(s_h2, j - 1)
                pool.tensor_tensor(rs2[:, j % 2:j % 2 + 1], ve2[:, j % 2:j % 2 + 1],
                                   minus_half[:, 0:1], ALU.pow).then_inc(s_rstd2, 1)

            def scatter(j):
                pool.wait_ge(s_h2, j + 1)
                pool.indirect_dma_start(x1_rows, bass.IndirectOffsetOnAxis(ap=list_s[:, j:j + 1], axis=0),
                                        yrow[:, j % 2, :], None, bounds_check=T - 1,
                                        oob_is_err=False).then_inc(s_x1s[j % 2], 16)
            AHEAD = 5
            gather(0)
            gather(1)
            for j in range(3):
                rstdA(j)
                gather(j + 2)
            for j in range(NT):
                if j + AHEAD < NT:
                    gather(j + AHEAD)
                if j >= 2:
                    scatter(j - 2)
                if j + 3 < NT:
                    rstdA(j + 3)
                if j >= 1:
                    rstd2(j - 1)
            scatter(NT - 2)
            rstd2(NT - 1)
            scatter(NT - 1)
            pool.wait_ge(s_slot, 1)
            pool.wait_ge(s_pad, 16)
            for i in range(NTOK):
                for k in range(TOPK):
                    pool.indirect_dma_start(slot_token, bass.IndirectOffsetOnAxis(ap=slot_of[:, i, k:k + 1], axis=0),
                                            tok_id[:, i:i + 1], None, bounds_check=E * CAP - 1,
                                            oob_is_err=False).then_inc(s_disp, 16)

            def gather_rows(e, par):
                pool.wait_ge(s_gt, e + 1)
                if not isinstance(e, int) or e > 1:
                    pool.wait_ge(s_wc, 2 * (e - 1))
                for c in range(2):
                    if c == 0 and (not isinstance(e, int) or e > 1):
                        wait_apart(pool, s_tx, e - 1)
                    pool.indirect_dma_start(xg[:, par, c, :], None, token_rows,
                                            bass.IndirectOffsetOnAxis(ap=gtok[:, par, c:c + 1], axis=0),
                                            bounds_check=T - 1, oob_is_err=False).then_inc(s_xg[par], 16)
            pool.wait_ge(s_rows, 64)
            gather_rows(0, 0)
            gather_rows(1, 1)
            pool.wait_ge(s_st[0], 16 * NGRP // 2)
            pool.wait_ge(s_st[1], 16 * NGRP // 2)

            def add_rows(e, par):
                pool.wait_ge(s_wc, 2 * (e + 1))
                at_least(pool, s_add, 32 * e)
                for c in range(2):
                    wait_apart(pool, s_ot, 2 * e + c + 1)
                    pool.indirect_dma_start(out, bass.IndirectOffsetOnAxis(ap=tokc[:, par, c:c + 1], axis=0),
                                            ot[:, par, c, :], None, bounds_check=T - 1, oob_is_err=False,
                                            compute_op=ALU.add).then_inc(s_add, 16)
            for e in range(2):
                gather_rows(e + 2, e)
                add_rows(e, e)
            with pool.Fori(0, E // 2 - 2) as it:
                for p in range(2):
                    gather_rows(2 * it + 4 + p, p)
                    add_rows(2 * it + 2 + p, p)
            add_rows(E - 2, 0)
            add_rows(E - 1, 1)
            for r in range(8):
                for par in range(2):
                    pool.wait_ge(s_fe[par], r + 1)
                if r == 0:
                    pool.wait_ge(s_add, 32 * E)
                pool.dma_start(out_tiled[:, 2 * r:2 * r + 2, :], fb[:, 2 * r:2 * r + 2, :],
                               accum_op=ALU.add).then_inc(s_fa, 16)
            pool.wait_ge(s_fa, 128)

        @block.scalar
        def _(act):
            act.wait_ge(s_gates, 32)
            nc.scalar.activation(tg[:, :], gates[:, :], ACT.Tanh).then_inc(s_tg, 1)
            for e in range(XE):
                act.wait_ge(s_wx[e], 16)
                n = KH * XF
                nc.scalar.activation(parts[:, e * n:(e + 1) * n], raw[:, e * n:(e + 1) * n], ACT.Copy).then_inc(s_wxhi, 1)

            def hi1(j, p):
                act.wait_ge(s_t1, j + 1)
                at_least(act, s_mm1, j - 1 if not isinstance(j, int) or j > 1 else 0)
                nc.scalar.activation(hT[:, p, 0].rearrange("p k n -> p (k n)"), PS[:, 0, :], ACT.Copy).then_inc(s_h1hi, 1)

            def stepA(j, p, more):
                act.wait_ge(s_mm1, j + 1)
                if not isinstance(j, int) or j > 1:
                    act.wait_ge(s_ac, j - 1)
                nc.scalar.activation(suA[:, p, :], PS[:, 2 + p, :], ACT.Silu).then_inc(s_su, 1)
                if more:
                    hi1(j + 1, 1 - p)
                act.wait_ge(s_t2, j + 1)
                if not isinstance(j, int) or j > 1:
                    act.wait_ge(s_mm2, j - 1)
                nc.scalar.activation(aT[:, p, 0].rearrange("p k n -> p (k n)"), PS[:, 1, :], ACT.Copy).then_inc(s_h2hi, 1)
            hi1(0, 0)
            stepA(0, 0, True)
            stepA(1, 1, True)
            stepA(2, 0, True)
            with act.Fori(0, (NT - 5) // 2) as it:
                stepA(2 * it + 3, 1, True)
                stepA(2 * it + 4, 0, True)
            stepA(NT - 2, 1, True)
            stepA(NT - 1, 0, False)
            act.wait_ge(s_mm2, NT)
            act.wait_ge(s_sh[0], 16 * KH)
            for n_, (lo, n, r) in enumerate(SH_CHUNKS):
                if n_ == KH:
                    act.wait_ge(s_sh[1], 32)
                nc.scalar.activation(sh_part(0, lo, n, r), raw[0:r, lo:lo + n], ACT.Copy).then_inc(s_shhi, 1)

            act.wait_ge(s_x1s[1], 16 * (NT // 2))
            for c in range(4):
                for k in range(KH):
                    act.wait_ge(s_tB, KH * c + k + 1)
                    if c >= 2:
                        act.wait_ge(s_lg, c - 1)
                    nc.scalar.activation(hTf[:, c % 2, k, :], PS[:, k, :], ACT.Copy).then_inc(s_hTf, 1)

            def hiB(g, gp):
                for q in range(GROUP):
                    act.wait_ge(s_tg2, GROUP * g + q + 1)
                    if not isinstance(g, int) or g > 1:
                        act.wait_ge(s_gu, 6 * (g - 1))
                    else:
                        act.wait_ge(s_lg, 3 + g)
                    nc.scalar.activation(hTg[:, gp, 0, :, q * P:(q + 1) * P],
                                         PS[:, q, :].rearrange("p (k n) -> p k n", k=KH), ACT.Copy).then_inc(s_ghi, 1)

            def stepB(g, gp, more):
                for m in range(6):
                    n = 6 * g + m
                    r = MST[m]
                    act.wait_ge(s_gu, n + 1)
                    if not isinstance(g, int) or n > 1:
                        act.wait_ge(s_acB, n - 1)
                    nc.scalar.activation(suB[0:r, m % 2, :], PS[0:r, 2 + m % 2, 0:GN], ACT.Silu).then_inc(s_suB, 1)
                    act.wait_ge(s_acB, n + 1)
                    if not isinstance(g, int) or g > 0:
                        act.wait_ge(s_dn, GROUP * g)
                    nc.scalar.activation(actB[0:r, 0, m, :], acB[0:r, m % 2, :], ACT.Copy).then_inc(s_bhi, 1)
                if more:
                    hiB(g + 1, 1 - gp)

            def over_copy(c):
                act.wait_ge(s_ovT, c + 1)
                nc.scalar.activation(over_wT[0:E, 4 * c:4 * c + 4, :].rearrange("e i t -> e (i t)"),
                                     PS[0:E, 6 + c % 2, :], ACT.Copy).then_inc(s_ovTc, 1)
            hiB(0, 0)
            act.wait_ge(s_d, 1)
            nc.scalar.activation(z1[:, :, 0:E], z0[:, :, 0:E], ACT.Exp).then_inc(s_exp, 1)
            for g in range(3):
                stepB(g, g % 2, True)
            for c in range(4):
                over_copy(c)
            with act.Fori(0, NGRP // 2 - 2) as it:
                stepB(2 * it + 3, 1, True)
                stepB(2 * it + 4, 0, True)
            stepB(NGRP - 1, 1, False)

            def hi_w(e, par, k):
                lo, n, r = W_CHUNKS[k]
                if k == KH:
                    act.wait_ge(s_rawd[par], (e - par) * 16 + 32)
                nc.scalar.activation(w_part(par, 0, lo, n, r), raw[0:r, par * WE + lo:par * WE + lo + n], ACT.Copy).then_inc(s_whi, 1)

            def wait_w(e, par):
                act.wait_ge(s_raw[par], (e - par) * 8 + 16)
                if not isinstance(e, int) or e > 1:
                    act.wait_ge(s_cd, 2 * (e - 1))

            def hi_x(e, par, b_):
                act.wait_ge(s_tx, e + 1)
                if not isinstance(e, int) or e > 1:
                    act.wait_ge(s_cgu, 3 * (e - 1))
                nc.scalar.activation(xT[:, par, 2 * b_:2 * b_ + 2, 0, :],
                                     PS[:, b_, 0:2 * CAP].rearrange("p (k n) -> p k n", k=2), ACT.Copy).then_inc(s_xhi, 1)

            def stepC(e, par, more):
                if more:
                    wait_w(e + 1, 1 - par)
                    hi_w(e + 1, 1 - par, 0)
                def keep_x_lo(m):
                    act.wait_ge(s_cgu, 3 * e + m + 1)
                    at_least(act, s_cg, 3 * e + m - 2 if not isinstance(e, int) or e > 0 else 0)
                    nc.scalar.activation(xlC[0:MT[m], m, :, :], PS[0:MT[m], cbank(par, m), CAP:2 * CAP],
                                         ACT.Copy).then_inc(s_cxlc, 1)

                def silu(m):
                    act.wait_ge(s_cg, 3 * e + m + 1)
                    at_least(act, s_cac, 3 * e + m - 2 if not isinstance(e, int) or e > 0 else 0)
                    nc.scalar.activation(suC[0:MT[m], m, :], guC[0:MT[m], m, 0, :], ACT.Silu).then_inc(s_csu, 1)

                def hi_act(m):
                    act.wait_ge(s_cac, 3 * e + m + 1)
                    if not isinstance(e, int) or e > 1:
                        act.wait_ge(s_cd, 2 * (e - 1))
                    nc.scalar.activation(actC[0:MT[m], par, 0, m, :], acC[0:MT[m], m, :], ACT.Copy).then_inc(s_ahi, 1)
                keep_x_lo(0)
                if more:
                    hi_w(e + 1, 1 - par, 1)
                silu(0)
                hi_act(0)
                keep_x_lo(1)
                if more:
                    hi_w(e + 1, 1 - par, 2)
                silu(1)
                keep_x_lo(2)
                hi_act(1)
                if more:
                    hi_x(e + 1, 1 - par, 0)
                silu(2)
                if more:
                    hi_x(e + 1, 1 - par, 1)
                hi_act(2)
                if more:
                    for k in range(3, 7):
                        hi_w(e + 1, 1 - par, k)
                act.wait_ge(s_wc, 2 * (e + 1))
                if not isinstance(e, int) or e > 1:
                    act.wait_ge(s_add, 32 * (e - 1))
                    act.wait_ge(s_last[par], (e - par) * 8)
                for c in range(2):
                    act.wait_ge(s_cd, 2 * e + c + 1)
                    nc.scalar.activation(ot[:, par, c, :], PS[0:HC, 4 + c, :], ACT.Copy,
                                         scale=wcol[:, par, c:c + 1]).then_inc(s_ot, 1)
            act.wait_ge(s_gu, 6 * NGRP)
            wait_w(0, 0)
            for k in range(KH):
                hi_w(0, 0, k)
            hi_x(0, 0, 0)
            hi_x(0, 0, 1)
            act.wait_ge(s_dn, NTOK)
            for k in range(KH, len(W_CHUNKS)):
                hi_w(0, 0, k)
            stepC(0, 0, True)
            stepC(1, 1, True)
            with act.Fori(0, E // 2 - 2) as it:
                stepC(2 * it + 2, 0, True)
                stepC(2 * it + 3, 1, True)
            stepC(E - 2, 0, True)
            act.wait_ge(s_wlo, 7 * (E - 1))
            act.wait_ge(s_twice, 16)
            nc.scalar.activation(over_p[:, :, :].rearrange("e i t -> e (i t)"), over_wT[:, :, :].rearrange("e i t -> e (i t)"),
                                 ACT.Copy).then_inc(s_ophi, 1)
            stepC(E - 1, 1, False)
            act.wait_ge(s_ll, 64)
            nc.scalar.activation(last_p[:, 0, :], lastS[:, :], ACT.Copy).then_inc(s_lhi, 1)
            for i in range(0, NTOK, 2):
                act.wait_ge(s_f, i + 1)
                nc.scalar.activation(fb[:, i, :], PS[:, i % 4, :], ACT.Copy).then_inc(s_fe[0], 1)

        @block.vector
        def _(dve):
            v = nc.vector
            count = [0]

            def link(ins):
                count[0] += 1
                ins.then_inc(v_a, 1)
                dve.wait_ge(v_a, count[0])
            dve.wait_ge(s_tid, 16)
            link(v.tensor_copy(tidf[:, :], tidi[:, :]))
            v.memset(ge[:, 0, :], 1.0)
            v.memset(ge[:, XE, :], 0.0)
            for e in range(1, XE - 1):
                v.tensor_scalar(ge[:, e, :], tidf[:, :], float(e * PER_EXPERT), None, ALU.is_ge)
            link(v.tensor_scalar(ge[:, XE - 1, :], tidf[:, :], float((XE - 1) * PER_EXPERT), None, ALU.is_ge))
            v.memset(preA[:, :, 0:1], 0.0)
            link(v.tensor_tensor(ohA[:, :, :], ge[:, 0:XE, :], ge[:, 1:XE + 1, :], ALU.subtract))
            src = ohA[:, :, :]
            for n_ in range(4):
                d = 1 << n_
                dst = sumA[:, n_ % 2] if n_ < 3 else preA[:, :, 1:NTOK + 1]
                v.tensor_copy(dst[:, :, 0:d], src[:, :, 0:d])
                link(v.tensor_tensor(dst[:, :, d:NTOK], src[:, :, d:NTOK], src[:, :, 0:NTOK - d], ALU.add))
                src = dst
            v.memset(tilesA[:, :], 0.0).then_inc(s_ohA, 1)
            dve.wait_ge(s_cntA, 1)
            dve.wait_ge(s_const2, 2)
            dve.wait_ge(s_ohA, 1)
            link(v.tensor_copy(cntA[:, :], PS[:, 6, 64:64 + XE]))
            link(v.tensor_tensor(over_m[:, :, :], cntA[:, :].unsqueeze(2).broadcast_to([P, XE, NTOK]),
                                 limit[:, :, :], ALU.is_gt))
            v.memset(startA[:, 0:1], 0.0)
            link(v.tensor_reduce(tilesA[:, :], over_m[:, :, :], X, ALU.add))
            for e in range(1, XE):
                link(v.tensor_tensor(startA[:, e:e + 1], startA[:, e - 1:e], tilesA[:, e - 1:e], ALU.add))
            link(v.tensor_scalar(base_slot[:, :], startA[:, :], float(P), None, ALU.mult))
            link(v.tensor_tensor(posA[:, :, :], PS[:, 6, 0:64].rearrange("p (e i) -> p e i", e=XE),
                                 base_slot[:, :].unsqueeze(2).broadcast_to([P, XE, NTOK]), ALU.add))
            link(v.tensor_tensor(posB[:, :, :], posA[:, :, :], ohA[:, :, :], ALU.mult))
            link(v.tensor_reduce(slotA[:, :], posB[:, :, :].rearrange("p e i -> p i e"), X, ALU.add))
            link(v.tensor_copy(slotI[:, :], slotA[:, :]))
            v.tensor_scalar(slot_hi[:, :], slotI[:, :], 7, None, ALU.logical_shift_right)
            link(v.tensor_scalar(slot_lo[:, :], slotI[:, :], P - 1, None, ALU.bitwise_and))
            v.tensor_copy(place[:, 0, :], slot_hi[:, :])
            link(v.tensor_copy(place[:, 1, :], slot_lo[:, :]))
            link(v.tensor_tensor(at_tile[:, :, 2, :], row_no[:, 0:NT].unsqueeze(1).broadcast_to([P, NTOK, NT]),
                                 place[:, 0, :].unsqueeze(2).broadcast_to([P, NTOK, NT]), ALU.is_equal))
            v.tensor_scalar(at_tile[:, :, 0, :], at_tile[:, :, 2, :], part_no[:, 0:1], None, ALU.mult)
            v.tensor_tensor(at_tile[:, :, 1, :], at_tile[:, :, 2, :],
                            step_no[:, :].unsqueeze(2).broadcast_to([P, NTOK, NT]), ALU.mult)
            v.tensor_tensor(at_row[:, :, :], row_no[:, :].unsqueeze(1).broadcast_to([P, NTOK, P]),
                            place[:, 1, :].unsqueeze(2).broadcast_to([P, NTOK, P]), ALU.is_equal).then_inc(s_place, 1)
            link(v.tensor_scalar(tile_e[:, 0, :], tile_no[:, :], startA[0:1, 1:2], None, ALU.is_ge))
            for e in (2, 3):
                link(v.scalar_tensor_tensor(tile_e[:, e - 1, :], tile_no[:, :], startA[0:1, e:e + 1],
                                            tile_e[:, e - 2, :], ALU.is_ge, ALU.add))
            v.tensor_scalar(tile_w[:, :], tile_e[:, 2, :], float(KH * XF), None, ALU.mult).then_inc(s_slotA, 1)
            dve.wait_ge(s_lmm, 1)
            link(v.tensor_scalar(list_f[:, 0, :], PS[:, 7, NT:2 * NT], float(P), float(SKIP), ALU.mult, ALU.add))
            link(v.tensor_tensor(list_f[:, 1, :], PS[:, 7, 0:NT], list_f[:, 0, :], ALU.add))
            link(v.scalar_tensor_tensor(list_f[:, 0, :], PS[:, 7, 2 * NT:3 * NT], -float(SKIP), list_f[:, 1, :],
                                        ALU.mult, ALU.add))
            v.tensor_scalar(list_g[:, :], list_f[:, 0, :], float(T - 1), None, ALU.min)
            v.tensor_copy(list_s[:, :], list_f[:, 0, :]).then_inc(s_list, 1)

            def lo_wx(e):
                dve.wait_ge(s_wxhi, e + 1)
                n = KH * XF
                v.tensor_tensor(parts[:, half + e * n:half + (e + 1) * n], raw[:, e * n:(e + 1) * n],
                                parts[:, e * n:(e + 1) * n].bitcast(F32), ALU.subtract).then_inc(s_wxlo, 1)
            for e in range(1, XE - 1):
                lo_wx(e)

            def bn1(j, p):
                dve.wait_ge(s_x[p], (j - p) * 8 + 16)
                v.bn_stats(st6[:, p, :], xs[:, bass.ds(j, 1), :].rearrange("p o h -> p (o h)")).then_inc(s_bn1, 1)

            def ve1(j, p):
                dve.wait_ge(s_ag1, j + 1)
                if not isinstance(j, int) or j > 1:
                    dve.wait_ge(s_rstd, j - 1)
                v.tensor_scalar(veA[:, p:p + 1], mvA[:, p, 1:2], EPS, None, ALU.add).then_inc(s_var, 1)

            def bn2(j, p):
                dve.wait_ge(s_x1, j + 1)
                v.bn_stats(st2[:, p, :], yrow[:, p, 0:H]).then_inc(s_bn2, 1)

            def var2(j, p):
                dve.wait_ge(s_ag2, j + 1)
                if not isinstance(j, int) or j > 1:
                    dve.wait_ge(s_rstd2, j - 1)
                v.tensor_scalar(ve2[:, p:p + 1], mv2[:, p, 1:2], EPS, None, ALU.add).then_inc(s_var2, 1)

            def norm2(j, p):
                dve.wait_ge(s_rstd2, j + 1)
                v.tensor_scalar(yrow[:, p, H:2 * H], yrow[:, p, 0:H], mv2[:, p, 0:1], rs2[:, p:p + 1],
                                ALU.subtract, ALU.mult).then_inc(s_h2, 1)

            def norm(j, p):
                dve.wait_ge(s_rstd, j + 1)
                if not isinstance(j, int) or j > 1:
                    dve.wait_ge(s_t1, j - 1)
                v.tensor_scalar(hn[:, p, :], xs[:, bass.ds(j, 1), :].rearrange("p o h -> p (o h)"),
                                mvA[:, p, 0:1], rsA[:, p:p + 1], ALU.subtract, ALU.mult).then_inc(s_hn, 1)

            def lo1(j, p):
                dve.wait_ge(s_h1hi, j + 1)
                v.tensor_tensor(hT[:, p, 1].rearrange("p k n -> p (k n)"), PS[:, 0, :],
                                hT[:, p, 0].rearrange("p k n -> p (k n)").bitcast(F32), ALU.subtract).then_inc(s_h1lo, 1)

            def product(j, p):
                dve.wait_ge(s_su, j + 1)
                if not isinstance(j, int) or j > 1:
                    dve.wait_ge(s_t2, j - 1)
                v.tensor_tensor(acA[:, p, :], PS[:, 2 + p, :], suA[:, p, :], ALU.mult).then_inc(s_ac, 1)

            def lo2(j, p):
                dve.wait_ge(s_h2hi, j + 1)
                v.tensor_tensor(aT[:, p, 1].rearrange("p k n -> p (k n)"), PS[:, 1, :],
                                aT[:, p, 0].rearrange("p k n -> p (k n)").bitcast(F32), ALU.subtract).then_inc(s_h2lo, 1)

            def resid(j, p):
                dve.wait_ge(s_mm2, j + 1)
                if not isinstance(j, int) or j > 1:
                    dve.wait_ge(s_x1s[p], (j - p) * 8)
                row = xs[:, bass.ds(j, 1), :].rearrange("p o h -> p (o h)")
                v.scalar_tensor_tensor(yrow[:, p, 0:H], PS[:, 4 + p, :], tg[:, 0:1], row, ALU.mult, ALU.add).then_inc(s_x1, 1)

            for j in range(3):
                bn1(j, j % 2)
                dve.wait_ge(s_bn1, j + 1)
                v.bn_aggr(mvA[:, j % 2, :], st6[:, j % 2, :]).then_inc(s_ag1, 1)
                ve1(j, j % 2)
                if j < 2:
                    norm(j, j)
                if j == 0:
                    lo_wx(XE - 1)
                    lo1(0, 0)
            dve.wait_ge(s_tg, 1)

            def stepA(j, p, more, more2, more3):
                q = 1 - p
                back = not isinstance(j, int) or j > 0
                back2 = not isinstance(j, int) or j > 1
                product(j, p)
                if more:
                    lo1(j + 1, q)
                if more2:
                    norm(j + 2, p)
                if back2:
                    norm2(j - 2, p)
                if more3:
                    bn1(j + 3, q)
                if not more3:
                    lo2(j, p)
                if back:
                    resid(j - 1, q)
                    if more3:
                        dve.wait_ge(s_bn1, j + 4)
                    bn2(j - 1, q)
                elif more3:
                    dve.wait_ge(s_bn1, j + 4)
                if more3:
                    v.bn_aggr(mvA[:, q, :], st6[:, q, :]).then_inc(s_ag1, 1)
                    if back:
                        dve.wait_ge(s_bn2, j)
                    ve1(j + 3, q)
                elif back:
                    dve.wait_ge(s_bn2, j)
                if back:
                    v.bn_aggr(mv2[:, q, :], st2[:, q, :]).then_inc(s_ag2, 1)
                if more3:
                    lo2(j, p)
                if back:
                    var2(j - 1, q)
            for j in range(4):
                stepA(j, j % 2, True, True, True)
            with dve.Fori(0, (NT - 7) // 2) as it:
                for p in range(2):
                    stepA(2 * it + 4 + p, p, True, True, True)
            stepA(NT - 3, 0, True, True, False)
            stepA(NT - 2, 1, True, False, False)
            stepA(NT - 1, 0, False, False, False)
            norm2(NT - 2, 1)
            resid(NT - 1, 0)
            bn2(NT - 1, 0)
            dve.wait_ge(s_bn2, NT)
            v.bn_aggr(mv2[:, 0, :], st2[:, 0, :]).then_inc(s_ag2, 1)
            var2(NT - 1, 0)
            norm2(NT - 1, 0)

            for n_, (lo, n, r) in enumerate(SH_CHUNKS):
                dve.wait_ge(s_shhi, n_ + 1)
                v.tensor_tensor(sh_part(1, lo, n, r), raw[0:r, lo:lo + n],
                                sh_part(0, lo, n, r).bitcast(F32), ALU.subtract).then_inc(s_shlo, 1)
            def loB(g, gp):
                for q in range(GROUP):
                    dve.wait_ge(s_ghi, GROUP * g + q + 1)
                    v.tensor_tensor(hTg[:, gp, 1, :, q * P:(q + 1) * P], PS[:, q, :].rearrange("p (k n) -> p k n", k=KH),
                                    hTg[:, gp, 0, :, q * P:(q + 1) * P].bitcast(F32), ALU.subtract).then_inc(s_glo, 1)

            for c in range(5):
                if c == 3:
                    loB(0, 0)
                if c < 4:
                    dve.wait_ge(s_lg, c + 1)
                    if c >= 2:
                        dve.wait_ge(s_lgb, c - 1)
                    v.tensor_copy(lgT[:, c % 2, :], PS[0:E, 4 + c % 2, :]).then_inc(s_lgT, 1)
                if c > 0:
                    dve.wait_ge(s_lgb, c)
                    v.tensor_copy(logits[:, 4 * c - 4:4 * c, :].rearrange("p i e -> p (i e)"),
                                  PS[:, 6 + (c - 1) % 2, 0:4 * E]).then_inc(s_lgc, 1)

            rcount = [0]

            def rlink(ins):
                rcount[0] += 1
                ins.then_inc(v_r, 1)
                dve.wait_ge(v_r, rcount[0])

            def by_tile(t, n=E):
                return t[:, :].unsqueeze(2).broadcast_to([P, NTOK, n])

            def by_expert(t):
                return t[:, :].unsqueeze(1).broadcast_to([P, NTOK, E])

            def each(op, tiles=range(NTOK)):
                for i in tiles:
                    ins = op(i)
                rlink(ins)
            early, late = range(NTOK // 2), range(NTOK // 2, NTOK)

            def largest():
                dve.wait_ge(s_lgc, 4)
                rlink(v.tensor_reduce(mx[:, :], logits[:, :, :], X, ALU.max))

            def shifted():
                v.tensor_tensor(z0[:, :, 0:E], logits[:, :, :], by_tile(mx), ALU.subtract).then_inc(s_d, 1)

            def floored():
                dve.wait_ge(s_d, 1)
                v.memset(z4[:, :, E:EW], BIG)
                v.memset(g13[:, :, NG:NG + 5], BIG)
                rlink(v.tensor_scalar(z3[:, :, 0:E], z0[:, :, 0:E], FLOOR, None, ALU.max))

            def group_best():
                rlink(v.tensor_reduce(g13[:, :, 0:NG], z3[:, :, 0:E].rearrange("p i (g s) -> p i g s", g=NG), X, ALU.max))

            def best_groups():
                each(lambda i: v.max(g8[:, i, :], g13[:, i, :]))

            def mark_groups():
                each(lambda i: v.match_replace(g13r[:, i, :], g8[:, i, :], g13[:, i, :], -BIG))

            def in_groups():
                rlink(v.tensor_scalar(pen[:, :, :], g13r[:, :, 0:NG], -BIG, BIG, ALU.is_equal, ALU.mult))
                rlink(v.tensor_scalar(g8[:, :, :], pen[:, :, :], FLOOR, None, ALU.add))
                rlink(v.tensor_tensor(z4[:, :, 0:E].rearrange("p i (g s) -> p i g s", g=NG),
                                      z3[:, :, 0:E].rearrange("p i (g s) -> p i g s", g=NG),
                                      g8[:, :, :].unsqueeze(3).broadcast_to([P, NTOK, NG, GS]), ALU.min))

            def best_experts(tiles):
                each(lambda i: v.max(key8[:, i, :], z4[:, i, :]), tiles)

            def mark_experts(tiles):
                each(lambda i: v.match_replace(z5[:, i, :], key8[:, i, :], z4[:, i, :], -BIG), tiles)

            def chosen():
                v.memset(pre[:, 0, :], 0.0)
                rlink(v.tensor_scalar(mask[:, :, :], z5[:, :, 0:E], -BIG, None, ALU.is_equal))

            def prefixes(q):
                for i in range(4 * q, 4 * q + 4):
                    rlink(v.tensor_tensor(pre[:, i + 1, :], pre[:, i, :], mask[:, i, :], ALU.add))
                if q == 3:
                    v.memset(sm[:, :], 0.0).then_inc(s_pre, 1)

            def exp_sum():
                dve.wait_ge(s_exp, 1)
                dve.wait_ge(s_pre, 1)
                rlink(v.tensor_reduce(sm[:, :], z1[:, :, 0:E], X, ALU.add))

            def probabilities():
                rlink(v.reciprocal(rc[:, :], sm[:, :]))
                rlink(v.tensor_tensor(z2[:, :, 0:E], z1[:, :, 0:E], by_tile(rc), ALU.mult))

            def counts():
                dve.wait_ge(s_cnt, 1)
                v.tensor_scalar(cm1[:, :], PS[:, 6, 0:E], -1.0, None, ALU.add).then_inc(s_cm1, 1)
            pos = PS[:, 6:8, :].rearrange("p b (i e) -> p (b i) e", e=E)

            def within():
                dve.wait_ge(s_pos, 1)
                dve.wait_ge(s_cm1, 1)
                v.scalar_tensor_tensor(z0[:, :, 0:E], pos, float(CAP - 1), mask[:, :, :], ALU.is_lt, ALU.mult)

            def is_last():
                rlink(v.tensor_tensor(z1[:, :, 0:E], pos, by_expert(cm1), ALU.is_equal))

            def last_past():
                rlink(v.scalar_tensor_tensor(z3[:, :, 0:E], pos, float(CAP - 1), z1[:, :, 0:E], ALU.is_ge, ALU.mult))

            def last_chosen():
                rlink(v.tensor_tensor(z1[:, :, 0:E], z3[:, :, 0:E], mask[:, :, :], ALU.mult))

            def slot_number():
                rlink(v.scalar_tensor_tensor(z5[:, :, 0:E], pos, float(CAP - 1), by_expert(e_slot), ALU.min, ALU.add))

            def kept():
                rlink(v.tensor_tensor(z4[:, :, 0:E], z0[:, :, 0:E], z1[:, :, 0:E], ALU.add))

            def kept_slots():
                rlink(v.tensor_tensor(z7[:, :, 0:E], z4[:, :, 0:E], z5[:, :, 0:E], ALU.mult))

            def token_slots(tiles):
                each(lambda i: v.max(key8[:, i, :], z7[:, i, 0:E]), tiles)

            def slot_ids():
                rlink(v.tensor_scalar(none8[:, :, :], key8[:, :, :], 0.0, float(NOSLOT), ALU.is_le, ALU.mult))
                v.scalar_tensor_tensor(slot_of[:, :, :], key8[:, :, :], -1.0, none8[:, :, :],
                                       ALU.add, ALU.add).then_inc(s_slot, 1)

            def kept_weights():
                rlink(v.tensor_tensor(z3[:, :, 0:E], z0[:, :, 0:E], z2[:, :, 0:E], ALU.mult))

            def row_weights():
                v.tensor_tensor(rows[:, :, H:H + E], z3[:, :, 0:E], z1[:, :, 0:E], ALU.add).then_inc(s_roww, 1)

            def past():
                rlink(v.tensor_tensor(z4[:, :, 0:E], mask[:, :, :], z0[:, :, 0:E], ALU.subtract))

            def past_weights():
                v.tensor_tensor(over_w[:, :, :], z4[:, :, 0:E], z2[:, :, 0:E], ALU.mult).then_inc(s_over, 1)

            def slot_lists():
                dve.wait_ge(s_lct, 1)
                v.tensor_copy(list_T[:, :, :].rearrange("p e c -> p (e c)"), PS[0:HC, 0, 0:2 * E]).then_inc(s_lcc, 1)
                dve.wait_ge(s_lcc, 1)
                row_index(0, 0)
                row_index(1, 1)

            def row_index(e, par):
                v.tensor_scalar(gtok[:, par, :], list_T[:, bass.ds(e, 1), :].rearrange("p e c -> p (e c)"),
                                float(T - 1), None, ALU.min).then_inc(s_gt, 1)

            def nothing():
                pass
            before_b2 = [largest, shifted, floored]
            gaps = [[group_best, best_groups, mark_groups, in_groups, lambda: best_experts(early),
                     lambda: best_experts(late), lambda: mark_experts(early), lambda: mark_experts(late),
                     chosen, lambda: prefixes(0), lambda: prefixes(1)],
                    [lambda: prefixes(2), lambda: prefixes(3), exp_sum, probabilities, counts, nothing,
                     within, is_last, last_past, last_chosen, slot_number],
                    [kept, kept_slots, lambda: token_slots(early), lambda: token_slots(late), slot_ids,
                     kept_weights, row_weights, past, past_weights]]

            def residB(g, gp):
                for q in range(GROUP):
                    dve.wait_ge(s_dn, GROUP * g + q + 1)
                    v.scalar_tensor_tensor(xrow[:, gp, q, 0:H], PS[:, 4 + q, :], tg[:, 1:2], xrow[:, gp, q, 0:H],
                                           ALU.mult, ALU.add).then_inc(s_res, 1)

            def stepB(g, gp, more, routing=()):
                for m in range(6):
                    n, r = 6 * g + m, MST[m]
                    dve.wait_ge(s_suB, n + 1)
                    if not isinstance(g, int) or n > 1:
                        dve.wait_ge(s_bhi, n - 1)
                    v.tensor_tensor(acB[0:r, m % 2, :], PS[0:r, 2 + m % 2, GN:2 * GN], suB[0:r, m % 2, :], ALU.mult).then_inc(s_acB, 1)
                    dve.wait_ge(s_bhi, n + 1)
                    v.tensor_tensor(actB[0:r, 1, m, :], acB[0:r, m % 2, :], actB[0:r, 0, m, :].bitcast(F32),
                                    ALU.subtract).then_inc(s_blo, 1)
                    if m < len(routing):
                        routing[m]()
                if more:
                    loB(g + 1, 1 - gp)
                    for step in routing[6:10]:
                        step()
                    residB(g, gp)
                    for step in routing[10:]:
                        step()
            for step in before_b2:
                step()
            for g in range(3):
                stepB(g, g % 2, True, gaps[g])
            with dve.Fori(0, NGRP // 2 - 2) as it:
                stepB(2 * it + 3, 1, True)
                stepB(2 * it + 4, 0, True)
            stepB(NGRP - 1, 1, False, [slot_lists])

            def lo_w(e, par, k):
                lo, n, r = W_CHUNKS[k]
                dve.wait_ge(s_whi, 7 * e + k + 1)
                v.tensor_tensor(w_part(par, 1, lo, n, r), raw[0:r, par * WE + lo:par * WE + lo + n],
                                w_part(par, 0, lo, n, r).bitcast(F32), ALU.subtract).then_inc(s_wlo, 1)

            def lo_x(e, par, b_):
                dve.wait_ge(s_xhi, 2 * e + b_ + 1)
                v.tensor_tensor(xT[:, par, 2 * b_:2 * b_ + 2, 1, :],
                                PS[:, b_, 0:2 * CAP].rearrange("p (k n) -> p k n", k=2),
                                xT[:, par, 2 * b_:2 * b_ + 2, 0, :].bitcast(F32),
                                ALU.subtract).then_inc(s_xlo, 1)

            def weights_of(e, par, more2):
                dve.wait_ge(s_xg[par], (e - par) * 16 + 32)
                if not isinstance(e, int) or e > 1:
                    dve.wait_ge(s_add, 32 * (e - 1))
                    dve.wait_ge(s_ot, 2 * (e - 1))
                v.tensor_scalar(wcol[:, par, :], xg[:, par, :, bass.ds(e + H, 1)].rearrange("p c o -> p (c o)"),
                                tg[0:HC, 1:2], None, ALU.mult).then_inc(s_wc, 1)
                v.tensor_tensor(tokc[:, par, :], list_T[:, bass.ds(e, 1), :].rearrange("p e c -> p (e c)"),
                                last_skip[:, :], ALU.add).then_inc(s_wc, 1)
                if more2:
                    row_index(e + 2, par)

            def stepC(e, par, more):
                weights_of(e, par, not isinstance(e, int) or e < E - 2)
                if more:
                    lo_w(e + 1, 1 - par, 0)
                def gu_sum(m):
                    dve.wait_ge(s_cxlc, 3 * e + m + 1)
                    if not isinstance(e, int) or e > 0:
                        dve.wait_ge(s_cac, 3 * e + m - 2)
                    v.tensor_tensor(guC[0:MT[m], m, :, :], PS[0:MT[m], cbank(par, m), 0:CAP], xlC[0:MT[m], m, :, :],
                                    ALU.add).then_inc(s_cg, 1)

                def gated(m):
                    dve.wait_ge(s_csu, 3 * e + m + 1)
                    if not isinstance(e, int) or e > 0:
                        dve.wait_ge(s_ahi, 3 * e + m - 2)
                    v.tensor_tensor(acC[0:MT[m], m, :], guC[0:MT[m], m, 1, :], suC[0:MT[m], m, :], ALU.mult).then_inc(s_cac, 1)

                def lo_act(m):
                    dve.wait_ge(s_ahi, 3 * e + m + 1)
                    v.tensor_tensor(actC[0:MT[m], par, 1, m, :], acC[0:MT[m], m, :],
                                    actC[0:MT[m], par, 0, m, :].bitcast(F32), ALU.subtract).then_inc(s_alo, 1)
                gu_sum(0)
                gated(0)
                if more:
                    lo_w(e + 1, 1 - par, 1)
                lo_act(0)
                gu_sum(1)
                gated(1)
                gu_sum(2)
                lo_act(1)
                if more:
                    lo_x(e + 1, 1 - par, 0)
                gated(2)
                if more:
                    lo_x(e + 1, 1 - par, 1)
                lo_act(2)
                if more:
                    for k in range(2, 7):
                        lo_w(e + 1, 1 - par, k)
            for k in range(KH):
                lo_w(0, 0, k)
            lo_x(0, 0, 0)
            lo_x(0, 0, 1)
            residB(NGRP - 1, 1)
            for k in range(KH, 7):
                lo_w(0, 0, k)
            stepC(0, 0, True)
            stepC(1, 1, True)
            with dve.Fori(0, E // 2 - 2) as it:
                stepC(2 * it + 2, 0, True)
                stepC(2 * it + 3, 1, True)
            stepC(E - 2, 0, True)
            stepC(E - 1, 1, False)
            dve.wait_ge(s_ophi, 1)
            v.tensor_tensor(over_p[E:2 * E, :, :].rearrange("e i t -> e (i t)"), over_wT[E:2 * E, :, :].rearrange("e i t -> e (i t)"),
                            over_p[E:2 * E, :, :].rearrange("e i t -> e (i t)").bitcast(F32), ALU.subtract).then_inc(s_opp, 1)
            dve.wait_ge(s_lhi, 1)
            v.tensor_tensor(last_p[:, 1, :], lastS[:, :], last_p[:, 0, :].bitcast(F32), ALU.subtract).then_inc(s_llo, 1)
            for i in range(1, NTOK, 2):
                dve.wait_ge(s_f, i + 1)
                v.tensor_copy(fb[:, i, :], PS[:, i % 4, :]).then_inc(s_fe[1], 1)

        @block.tensor
        def _(pe):
            mm = nc.tensor.matmul

            def split_product(dst, terms):
                for n, (ah, al, bh, bl) in enumerate(terms):
                    mm(dst, ah, bh, start=(n == 0), stop=False)
                    mm(dst, ah, bl, start=False, stop=False)
                    last = mm(dst, al, bh, start=False, stop=(n == len(terms) - 1))
                return last

            def keep_warm(bank, n):
                for _ in range(n):
                    mm(PS[:, bank, 0:P], ident[:, :], ident[:, :], start=True, stop=True)

            pe.wait_ge(s_ohA, 1)
            pe.wait_ge(s_const2, 2)
            mm(PS[:, 6, 0:64], before[:, :], ohA[:, :, :].rearrange("p e i -> p (e i)"), start=True, stop=False)
            mm(PS[:, 6, 0:64], ones[:, :], preA[:, :, 0:NTOK], start=False, stop=True)
            mm(PS[:, 6, 64:64 + XE], ones[:, :], preA[:, :, NTOK], start=True, stop=True).then_inc(s_cntA, 1)
            pe.wait_ge(s_place, 1)
            for i in range(NTOK):
                last = mm(PS[:, 7, 0:3 * NT], at_row[:, i, :], at_tile[:, i, :, :].rearrange("p c j -> p (c j)"),
                          start=(i == 0), stop=(i == NTOK - 1))
            last.then_inc(s_lmm, 1)

            def turn1(j, p):
                pe.wait_ge(s_hn, j + 1)
                if not isinstance(j, int) or j > 0:
                    pe.wait_ge(s_h1lo, j)
                for k in range(KH):
                    last = nc.tensor.transpose(PS[:, 0, k * P:(k + 1) * P], hn[:, p, k * P:(k + 1) * P], ident[:, :])
                last.then_inc(s_t1, 1)

            def weights_at(w0):
                return [(parts[:, bass.ds(w0 + k * XF, XF)], parts[:, bass.ds(w0 + (half + k * XF), XF)]) for k in range(KH)]

            def first(j, p):
                w0 = nc.tensor.value_load(tile_w[0:1, bass.ds(j, 1)], min_val=0, max_val=(XE - 1) * KH * XF)
                pe.wait_ge(s_h1lo, j + 1)
                if not isinstance(j, int) or j > 1:
                    pe.wait_ge(s_ac, j - 1)
                split_product(PS[:, 2 + p, :], [(hT[:, p, 0, k, :], hT[:, p, 1, k, :], wh, wl)
                                                for k, (wh, wl) in enumerate(weights_at(w0))]).then_inc(s_mm1, 1)

            def second(j, p):
                w0 = nc.tensor.value_load(tile_w[0:1, bass.ds(j, 1)], min_val=0, max_val=(XE - 1) * KH * XF)
                pe.wait_ge(s_h2lo, j + 1)
                if not isinstance(j, int) or j > 1:
                    pe.wait_ge(s_x1, j - 1)
                split_product(PS[:, 4 + p, :], [(aT[:, p, 0, k, :], aT[:, p, 1, k, :], wh, wl)
                                                for k, (wh, wl) in enumerate(weights_at(w0))]).then_inc(s_mm2, 1)

            def turn2(j, p):
                pe.wait_ge(s_ac, j + 1)
                if not isinstance(j, int) or j > 0:
                    pe.wait_ge(s_h2lo, j)
                for k in range(KH):
                    last = nc.tensor.transpose(PS[:, 1, k * P:(k + 1) * P], acA[:, p, k * P:(k + 1) * P], ident[:, :])
                last.then_inc(s_t2, 1)

            def stepA(j, p, more):
                first(j, p)
                if more:
                    turn1(j + 1, 1 - p)
                if not isinstance(j, int) or j > 0:
                    second(j - 1, 1 - p)
                turn2(j, p)
            keep_warm(5, 24)
            turn1(0, 0)
            keep_warm(5, 8)
            pe.wait_ge(s_wxlo, XE - 1)
            pe.wait_ge(s_wxlo0, 1)
            pe.wait_ge(s_slotA, 1)
            stepA(0, 0, True)
            stepA(1, 1, True)
            stepA(2, 0, True)
            with pe.Fori(0, (NT - 5) // 2) as it:
                stepA(2 * it + 3, 1, True)
                stepA(2 * it + 4, 0, True)
            stepA(NT - 2, 1, True)
            stepA(NT - 1, 0, False)
            second(NT - 1, 0)

            keep_warm(7, 40)
            pe.wait_ge(s_gatew, 16)
            pe.wait_ge(s_h2lo, NT)
            pe.wait_ge(s_ac, NT)

            def turnB(c):
                if c > 0:
                    pe.wait_ge(s_hl[c], 16)
                for k in range(KH):
                    if c == 0:
                        pe.wait_ge(s_h0[k], 16)
                    if c > 0:
                        pe.wait_ge(s_hTf, KH * (c - 1) + k + 1)
                    for n in range(4):
                        last = nc.tensor.transpose(PS[:, k, n * P:(n + 1) * P], rows[:, 4 * c + n, k * P:(k + 1) * P], ident[:, :])
                    last.then_inc(s_tB, 1)

            def logit(c):
                if c > 1:
                    pe.wait_ge(s_lgT, c - 1)
                for k in range(KH):
                    pe.wait_ge(s_hTf, KH * c + k + 1)
                    last = mm(PS[0:E, 4 + c % 2, :], gate_w[:, k, :], hTf[:, c % 2, k, :], start=(k == 0), stop=(k == KH - 1))
                last.then_inc(s_lg, 1)

            def turn_logits(c):
                pe.wait_ge(s_lgT, c + 1)
                if c > 1:
                    pe.wait_ge(s_lgc, c - 1)
                for n in range(4):
                    last = nc.tensor.transpose(PS[:, 6 + c % 2, n * E:(n + 1) * E], lgT[:, c % 2, n * P:(n + 1) * P], ident[0:E, 0:E])
                last.then_inc(s_lgb, 1)
            def turn_group(g, gp):
                for q in range(GROUP):
                    if q == 0:
                        pe.wait_ge(s_xr[gp], (g - gp) * 8 + 16)
                    if isinstance(g, int) and g == 0:
                        pe.wait_ge(s_hTf, 4 * KH)
                    else:
                        pe.wait_ge(s_glo, GROUP * g + q - 1)
                    for k in range(KH):
                        last = nc.tensor.transpose(PS[:, q, k * P:(k + 1) * P], xrow[:, gp, q, H + k * P:H + (k + 1) * P], ident[:, :])
                    last.then_inc(s_tg2, 1)

            def gate_up(g, gp, m):
                n, r = 6 * g + m, MST[m]
                if not isinstance(g, int) or n > 1:
                    pe.wait_ge(s_acB, n - 1)
                for u in range(2):
                    terms = []
                    for k in range(KH):
                        lo = k * 2 * MS + u * MS + MSO[m]
                        terms.append((sh_part(0, lo, r), sh_part(1, lo, r), hTg[:, gp, 0, k, :], hTg[:, gp, 1, k, :]))
                    last = split_product(PS[0:r, 2 + m % 2, u * GN:(u + 1) * GN], terms)
                last.then_inc(s_gu, 1)

            def down(g, gp):
                def part(q, ms):
                    for m in ms:
                        r = MST[m]
                        lo = SGU + m * H
                        for pa, pb in ((0, 0), (0, 1), (1, 0)):
                            last = mm(PS[:, 4 + q, :], actB[0:r, pa, m, q * P:(q + 1) * P], sh_part(pb, lo, H, r),
                                      start=(m == 0 and pa == pb), stop=(m == 5 and pa == 1))
                    return last
                pe.wait_ge(s_blo, 6 * g + 5)
                if not isinstance(g, int) or g > 0:
                    pe.wait_ge(s_res, GROUP * g)
                for q in range(GROUP):
                    part(q, range(5))
                pe.wait_ge(s_blo, 6 * g + 6)
                for q in range(GROUP):
                    part(q, [5]).then_inc(s_dn, 1)

            def count():
                pe.wait_ge(s_pre, 1)
                pe.wait_ge(s_lgc, 4)
                mm(PS[:, 6, 0:E], ones[:, :], pre[:, NTOK, :], start=True, stop=True).then_inc(s_cnt, 1)

            def ranks():
                pe.wait_ge(s_cm1, 1)
                for b_ in range(2):
                    dst = PS[:, 6 + b_, :]
                    mm(dst, before[:, :], mask[:, 8 * b_:8 * b_ + 8, :].rearrange("p i e -> p (i e)"), start=True, stop=False)
                    last = mm(dst, ones[:, :], pre[:, 8 * b_:8 * b_ + 8, :].rearrange("p i e -> p (i e)"), start=False, stop=True)
                last.then_inc(s_pos, 1)

            def turn_over():
                pe.wait_ge(s_over, 1)
                for c in range(4):
                    if c >= 2:
                        pe.wait_ge(s_ovTc, c - 1)
                    for n in range(4):
                        last = nc.tensor.transpose(PS[0:E, 6 + c % 2, n * P:(n + 1) * P], over_w[:, 4 * c + n, :], ident[:, :])
                    last.then_inc(s_ovT, 1)

            def turn_x(e, par):
                pe.wait_ge(s_xg[par], (e - par) * 16 + 32)
                if not isinstance(e, int) or e > 0:
                    pe.wait_ge(s_xlo, 2 * e)
                else:
                    pe.wait_ge(s_glo, GROUP * NGRP)
                    pe.wait_ge(s_lcc, 1)
                for k in range(KH):
                    for c in range(2):
                        o = (k % 2) * CAP + c * HC
                        last = nc.tensor.transpose(PS[:, k // 2, o:o + HC], xg[:, par, c, k * P:(k + 1) * P], ident[0:HC, 0:HC])
                last.then_inc(s_tx, 1)

            def stepB(g, gp, more):
                for m in range(6):
                    if not more and m == 1:
                        pe.wait_ge(s_lc, 16)
                        nc.tensor.transpose(PS[0:HC, 0, 0:2 * E], slot_list[:, :], ident[:, :]).then_inc(s_lct, 1)
                    gate_up(g, gp, m)
                    if isinstance(g, int) and g == 1 and m == 3:
                        count()
                if isinstance(g, int) and g == 1:
                    ranks()
                if more:
                    turn_group(g + 1, 1 - gp)
                else:
                    turn_x(0, 0)
                down(g, gp)
            turnB(0)
            for c in range(4):
                if c < 3:
                    turnB(c + 1)
                else:
                    turn_group(0, 0)
                logit(c)
                if c > 0:
                    turn_logits(c - 1)
            turn_logits(3)
            pe.wait_ge(s_shlo, len(SH_CHUNKS))
            pe.wait_ge(s_glo, GROUP)
            stepB(0, 0, True)
            pe.wait_ge(s_glo, 2 * GROUP)
            stepB(1, 1, True)
            pe.wait_ge(s_glo, 3 * GROUP)
            stepB(2, 0, True)
            turn_over()
            with pe.Fori(0, NGRP // 2 - 2) as it:
                for p in range(2):
                    pe.wait_ge(s_glo, GROUP * (2 * it + 4 + p))
                    stepB(2 * it + 3 + p, 1 - p, True)
            pe.wait_ge(s_glo, GROUP * NGRP)
            stepB(NGRP - 1, 1, False)

            def stepC(e, par, more):
                pe.wait_ge(s_xlo, 2 * (e + 1))
                for m in range(3):
                    r = MT[m]
                    if not isinstance(e, int) or e > 0 or m > 1:
                        pe.wait_ge(s_cg, 3 * e + m - 1)
                    b0 = cbank(par, m).start
                    for u in range(2):
                        for k in range(KH):
                            if m == 0 and u == 0:
                                pe.wait_ge(s_wlo, 7 * e + k + 1)
                            lo = k * 2 * M + u * M + m * P
                            mm(PS[0:r, b0 + u, 0:2 * CAP], w_part(par, 0, lo, r),
                               xT[:, par, k, :, :].rearrange("p t n -> p (t n)"), start=(k == 0), stop=False)
                            last = mm(PS[0:r, b0 + u, 0:CAP], w_part(par, 1, lo, r), xT[:, par, k, 0, :],
                                      start=False, stop=(k == KH - 1))
                    last.then_inc(s_cgu, 1)
                if more:
                    turn_x(e + 1, 1 - par)
                pe.wait_ge(s_wlo, 7 * (e + 1))
                if not isinstance(e, int) or e > 0:
                    pe.wait_ge(s_ot, 2 * e)
                else:
                    pe.wait_ge(s_res, NTOK)

                def part(c, ms):
                    for m in ms:
                        r = MT[m]
                        for pa, pb in ((0, 0), (0, 1), (1, 0)):
                            last = mm(PS[0:HC, 4 + c, :], actC[0:r, par, pa, m, c * HC:(c + 1) * HC],
                                      w_part(par, pb, WGU + m * H, H, r), start=(m == 0 and pa == pb), stop=(m == 2 and pa == 1))
                    return last
                for m in range(2):
                    pe.wait_ge(s_alo, 3 * e + m + 1)
                    for c in range(2):
                        part(c, [m])
                pe.wait_ge(s_alo, 3 * e + 3)
                for c in range(2):
                    part(c, [2]).then_inc(s_cd, 1)
            pe.wait_ge(s_acB, 6 * NGRP)
            pe.wait_ge(s_ovTc, 4)
            stepC(0, 0, True)
            stepC(1, 1, True)
            with pe.Fori(0, E // 2 - 2) as it:
                stepC(2 * it + 2, 0, True)
                stepC(2 * it + 3, 1, True)
            stepC(E - 2, 0, True)
            stepC(E - 1, 1, False)

            keep_warm(7, 22)
            pe.wait_ge(s_opp, 1)
            pe.wait_ge(s_llo, 1)
            for i in range(NTOK):
                if i >= 4:
                    pe.wait_ge(s_fe[i % 2], (i - 4) // 2 + 1)
                for part_ in range(2):
                    last = mm(PS[:, i % 4, :], over_p[:, i, :], last_p[:, part_, :], start=(part_ == 0), stop=(part_ == 1))
                last.then_inc(s_f, 1)


_OUTS = [((4, 512, 512), "float32")]


def kernel(x, itok_BxS_13_99985, ctx_2048, g_xattn, g_ffn, L0_ffn_gate_weight, L0_ffn_Wg, L0_ffn_Wu,
           L0_ffn_Wd, L0_ffn_Sg, L0_ffn_Su, L0_ffn_Sd):
    import numpy as np
    import concourse.bacc as bacc
    from concourse.bass_utils import run_bass_kernel_spmd

    def turned(w):
        w = np.asarray(w)
        n = w.ndim
        w = w.reshape(w.shape[:-1] + (w.shape[-1] // P, P))
        return np.moveaxis(np.moveaxis(w, -1, n - 2), -1, n - 1)

    def inner_tiles(w, whole):
        w = np.swapaxes(np.asarray(w), -1, -2)
        head = w[..., :whole * P, :].reshape(w.shape[:-2] + (whole, P, H))
        return np.moveaxis(head, -3, -2).reshape(w.shape[:-2] + (P, whole * H)), w[..., whole * P:, :]

    ffn_gu = np.concatenate([turned(L0_ffn_Wg), turned(L0_ffn_Wu)], axis=-1).reshape(E, P, WGU)
    wdA, wdB = inner_tiles(L0_ffn_Wd, 2)
    sgu = np.concatenate([turned(L0_ffn_Sg), turned(L0_ffn_Su)], axis=-1).reshape(P, SGU)
    sdA, sd_rest = inner_tiles(L0_ffn_Sd, 4)
    sdB = np.moveaxis(sd_rest.reshape(2, 96, H), 0, 1).reshape(96, 2 * H)
    arrays = {
        "x": np.asarray(x).reshape(T, H),
        "tid": np.asarray(itok_BxS_13_99985).reshape(NTOK, P).T,
        "ctxT": turned(ctx_2048).reshape(XE, P, KH * XF),
        "g_x": np.asarray(g_xattn).reshape(1, 1),
        "g_f": np.asarray(g_ffn).reshape(1, 1),
        "gateT": turned(L0_ffn_gate_weight),
        "wgu": ffn_gu, "wdA": wdA, "wdB": wdB, "sgu": sgu, "sdA": sdA, "sdB": sdB,
    }
    arrays = {k: np.ascontiguousarray(a) for k, a in arrays.items()}
    nc = bacc.Bacc("TRN2", target_bir_lowering=False, num_devices=1)
    args = [nc.dram_tensor(k, a.shape, mybir.dt.from_np(a.dtype), kind="ExternalInput").ap() for k, a in arrays.items()]
    out = nc.dram_tensor("out", (T, H), F32, kind="ExternalOutput").ap()
    build(nc, *args, out)
    r = run_bass_kernel_spmd(nc, [arrays], core_ids=[0])
    return r.results[0]["out"].reshape(4, 512, 512)
```
